# Optimizing a Trainium2 kernel written in Bass

```python
import numpy as np
import jax
import jax.numpy as jnp

def _softmax(x, axis=-1):
    return jax.nn.softmax(x, axis=axis)

def _gelu(x):
    return jax.nn.gelu(x, approximate=True)

def _silu(x):
    return jax.nn.silu(x)

def _sigmoid(x):
    return jax.nn.sigmoid(x)

def _layernorm(x, axis=-1, eps=1e-05):
    m = jnp.mean(x, axis=axis, keepdims=True)
    v = jnp.var(x, axis=axis, keepdims=True)
    return (x - m) / jnp.sqrt(v + eps)

def _scatter_add(tgt, idx, src, axis=0):
    return tgt.at[idx].add(src)

def _segment_sum(src, seg, n):
    return jax.ops.segment_sum(src, seg, n)
kernel_name = 'mk_adj_ffn_d1_adj_r2_fcc31f'

def setup_inputs(seed: int=0):
    np.random.seed(seed)
    _w = jnp.asarray

    def _rec_inputs():
        import jax
        import jax.numpy as jnp
        _gk = jax.random.key(seed)
        x = -0.0001538 + 1 * jax.random.normal(jax.random.fold_in(_gk, 1), (128, 64, 384), jnp.float32)
        _a = jax.random.bernoulli(jax.random.fold_in(_gk, 2), 0.0625, (128, 64, 64))
        _a = jnp.logical_or(_a, jnp.swapaxes(_a, -1, -2))
        _a = jnp.logical_or(_a, jnp.eye(64, dtype=bool))
        adj = _a.astype(jnp.int32)
        return (x, adj)
    x, adj = _rec_inputs()

    def _L0_gnn_setup():
        import jax, jax.numpy as jnp
        import numpy as np
        D = 384
        NEG = -1000000000.0
        key = jax.random.key(seed)
        ks = jax.random.split(key, 12)
        B, N = (8, 512)
        x = jax.random.normal(ks[0], (B, N, D), dtype=jnp.float32)
        section_mask_full = jax.random.randint(ks[1], (B, N, N), 0, 2, dtype=jnp.int32)
        sentence_mask_full = jax.random.randint(ks[2], (B, N, N), 0, 2, dtype=jnp.int32)
        s = 1.0 / np.sqrt(D)
        W1 = jax.random.normal(ks[3], (D, D), dtype=jnp.float32) * s
        b1 = jnp.zeros((D,), dtype=jnp.float32)
        W2 = jax.random.normal(ks[4], (D, D), dtype=jnp.float32) * s
        b2 = jnp.zeros((D,), dtype=jnp.float32)
        W3 = jax.random.normal(ks[5], (D, D), dtype=jnp.float32) * s
        b3 = jnp.zeros((D,), dtype=jnp.float32)
        W4 = jax.random.normal(ks[6], (D, D), dtype=jnp.float32) * s
        b4 = jnp.zeros((D,), dtype=jnp.float32)
        return {'x': x, 'section_mask_full': section_mask_full, 'sentence_mask_full': sentence_mask_full, 'W1': W1, 'b1': b1, 'W2': W2, 'b2': b2, 'W3': W3, 'b3': b3, 'W4': W4, 'b4': b4}
    _L0_gnn_all = _L0_gnn_setup()
    _L0_gnn_in = {k: v for k, v in _L0_gnn_all.items() if k in ('W1', 'b1', 'W2', 'b2', 'W3', 'b3', 'W4', 'b4')}
    del _L0_gnn_all

    def _L0_ffn_setup():
        import jax, jax.numpy as jnp
        import numpy as np
        B, L, D, H, F = (4, 1024, 384, 12, 1536)
        ROUTE_FRAC = 0.15
        LN_EPS = 1e-05

        def _ln(x, g, b):
            m = jnp.mean(x, axis=-1, keepdims=True)
            v = jnp.mean((x - m) ** 2, axis=-1, keepdims=True)
            return (x - m) * jax.lax.rsqrt(v + LN_EPS) * g + b
        key = jax.random.key(seed)
        ks = jax.random.split(key, 20)
        s = 0.02
        return {'hidden_states': jax.random.normal(ks[0], (B, L, D), dtype=jnp.float32), 'g1': jnp.ones((D,), jnp.float32), 'b1': jnp.zeros((D,), jnp.float32), 'g2': jnp.ones((D,), jnp.float32), 'b2': jnp.zeros((D,), jnp.float32), 'Wr': jax.random.normal(ks[1], (D,), jnp.float32) * s, 'br': jnp.zeros((), jnp.float32), 'Wq': jax.random.normal(ks[2], (D, D), jnp.float32) * s, 'bq': jnp.zeros((D,), jnp.float32), 'Wk': jax.random.normal(ks[3], (D, D), jnp.float32) * s, 'bk': jnp.zeros((D,), jnp.float32), 'Wv': jax.random.normal(ks[4], (D, D), jnp.float32) * s, 'bv': jnp.zeros((D,), jnp.float32), 'Wo': jax.random.normal(ks[5], (D, D), jnp.float32) * s, 'bo': jnp.zeros((D,), jnp.float32), 'Wm': jax.random.normal(ks[6], (D, D), jnp.float32) * s, 'bm': jnp.zeros((D,), jnp.float32), 'W1': jax.random.normal(ks[7], (D, F), jnp.float32) * s, 'bf1': jnp.zeros((F,), jnp.float32), 'W2': jax.random.normal(ks[8], (F, D), jnp.float32) * s, 'bf2': jnp.zeros((D,), jnp.float32)}
    _L0_ffn_all = _L0_ffn_setup()
    _L0_ffn_in = {k: v for k, v in _L0_ffn_all.items() if k in ('g1', 'b1', 'g2', 'b2', 'Wr', 'br', 'Wq', 'bq', 'Wk', 'bk', 'Wv', 'bv', 'Wo', 'bo', 'Wm', 'bm', 'W1', 'bf1', 'W2', 'bf2')}
    del _L0_ffn_all
    return {'x': x, 'adj': adj, 'L0_gnn_W1': _L0_gnn_in['W1'], 'L0_gnn_b1': _L0_gnn_in['b1'], 'L0_gnn_W2': _L0_gnn_in['W2'], 'L0_gnn_b2': _L0_gnn_in['b2'], 'L0_gnn_W3': _L0_gnn_in['W3'], 'L0_gnn_b3': _L0_gnn_in['b3'], 'L0_gnn_W4': _L0_gnn_in['W4'], 'L0_gnn_b4': _L0_gnn_in['b4'], 'L0_ffn_g1': _L0_ffn_in['g1'], 'L0_ffn_b1': _L0_ffn_in['b1'], 'L0_ffn_g2': _L0_ffn_in['g2'], 'L0_ffn_b2': _L0_ffn_in['b2'], 'L0_ffn_Wr': _L0_ffn_in['Wr'], 'L0_ffn_br': _L0_ffn_in['br'], 'L0_ffn_Wq': _L0_ffn_in['Wq'], 'L0_ffn_bq': _L0_ffn_in['bq'], 'L0_ffn_Wk': _L0_ffn_in['Wk'], 'L0_ffn_bk': _L0_ffn_in['bk'], 'L0_ffn_Wv': _L0_ffn_in['Wv'], 'L0_ffn_bv': _L0_ffn_in['bv'], 'L0_ffn_Wo': _L0_ffn_in['Wo'], 'L0_ffn_bo': _L0_ffn_in['bo'], 'L0_ffn_Wm': _L0_ffn_in['Wm'], 'L0_ffn_bm': _L0_ffn_in['bm'], 'L0_ffn_W1': _L0_ffn_in['W1'], 'L0_ffn_bf1': _L0_ffn_in['bf1'], 'L0_ffn_W2': _L0_ffn_in['W2'], 'L0_ffn_bf2': _L0_ffn_in['bf2']}

def reference(x, adj, L0_gnn_W1, L0_gnn_b1, L0_gnn_W2, L0_gnn_b2, L0_gnn_W3, L0_gnn_b3, L0_gnn_W4, L0_gnn_b4, L0_ffn_g1, L0_ffn_b1, L0_ffn_g2, L0_ffn_b2, L0_ffn_Wr, L0_ffn_br, L0_ffn_Wq, L0_ffn_bq, L0_ffn_Wk, L0_ffn_bk, L0_ffn_Wv, L0_ffn_bv, L0_ffn_Wo, L0_ffn_bo, L0_ffn_Wm, L0_ffn_bm, L0_ffn_W1, L0_ffn_bf1, L0_ffn_W2, L0_ffn_bf2):
    import jax
    import jax.numpy as jnp

    def _L0_gnn_ref(x, section_mask_full, sentence_mask_full, W1, b1, W2, b2, W3, b3, W4, b4):
        import jax, jax.numpy as jnp
        import numpy as np
        D = 384
        NEG = -1000000000.0
        sec = section_mask_full.astype(x.dtype)
        sen = sentence_mask_full.astype(x.dtype)
        mask0 = section_mask_full == 0
        mask1 = section_mask_full == 1
        q = x @ W1.T + b1
        k = x @ W2.T + b2
        att = jnp.einsum('bnd,bmd->bnm', q, k) / 28.0
        dia_att = jax.nn.softmax(jnp.where(mask0, NEG, att), axis=2)
        prior_att = jax.nn.softmax(jnp.where(mask0, NEG, 2.0 * sec + 4.0 * sen), axis=2)
        fusion_att = jax.nn.softmax(jnp.where(mask0, NEG, dia_att * prior_att), axis=2)
        g_x1 = jnp.einsum('bnm,bmd->bnd', fusion_att, x) @ W3.T + b3
        no_self_att = jax.nn.softmax(jnp.where(mask1, NEG, att), axis=2)
        g_x2 = jnp.einsum('bnm,bmd->bnd', no_self_att, g_x1) @ W4.T + b4
        return g_x1 + g_x2

    def _L0_ffn_ref(hidden_states, g1, b1, g2, b2, Wr, br, Wq, bq, Wk, bk, Wv, bv, Wo, bo, Wm, bm, W1, bf1, W2, bf2):
        import jax, jax.numpy as jnp
        import numpy as np
        B, L, D, H, F = (4, 1024, 384, 12, 1536)
        ROUTE_FRAC = 0.15
        LN_EPS = 1e-05

        def _ln(x, g, b):
            m = jnp.mean(x, axis=-1, keepdims=True)
            v = jnp.mean((x - m) ** 2, axis=-1, keepdims=True)
            return (x - m) * jax.lax.rsqrt(v + LN_EPS) * g + b
        b, l, d = hidden_states.shape
        dh = d // H
        normed = _ln(hidden_states, g1, b1)
        scores = jax.nn.sigmoid(jnp.einsum('bld,d->bl', normed, Wr) + br)
        k = max(1, int(round(ROUTE_FRAC * l)))
        _, idx = jax.lax.top_k(-scores, k)
        attn_mask = jnp.zeros((b, l), bool).at[jnp.arange(b)[:, None], idx].set(True)
        q = (normed @ Wq + bq).reshape(b, l, H, dh)
        kk = (normed @ Wk + bk).reshape(b, l, H, dh)
        v = (normed @ Wv + bv).reshape(b, l, H, dh)
        logits = jnp.einsum('blhd,bmhd->bhlm', q, kk) / jnp.sqrt(jnp.float32(dh))
        probs = jax.nn.softmax(logits, axis=-1)
        ctx = jnp.einsum('bhlm,bmhd->blhd', probs, v).reshape(b, l, d)
        attn_out = ctx @ Wo + bo
        w = scores / (jnp.sum(scores, axis=1, keepdims=True) + 1e-06)
        pooled = jnp.einsum('bl,bld->bd', w, normed)
        mix_out = (normed + scores[..., None] * pooled[:, None, :]) @ Wm + bm
        merged = jnp.where(attn_mask[..., None], attn_out, mix_out)
        h = hidden_states + merged
        n2 = _ln(h, g2, b2)
        ffn = jax.nn.gelu(n2 @ W1 + bf1, approximate=False) @ W2 + bf2
        return h + ffn
    x = x + _L0_gnn_ref(_layernorm(x, axis=-1), adj, adj, L0_gnn_W1, L0_gnn_b1, L0_gnn_W2, L0_gnn_b2, L0_gnn_W3, L0_gnn_b3, L0_gnn_W4, L0_gnn_b4)
    x = x + _L0_ffn_ref(_layernorm(x, axis=-1), L0_ffn_g1, L0_ffn_b1, L0_ffn_g2, L0_ffn_b2, L0_ffn_Wr, L0_ffn_br, L0_ffn_Wq, L0_ffn_bq, L0_ffn_Wk, L0_ffn_bk, L0_ffn_Wv, L0_ffn_bv, L0_ffn_Wo, L0_ffn_bo, L0_ffn_Wm, L0_ffn_bm, L0_ffn_W1, L0_ffn_bf1, L0_ffn_W2, L0_ffn_bf2)
    return x

_drawn_inputs = setup_inputs


def setup_inputs(seed=0):
    import zlib

    import numpy as np

    out = dict(_drawn_inputs(seed))
    spreads = {'L0_gnn_b1': (0.0, 0.8),
     'L0_gnn_b2': (0.0, 2.0),
     'L0_gnn_b3': (0.0, 0.1),
     'L0_gnn_b4': (0.0, 0.1),
     'L0_ffn_g1': (1.0, 0.2),
     'L0_ffn_b1': (0.0, 0.294),
     'L0_ffn_g2': (1.0, 0.6),
     'L0_ffn_b2': (0.0, 0.8),
     'L0_ffn_bq': (0.0, 0.8),
     'L0_ffn_bk': (0.0, 2.0),
     'L0_ffn_bv': (0.0, 0.8),
     'L0_ffn_bo': (0.0, 0.411),
     'L0_ffn_bm': (0.0, 0.289),
     'L0_ffn_bf1': (0.0, 0.387),
     'L0_ffn_bf2': (0.0, 0.1)}
    factors = {'L0_ffn_Wq': 8.0, 'L0_ffn_Wk': 8.0, 'L0_ffn_Wv': 7.321, 'L0_ffn_Wo': 5.458}
    for name, (base, spread) in spreads.items():
        noise = np.random.default_rng([zlib.crc32(name.encode()), seed]).standard_normal(out[name].shape)
        drawn = base * np.exp(spread * noise) if base else spread * noise
        out[name] = jnp.asarray(drawn.astype(out[name].dtype))
    for name, factor in factors.items():
        out[name] = (out[name] * factor).astype(out[name].dtype)
    return out
```

```python
from contextlib import ExitStack

import numpy as np
import concourse.bass as bass
from concourse import mybir

F32 = mybir.dt.float32
F32R = mybir.dt.float32r
I32 = mybir.dt.int32
ALU = mybir.AluOpType
ACT = mybir.ActivationFunctionType
AX = mybir.AxisListType

P = 128
B, L, D = 128, 64, 384
C = D // P
H, DH, F = 12, 32, 1536
HC = P // DH
FC = F // P
T = 4
GT = T * P
GB = GT // L
G = B * L // GT
K = max(1, int(round(0.15 * L)))
EPS = 1e-5
NEG = -1e9
WM = D + 2
SELW = 2 * K + 2
RR = 96
ROW_POOL, ROW_BIAS, ROW_B1 = GB * K, GB * K + GB, GB * K + GB + 1
ONES = [(a, b) for a, b in ((0, 0), (1, 0), (0, 1))]


def constants():
    p = np.arange(P)
    m = np.arange(L)
    ident = np.eye(P)
    same = (p[:, None] // L == p[None, :] // L) * 1.0
    node = (p[:, None] % L == m[None, :]) * 1.0
    earlier = (m[None, :] < p[:, None] % L) * 1.0
    iota = np.broadcast_to(np.arange(K), (P, K))
    picked = np.broadcast_to(np.arange(RR) < GB * K, (P, RR))
    bias = np.broadcast_to(np.arange(RR) == ROW_BIAS, (P, RR))
    return np.concatenate([ident, same, node, earlier, iota, picked, bias], axis=1).astype(np.float32)


CONST_W = constants().shape[1]


def program(nc, x, adj, gW1, gb1, gW2, gb2, gW3, gb3, gW4, gb4, g1, b1, g2, b2, Wr, br, Wq, bq, Wk, bk,
            Wv, bv, Wo, bo, Wm, bm, W1, bf1, W2, bf2, consts, out):
    xh_d = nc.dram_tensor("residual_scratch", (B * L, D), F32).ap()
    n2_d = nc.dram_tensor("normed_scratch", (B * L, D), F32).ap()
    tiles = lambda a: a.rearrange("(g t p) d -> g p t d", t=T, p=P)
    x_g = tiles(x.rearrange("b n d -> (b n) d"))
    adj_g = tiles(adj.rearrange("b n d -> (b n) d"))
    out_g = tiles(out.rearrange("b n d -> (b n) d"))
    xh_g, n2_g = tiles(xh_d), tiles(n2_d)
    chunks = lambda w: w.rearrange("(c p) n -> p c n", p=P)
    column = lambda v: v.rearrange("(c p) -> p c", p=P)
    row = lambda v: v.rearrange("(a n) -> a n", a=1)

    with ExitStack() as ctx:
        def sb(name, shape, dt=F32, where=ctx):
            return where.enter_context(nc.sbuf_tensor(name, shape, dt))

        def sem(name, where=ctx):
            return where.enter_context(nc.semaphore(name))

        bank = [ctx.enter_context(nc.psum_tensor(f"bank{i}", [P, 512], F32)) for i in range(8)]

        cst = sb("cst", [P, CONST_W])
        ident = cst[:, 0:P]
        same = cst[:, P:2 * P]
        node = cst[:, 2 * P:2 * P + L]
        earlier = cst[:, 2 * P + L:2 * P + 2 * L]
        o = 2 * P + 2 * L
        iota, picked, biasrow = cst[:, o:o + K], cst[:, o + K:o + K + RR], cst[:, o + K + RR:o + K + 2 * RR]
        phase1 = ctx.enter_context(ExitStack())
        p1 = lambda name, shape, dt=F32: sb(name, shape, dt, phase1)
        WA = [p1(f"wa{i}", [P, C, D], F32R) for i in range(2)]
        W3T = [p1(f"w3t{i}", [P, C, D], F32R) for i in range(2)]
        W4T = [p1(f"w4t{i}", [P, C, D], F32R) for i in range(2)]
        WMR = [p1(f"wmr{i}", [P, C, WM], F32R) for i in range(2)]
        WK = [p1(f"wk{i}", [P, C, D], F32R) for i in range(2)]
        WV = [p1(f"wv{i}", [P, C, D], F32R) for i in range(2)]
        WQ = p1("wq", [P, C, D])
        WO = p1("wo", [P, C, D])
        cT = p1("cT", [P, C])
        u_bc = p1("u_bc", [P, D])
        beta = p1("beta", [P, 1])
        g_bias = p1("g_bias", [P, D])
        bqT, bkT, bvT = (p1(n, [P, C]) for n in ("bqT", "bkT", "bvT"))
        brn = p1("brn", [P, 1])
        r_bias = p1("r_bias", [RR, D])
        mhalf = p1("mhalf", [P, T])
        eps = p1("eps", [P, T])

        with ExitStack() as stage:
            s = lambda name, shape, dt=F32: sb(name, shape, dt, stage)
            raw = {n: s(f"raw_{n}", [P, C, D]) for n in ("w1", "w2", "w3", "w4", "wk", "wv", "wm")}
            raw["wr"] = s("raw_wr", [P, C])
            col = {n: s(f"col_{n}", [P, C]) for n in ("gb1", "gb2", "gb3", "g1", "b1", "bq", "bk", "bv")}
            rows = s("rows", [1, 6, D])
            fold = {n: s(f"fold_{n}", [P, C, WM]) for n in ("wk", "wv", "wm")}
            w4t = s("w4t", [P, C, D])
            b2_bc, b3_bc, b1_bc = (s(n, [P, C, P]) for n in ("b2_bc", "b3_bc", "b1_bc"))
            place = s("place", [P, C, RR])
            ones = s("ones", [P, P])
            loaded = sem("setup_loaded", stage)
            ones_set = sem("setup_ones", stage)
            made = sem("setup_made", stage)
            mults = sem("setup_products", stage)
            taken = sem("setup_taken", stage)
            low = sem("setup_low", stage)
            n_dma = 0
            with nc.Block() as block:
                loads = [(cst[:, :], consts)]
                loads += [(raw[n][:, :, :], chunks(w)) for n, w in
                          (("w1", gW1), ("w2", gW2), ("w3", gW3), ("w4", gW4), ("wk", Wk), ("wv", Wv), ("wm", Wm))]
                loads += [(WQ[:, :, :], chunks(Wq)), (WO[:, :, :], chunks(Wo)), (raw["wr"][:, :], column(Wr))]
                loads += [(col[n][:, :], column(v)) for n, v in
                          (("gb1", gb1), ("gb2", gb2), ("gb3", gb3), ("g1", g1), ("b1", b1), ("bq", bq), ("bk", bk), ("bv", bv))]
                loads += [(rows[0:1, i, :], row(v)) for i, v in enumerate((gb3, gb4, bo, bm))]
                loads += [(rows[0:1, 4, 0:1], br)]
                n_loads = len(loads)

                @block.sync
                def _(sp):
                    for dst, src in loads:
                        sp.dma_start(dst, src, allow_slow_non_contiguous=True).then_inc(loaded, 16)

                @block.vector
                def _(dve):
                    nc.vector.memset(mhalf[:, :], -0.5)
                    nc.vector.memset(eps[:, :], EPS)
                    for n in ("wk", "wv", "wm"):
                        nc.vector.memset(fold[n][:, :, D:WM], 0.0)
                    nc.vector.memset(ones[:, :], 1.0).then_inc(ones_set, 1)
                    nc.vector.memset(place[:, :, :], 0.0).then_inc(ones_set, 1)
                    dve.wait_ge(loaded, 16 * n_loads)
                    dve.wait_ge(ones_set, 2)
                    for c in range(C):
                        for bc, v in ((b2_bc, "gb2"), (b3_bc, "gb3"), (b1_bc, "b1")):
                            nc.vector.tensor_scalar(bc[:, c, :], ones[:, :], col[v][:, c:c + 1], None, ALU.mult)
                        nc.vector.tensor_scalar(place[:, c, ROW_BIAS:ROW_B1 + 1], ones[:, 0:2],
                                                col["b1"][:, c:c + 1], None, ALU.mult)
                        nc.vector.tensor_scalar(fold["wk"][:, c, 0:D], raw["wk"][:, c, :], col["g1"][:, c:c + 1], None, ALU.mult)
                        nc.vector.tensor_scalar(fold["wv"][:, c, 0:D], raw["wv"][:, c, :], col["g1"][:, c:c + 1], None, ALU.mult)
                        nc.vector.tensor_scalar(fold["wm"][:, c, 0:D], raw["wm"][:, c, :], col["g1"][:, c:c + 1], None, ALU.mult)
                        nc.vector.tensor_tensor(fold["wm"][:, c, D:D + 1], raw["wr"][:, c:c + 1], col["g1"][:, c:c + 1],
                                                ALU.mult).then_inc(made, 1)
                    dve.wait_ge(mults, 4)
                    for c in range(C):
                        nc.vector.tensor_scalar(WQ[:, c, :], WQ[:, c, :], col["g1"][:, c:c + 1], float(DH) ** -0.5,
                                                ALU.mult, ALU.mult)
                    dve.wait_ge(made, C)
                    for wide, (hi, lo) in (("wk", WK), ("wv", WV), ("wm", WMR)):
                        w = hi.shape[2]
                        nc.vector.tensor_copy(hi[:, :, :], fold[wide][:, :, 0:w]).then_inc(low, 1)
                    dve.wait_ge(low, 3)
                    for wide, (hi, lo) in (("wk", WK), ("wv", WV), ("wm", WMR)):
                        w = hi.shape[2]
                        nc.vector.tensor_tensor(lo[:, :, :], fold[wide][:, :, 0:w], hi[:, :, :], ALU.subtract)
                    v = bank[7]
                    nc.vector.tensor_copy(cT[:, :], v[:, 0:C])
                    nc.vector.tensor_copy(beta[:, :], v[:, 4:5])
                    nc.vector.tensor_tensor(bkT[:, :], v[:, 8:8 + C], col["bk"][:, :], ALU.add)
                    nc.vector.tensor_tensor(bvT[:, :], v[:, 12:12 + C], col["bv"][:, :], ALU.add)
                    nc.vector.tensor_tensor(bqT[:, :], v[:, 16:16 + C], col["bq"][:, :], ALU.add).then_inc(low, 1)
                    nc.vector.tensor_scalar(brn[:, :], v[:, 20:21], -1.0, None, ALU.mult)
                    dve.wait_ge(low, 4)
                    nc.vector.tensor_scalar(bqT[:, :], bqT[:, :], float(DH) ** -0.5, None, ALU.mult)
                    nc.vector.tensor_copy(u_bc[:, :], bank[6][:, 0:D])
                    nc.vector.tensor_copy(r_bias[:, :], bank[5][0:RR, 0:D])
                    for n, (hi, lo) in enumerate((WA, W3T, W4T)):
                        dve.wait_ge(mults, 5 + n)
                        for c in range(C):
                            nc.vector.tensor_copy(hi[:, c, :], bank[c][:, 0:D]).then_inc(low, 1)
                            if n == 2:
                                nc.vector.tensor_copy(w4t[:, c, :], bank[c][:, 0:D])
                            dve.wait_ge(low, 5 + 3 * n + c)
                            nc.vector.tensor_tensor(lo[:, c, :], bank[c][:, 0:D], hi[:, c, :], ALU.subtract).then_inc(taken, 1)
                    dve.wait_ge(mults, 8)
                    nc.vector.tensor_copy(g_bias[:, :], bank[4][:, 0:D])

                @block.tensor
                def _(pe):
                    pe.wait_ge(loaded, 16 * n_loads)
                    pe.wait_ge(made, C)
                    v = bank[7]

                    def by_feature(at, lhsT, rhs):
                        for m in range(C):
                            for c in range(C):
                                mm = nc.tensor.matmul(v[:, at + m:at + m + 1], lhsT[:, c, m * P:(m + 1) * P], rhs[:, c:c + 1],
                                                      start=(c == 0), stop=(c == C - 1))
                        return mm

                    by_feature(0, raw["w2"], col["gb1"])
                    for c in range(C):
                        nc.tensor.matmul(v[:, 4:5], b2_bc[:, c, :], col["gb1"][:, c:c + 1], start=(c == 0), stop=(c == C - 1))
                    for c in range(C):
                        nc.tensor.matmul(v[:, 20:21], b1_bc[:, c, :], raw["wr"][:, c:c + 1], start=(c == 0), stop=False)
                    nc.tensor.matmul(v[:, 20:21], ones[0:1, :], rows[0:1, 4, 0:1], start=False, stop=True).then_inc(mults, 1)
                    by_feature(8, raw["wk"], col["b1"])
                    by_feature(12, raw["wv"], col["b1"])
                    by_feature(16, WQ, col["b1"]).then_inc(mults, 1)
                    for c in range(C):
                        mm = nc.tensor.matmul(bank[6][:, 0:D], b2_bc[:, c, :], raw["w1"][:, c, :], start=(c == 0), stop=(c == C - 1))
                    mm.then_inc(mults, 1)
                    for c in range(C):
                        nc.tensor.matmul(bank[5][0:RR, 0:D], place[:, c, :], raw["wm"][:, c, :], start=(c == 0), stop=False)
                    nc.tensor.matmul(bank[5][0:RR, 0:D], picked[0:1, :], rows[0:1, 2, :], start=False, stop=False)
                    nc.tensor.matmul(bank[5][0:RR, 0:D], biasrow[0:1, :], rows[0:1, 3, :], start=False, stop=True).then_inc(mults, 1)
                    for m in range(C):
                        for c in range(C):
                            mm = nc.tensor.matmul(bank[m][:, 0:D], raw["w1"][:, c, m * P:(m + 1) * P], raw["w2"][:, c, :],
                                                  start=(c == 0), stop=(c == C - 1))
                    mm.then_inc(mults, 1)
                    for n, w in enumerate(("w3", "w4")):
                        pe.wait_ge(taken, C * (n + 1))
                        for m in range(C):
                            for c in range(C):
                                mm = nc.tensor.transpose(bank[m][:, c * P:(c + 1) * P], raw[w][:, c, m * P:(m + 1) * P], ident)
                        mm.then_inc(mults, 1)
                    pe.wait_ge(taken, 3 * C)
                    for c in range(C):
                        nc.tensor.matmul(bank[4][:, 0:D], b3_bc[:, c, :], w4t[:, c, :], start=(c == 0), stop=False)
                    nc.tensor.matmul(bank[4][:, 0:D], ones[0:1, :], rows[0:1, 0, :], start=False, stop=False)
                    nc.tensor.matmul(bank[4][:, 0:D], ones[0:1, :], rows[0:1, 1, :], start=False, stop=True).then_inc(mults, 1)

        xn = p1("xn", [P, T, D])
        adj_in = p1("adj_in", [P, T, L], I32)
        XT = [p1(f"xt{i}", [P, C, GT], F32R) for i in range(2)]
        TT = [p1(f"tt{i}", [P, C, GT], F32R) for i in range(2)]
        keep = p1("keep", [P, 2, T, L])
        neg = p1("neg", [P, 2, T, L])
        lg = p1("lg", [P, 2, T, L])
        prior = p1("prior", [P, T, L])
        Fb, Nb = (p1(n, [P, T, P]) for n in ("Fb", "Nb"))
        FT, NT = (p1(n, [P, T, P]) for n in ("FT", "NT"))
        g_sb = p1("g_sb", [P, T, D])
        xg = p1("xg", [P, T, D])
        x1 = p1("x1", [P, T, D])
        hid = p1("hid", [P, T, D])
        nh = p1("nh", [P, T, D])
        NHT = [p1(f"nht{i}", [P, C, GT], F32R) for i in range(2)]
        y_sb = p1("y_sb", [P, T, WM])
        kT = p1("kT", [P, C, GT])
        v_sb = p1("v_sb", [P, T, D])
        q_blk = p1("q_blk", [P, C, GB, H, K])
        prob = p1("prob", [H * K, GB, L])
        p_blk = p1("p_blk", [P, C, T, 2, HC * K])
        ctxT = p1("ctxT", [P, C, GB * K])
        pool_f = p1("pool_f", [P, C, GB])
        POOL = [p1(f"pool{i}", [P, C, RR], F32R) for i in range(2)]
        sel_sb = p1("sel_sb", [P, C, T, SELW])
        gath = p1("gath", [P, T, SELW])
        scat = p1("scat", [P, T, RR])
        scatT = p1("scatT", [RR, T, P])
        r_sb = p1("r_sb", [RR, D])
        diag = p1("diag", [P, T, L])
        bc = p1("bc", [P, T, L])
        cmp = p1("cmp", [P, 2, T, L])
        stats = p1("stats", [P, T, 6])
        mv = p1("mv", [P, T, 2])
        mvh = p1("mvh", [P, T, 2])
        small = p1("small", [P, 24, 8])
        junk = cmp[:, :, :, :].rearrange("p a t m -> p (a t m)")[:, 0:D]

        with ExitStack() as c1:
            q = {n: sem(n, c1) for n in (
                "x_loaded adj_loaded residual_stored normed_stored zeroed zeroed_pool "
                "var_ready rstd_ready xn_ready xg_ready masks_ready rn_ready xt_mm xt_hi xt_lo t_mm t_hi t_lo att_mm att_taken "
                "logits_ready exp_done product_ready exp2_done blocks_ready fn_mm fn_taken y_mm y_hi y_lo g_mm g_taken g_added "
                "ng_mm ng_hi ng_lo x1_mm x1_taken "
                "var1_ready rstd1_ready nh_ready nht_mm nht_hi nht_lo wm_mm wm_taken k_mm k_taken z_exp score_diag bc_mm bc_taken "
                "v_mm v_taken picks_ready sel_mm sel_taken pool_hi pool_lo q_mm q_taken lg_mm lg_taken lgexp prob_ready pt_mm pt_taken "
                "pv_mm pv_taken r_mm r_taken st_mm st_taken out_mm h_ready "
                "xh_ready var2_ready rstd2_ready n2_ready dve_step pool_step").split()}
            def sm(i, w=T):
                return small[:, i, 0:w]

            DVE_STEPS, POOL_STEPS = 45, 4

            def parts(i):
                return (slice(0, L), slice(L, P))[i]

            with nc.Block() as block:
                @block.sync
                def _(sp):
                    with sp.Fori(0, G) as g:
                        sp.wait_ge(q["y_mm"], g * 3)
                        sp.wait_ge(q["rn_ready"], g)
                        sp.wait_ge(q["xg_ready"], g)
                        sp.dma_start(xn[:, :, :], x_g[g]).then_inc(q["x_loaded"], 16)
                        sp.wait_ge(q["masks_ready"], g)
                        sp.dma_start(adj_in[:, :, :], adj_g[g]).then_inc(q["adj_loaded"], 16)
                        sp.wait_ge(q["xh_ready"], g + 1)
                        sp.dma_start(xh_g[g], x1[:, :, :]).then_inc(q["residual_stored"], 16)
                        sp.wait_ge(q["n2_ready"], g + 1)
                        sp.dma_start(n2_g[g], nh[:, :, :]).then_inc(q["normed_stored"], 16)
                    sp.wait_ge(q["residual_stored"], 16 * G)
                    sp.wait_ge(q["normed_stored"], 16 * G)

                @block.gpsimd
                def _(pool):
                    nc.gpsimd.memset(Fb[:, :, :], 0.0)
                    nc.gpsimd.memset(Nb[:, :, :], 0.0)
                    nc.gpsimd.memset(q_blk[:, :, :, :, :], 0.0)
                    nc.gpsimd.memset(p_blk[:, :, :, :, :], 0.0)
                    nc.gpsimd.memset(scat[:, :, :], 0.0)
                    nc.gpsimd.memset(gath[:, :, :], 0.0).then_inc(q["zeroed_pool"], 1)
                    with pool.Fori(0, G) as g:
                        n = [0]

                        def step(ins):
                            n[0] += 1
                            ins.then_inc(q["pool_step"], 1)
                            pool.wait_ge(q["pool_step"], g * POOL_STEPS + n[0])

                        pool.wait_ge(q["x_loaded"], g * 16 + 16)
                        nc.gpsimd.tensor_tensor(xg[:, :, :], xn[:, :, :], g_bias[:, :].unsqueeze(1).to_broadcast([P, T, D]),
                                                ALU.add).then_inc(q["xg_ready"], 1)
                        pool.wait_ge(q["var_ready"], g + 1)
                        nc.gpsimd.tensor_tensor(sm(1), sm(0), mhalf[:, :], ALU.pow).then_inc(q["rstd_ready"], 1)
                        pool.wait_ge(q["var1_ready"], g + 1)
                        step(nc.gpsimd.tensor_tensor(sm(3), sm(2), mhalf[:, :], ALU.pow))
                        step(nc.gpsimd.tensor_tensor(sm(4), mvh[:, :, 1], sm(3), ALU.mult))
                        step(nc.gpsimd.tensor_tensor(sm(4), sm(4), sm(3), ALU.mult))
                        step(nc.gpsimd.tensor_tensor(sm(4), sm(4), eps[:, :], ALU.add))
                        nc.gpsimd.tensor_tensor(sm(5), sm(4), mhalf[:, :], ALU.pow).then_inc(q["rstd1_ready"], 1)
                        pool.wait_ge(q["var2_ready"], g + 1)
                        nc.gpsimd.tensor_tensor(sm(7), sm(6), mhalf[:, :], ALU.pow).then_inc(q["rstd2_ready"], 1)
                        pool.wait_ge(q["h_ready"], g * T + T)
                        nc.gpsimd.tensor_tensor(x1[:, :, :], x1[:, :, :], y_sb[:, :, 0:D], ALU.add).then_inc(q["xh_ready"], 1)
                        assert n[0] == POOL_STEPS, n

                @block.scalar
                def _(act):
                    with act.Fori(0, G) as g:
                        for c in range(C):
                            act.wait_ge(q["xt_mm"], g * 3 + c + 1)
                            nc.scalar.copy(XT[0][:, c, :], bank[c][:, :]).then_inc(q["xt_hi"], 1)
                        for c in range(C):
                            act.wait_ge(q["t_mm"], g * 3 + c + 1)
                            nc.scalar.activation(TT[0][:, c, :], bank[(3, 0, 1)[c]][:, :], ACT.Identity,
                                                 bias=cT[:, c:c + 1]).then_inc(q["t_hi"], 1)
                        act.wait_ge(q["logits_ready"], g * 2 + 1)
                        nc.scalar.activation(prior[:, :, :], prior[:, :, :], ACT.Exp).then_inc(q["exp_done"], 1)
                        act.wait_ge(q["logits_ready"], g * 2 + 2)
                        nc.scalar.activation(lg[:, :, :, :], lg[:, :, :, :], ACT.Exp).then_inc(q["exp_done"], 1)
                        act.wait_ge(q["product_ready"], g + 1)
                        nc.scalar.activation(prior[:, :, :], prior[:, :, :], ACT.Exp).then_inc(q["exp2_done"], 1)
                        for n, (dst, b) in enumerate(((FT, 3), (NT, 0))):
                            act.wait_ge(q["fn_mm"], g * 2 + n + 1)
                            nc.scalar.copy(dst[:, :, :], bank[b][:, :]).then_inc(q["fn_taken"], 1)
                        for c in range(C):
                            act.wait_ge(q["y_mm"], g * 3 + c + 1)
                            nc.scalar.copy(XT[0][:, c, :], bank[1 + c][:, :]).then_inc(q["y_hi"], 1)
                        for t in range(T):
                            act.wait_ge(q["g_mm"], g * T + t + 1)
                            nc.scalar.copy(g_sb[:, t, :], bank[t][:, 0:D]).then_inc(q["g_taken"], 1)
                        for c in range(C):
                            act.wait_ge(q["ng_mm"], g * 3 + c + 1)
                            nc.scalar.copy(TT[0][:, c, :], bank[c][:, :]).then_inc(q["ng_hi"], 1)
                        for c in range(C):
                            act.wait_ge(q["nht_mm"], g * 3 + c + 1)
                            nc.scalar.copy(NHT[0][:, c, :], bank[4 + c][:, :]).then_inc(q["nht_hi"], 1)
                        act.wait_ge(q["xh_ready"], g)
                        act.wait_ge(q["n2_ready"], g)
                        for t in range(T):
                            act.wait_ge(q["wm_mm"], g * T + t + 1)
                            nc.scalar.copy(y_sb[:, t, :], bank[(7, 4, 5, 6)[t]][:, 0:WM]).then_inc(q["wm_taken"], 1)
                        act.wait_ge(q["wm_taken"], g * T + T)
                        nc.scalar.activation(sm(8), y_sb[:, :, D], ACT.Exp, bias=brn[:, :], scale=-1.0).then_inc(q["z_exp"], 1)
                        for c in range(C):
                            act.wait_ge(q["k_mm"], g * 3 + c + 1)
                            nc.scalar.activation(kT[:, c, :], bank[(7, 4, 5)[c]][:, :], ACT.Identity,
                                                 bias=bkT[:, c:c + 1]).then_inc(q["k_taken"], 1)
                        for t in range(T):
                            act.wait_ge(q["v_mm"], g * T + t + 1)
                            nc.scalar.copy(v_sb[:, t, :], bank[(7, 4, 5, 6)[t]][:, 0:D]).then_inc(q["v_taken"], 1)
                        act.wait_ge(q["sel_mm"], g + 1)
                        nc.scalar.copy(sel_sb[:, :, :, :], bank[7][:, 0:C * T * SELW].rearrange("p (c t k) -> p c t k", c=C, t=T))\
                            .then_inc(q["sel_taken"], 1)
                        act.wait_ge(q["lg_taken"], g + 1)
                        nc.scalar.activation(prob[:, :, :], prob[:, :, :], ACT.Exp).then_inc(q["lgexp"], 1)
                        act.wait_ge(q["pt_mm"], g + 1)
                        pt = bank[6][:, 0:T * H * K].rearrange("p (t c k) -> p c t k", t=T, c=C)
                        for i in range(2):
                            nc.scalar.copy(p_blk[parts(i), :, :, i, :], pt[parts(i), :, :, :]).then_inc(q["pt_taken"], 1)
                        act.wait_ge(q["st_mm"], g + 1)
                        nc.scalar.copy(scatT[:, :, :], bank[6][0:RR, :]).then_inc(q["st_taken"], 1)

                @block.vector
                def _(dve):
                    dve.wait_ge(q["zeroed_pool"], 1)
                    nc.vector.memset(pool_f[:, :, :], 0.0)
                    nc.vector.memset(POOL[0][:, :, :].bitcast(F32), 0.0).then_inc(q["zeroed"], 1)
                    nc.vector.memset(POOL[1][:, :, :].bitcast(F32), 0.0).then_inc(q["zeroed"], 1)
                    dve.wait_ge(q["zeroed"], 2)
                    with dve.Fori(0, G) as g:
                        n = [0]

                        def step(ins):
                            n[0] += 1
                            ins.then_inc(q["dve_step"], 1)
                            dve.wait_ge(q["dve_step"], g * DVE_STEPS + n[0])

                        def wide(a):
                            return a.unsqueeze(2).to_broadcast([a.shape[0], T, L])

                        def stat(src, into):
                            for t in range(T):
                                ins = nc.vector.bn_stats(stats[:, t, :], src[:, t, 0:D])
                            step(ins)
                            nc.vector.tensor_copy(small[:, 23, 7:8], stats[:, 0, 0:1])
                            for t in range(T):
                                ins = nc.vector.bn_aggr(into[:, t, :], stats[:, t, :])
                            step(ins)

                        dve.wait_ge(q["x_loaded"], g * 16 + 16)
                        stat(xn, mv)
                        nc.vector.tensor_scalar(sm(0), mv[:, :, 1], EPS, None, ALU.add).then_inc(q["var_ready"], 1)
                        dve.wait_ge(q["adj_loaded"], g * 16 + 16)
                        nc.vector.tensor_scalar(keep[:, 0, :, :], adj_in[:, :, :], 0, None, ALU.not_equal)
                        nc.vector.tensor_scalar(keep[:, 1, :, :], adj_in[:, :, :], 1, None, ALU.not_equal)
                        nc.vector.tensor_scalar(neg[:, 0, :, :], adj_in[:, :, :], 0, NEG, ALU.is_equal, ALU.mult)
                        step(nc.vector.tensor_scalar(neg[:, 1, :, :], adj_in[:, :, :], 1, NEG, ALU.is_equal, ALU.mult))
                        step(nc.vector.scalar_tensor_tensor(out=prior[:, :, :], in0=adj_in[:, :, :], scalar=6.0, in1=neg[:, 0, :, :],
                                                            op0=ALU.mult, op1=ALU.add))
                        step(nc.vector.tensor_reduce(sm(10), prior[:, :, :], AX.X, ALU.max))
                        nc.vector.tensor_tensor(prior[:, :, :], prior[:, :, :], wide(sm(10)), ALU.subtract)\
                            .then_inc(q["logits_ready"], 1)
                        dve.wait_ge(q["rstd_ready"], g + 1)
                        dve.wait_ge(q["xg_ready"], g + 1)
                        for t in range(T):
                            nc.vector.tensor_scalar(xn[:, t, :], xn[:, t, :], mv[:, t, 0:1], small[:, 1, t:t + 1],
                                                    ALU.subtract, ALU.mult).then_inc(q["xn_ready"], 1)
                        dve.wait_ge(q["xn_ready"], g * T + T)
                        for t in range(T):
                            ins = nc.vector.tensor_tensor_reduce(out=junk, in0=xn[:, t, :], in1=u_bc[:, :], scale=1.0,
                                                                 scalar=0.0, op0=ALU.mult, op1=ALU.add,
                                                                 accum_out=small[:, 11, t:t + 1])
                            step(ins)
                        step(nc.vector.tensor_scalar(sm(11), sm(11), beta[:, 0:1], None, ALU.add))
                        nc.vector.tensor_copy(sm(12), sm(11)).then_inc(q["rn_ready"], 1)
                        for c in range(C):
                            dve.wait_ge(q["xt_hi"], g * 3 + c + 1)
                            nc.vector.tensor_tensor(XT[1][:, c, :], bank[c][:, :], XT[0][:, c, :], ALU.subtract)\
                                .then_inc(q["xt_lo"], 1)
                        dve.wait_ge(q["exp_done"], g * 2 + 1)
                        step(nc.vector.tensor_reduce(sm(13), prior[:, :, :], AX.X, ALU.add))
                        for c in range(C):
                            dve.wait_ge(q["t_hi"], g * 3 + c + 1)
                            nc.vector.scalar_tensor_tensor(out=TT[1][:, c, :], in0=bank[(3, 0, 1)[c]][:, :], scalar=cT[:, c:c + 1],
                                                           in1=TT[0][:, c, :], op0=ALU.add, op1=ALU.subtract)\
                                .then_inc(q["t_lo"], 1)
                        dve.wait_ge(q["att_mm"], g + 1)
                        att = bank[2][:, :].rearrange("p (t m) -> p t m", t=T)
                        for i in range(2):
                            r = parts(i)
                            ins = nc.vector.tensor_tensor(bc[r, :, :], att[r, :, i * L:(i + 1) * L], wide(sm(12)[r]), ALU.add)
                        step(ins)
                        for i in range(2):
                            ins = nc.vector.scalar_tensor_tensor(out=lg[:, i, :, :], in0=bc[:, :, :], scalar=1.0 / 28.0,
                                                                 in1=keep[:, i, :, :], op0=ALU.mult, op1=ALU.mult)
                        step(ins)
                        step(nc.vector.tensor_tensor(lg[:, :, :, :], lg[:, :, :, :], neg[:, :, :, :], ALU.add))
                        lgf = lg[:, :, :, :].rearrange("p a t m -> p (a t) m")
                        step(nc.vector.tensor_reduce(small[:, 14, 0:8], lgf, AX.X, ALU.max))
                        nc.vector.tensor_tensor(lgf, lgf, small[:, 14, 0:8].unsqueeze(2).to_broadcast([P, 8, L]), ALU.subtract)\
                            .then_inc(q["logits_ready"], 1)
                        dve.wait_ge(q["exp_done"], g * 2 + 2)
                        step(nc.vector.tensor_reduce(small[:, 15, 0:8], lgf, AX.X, ALU.add))
                        step(nc.vector.tensor_tensor(sm(16), sm(13), small[:, 15, 0:4], ALU.mult))
                        step(nc.vector.reciprocal(sm(16), sm(16)))
                        nc.vector.reciprocal(sm(17), small[:, 15, 4:8])
                        step(nc.vector.tensor_tensor(prior[:, :, :], prior[:, :, :], lg[:, 0, :, :], ALU.mult))
                        step(nc.vector.tensor_tensor(prior[:, :, :], prior[:, :, :], wide(sm(16)), ALU.mult))
                        step(nc.vector.tensor_tensor(prior[:, :, :], prior[:, :, :], keep[:, 0, :, :], ALU.mult))
                        step(nc.vector.tensor_tensor(prior[:, :, :], prior[:, :, :], neg[:, 0, :, :], ALU.add))
                        step(nc.vector.tensor_reduce(sm(10), prior[:, :, :], AX.X, ALU.max))
                        nc.vector.tensor_tensor(prior[:, :, :], prior[:, :, :], wide(sm(10)), ALU.subtract)\
                            .then_inc(q["product_ready"], 1)
                        for i in range(2):
                            r = parts(i)
                            ins = nc.vector.tensor_tensor(Nb[r, :, i * L:(i + 1) * L], lg[r, 1, :, :], wide(sm(17)[r]), ALU.mult)
                        dve.wait_ge(q["exp2_done"], g + 1)
                        step(nc.vector.tensor_reduce(sm(18), prior[:, :, :], AX.X, ALU.add))
                        step(nc.vector.reciprocal(sm(18), sm(18)))
                        for i in range(2):
                            r = parts(i)
                            ins = nc.vector.tensor_tensor(Fb[r, :, i * L:(i + 1) * L], prior[r, :, :], wide(sm(18)[r]), ALU.mult)
                        ins.then_inc(q["blocks_ready"], 1)
                        dve.wait_ge(q["blocks_ready"], g + 1)
                        nc.vector.tensor_copy(sm(19), sm(18)).then_inc(q["masks_ready"], 1)
                        for c in range(C):
                            dve.wait_ge(q["y_hi"], g * 3 + c + 1)
                            nc.vector.tensor_tensor(XT[1][:, c, :], bank[1 + c][:, :], XT[0][:, c, :], ALU.subtract)\
                                .then_inc(q["y_lo"], 1)
                        for t in range(T):
                            dve.wait_ge(q["g_taken"], g * T + t + 1)
                            nc.vector.tensor_tensor(xg[:, t, :], bank[t][:, 0:D], xg[:, t, :], ALU.add)\
                                .then_inc(q["g_added"], 1)
                        for c in range(C):
                            dve.wait_ge(q["ng_hi"], g * 3 + c + 1)
                            nc.vector.tensor_tensor(TT[1][:, c, :], bank[c][:, :], TT[0][:, c, :], ALU.subtract)\
                                .then_inc(q["ng_lo"], 1)
                        dve.wait_ge(q["residual_stored"], g * 16)
                        for t in range(T):
                            dve.wait_ge(q["x1_mm"], g * T + t + 1)
                            nc.vector.tensor_tensor(x1[:, t, :], bank[(3, 0, 1, 2)[t]][:, 0:D], xg[:, t, :], ALU.add)\
                                .then_inc(q["x1_taken"], 1)
                        dve.wait_ge(q["x1_taken"], g * T + T)
                        stat(x1, mvh)
                        nc.vector.tensor_scalar(sm(2), mvh[:, :, 1], EPS, None, ALU.add).then_inc(q["var1_ready"], 1)
                        dve.wait_ge(q["rstd1_ready"], g + 1)
                        for t in range(T):
                            ins = nc.vector.tensor_scalar(hid[:, t, :], x1[:, t, :], mvh[:, t, 0:1], small[:, 3, t:t + 1],
                                                          ALU.subtract, ALU.mult)
                        step(ins)
                        dve.wait_ge(q["normed_stored"], g * 16)
                        for t in range(T):
                            nc.vector.tensor_scalar(nh[:, t, :], hid[:, t, :], small[:, 5, t:t + 1], None, ALU.mult)\
                                .then_inc(q["nh_ready"], 1)
                        for c in range(C):
                            dve.wait_ge(q["nht_hi"], g * 3 + c + 1)
                            nc.vector.tensor_tensor(NHT[1][:, c, :], bank[4 + c][:, :], NHT[0][:, c, :], ALU.subtract)\
                                .then_inc(q["nht_lo"], 1)
                        dve.wait_ge(q["z_exp"], g + 1)
                        step(nc.vector.tensor_scalar(sm(9), sm(8), 1.0, None, ALU.add))
                        step(nc.vector.reciprocal(sm(9), sm(9)))
                        nc.vector.tensor_tensor(diag[:, :, :], node.unsqueeze(1).to_broadcast([P, T, L]), wide(sm(9)), ALU.mult)\
                            .then_inc(q["score_diag"], 1)
                        dve.wait_ge(q["bc_mm"], g + 1)
                        nc.vector.tensor_copy(bc[:, :, :], bank[6][:, 0:T * L]).then_inc(q["bc_taken"], 1)
                        dve.wait_ge(q["bc_taken"], g + 1)
                        nc.vector.tensor_reduce(sm(20), bc[:, :, :], AX.X, ALU.add)
                        step(nc.vector.tensor_tensor(cmp[:, 0, :, :], bc[:, :, :], node.unsqueeze(1).to_broadcast([P, T, L]), ALU.mult))
                        step(nc.vector.tensor_reduce(sm(9), cmp[:, 0, :, :], AX.X, ALU.add))
                        nc.vector.tensor_tensor(cmp[:, 0, :, :], bc[:, :, :], wide(sm(9)), ALU.is_lt)
                        step(nc.vector.tensor_tensor(cmp[:, 1, :, :], bc[:, :, :], wide(sm(9)), ALU.is_equal))
                        step(nc.vector.tensor_tensor(cmp[:, 1, :, :], cmp[:, 1, :, :], earlier.unsqueeze(1).to_broadcast([P, T, L]), ALU.mult))
                        step(nc.vector.tensor_tensor(cmp[:, 0, :, :], cmp[:, 0, :, :], cmp[:, 1, :, :], ALU.add))
                        step(nc.vector.tensor_reduce(sm(21), cmp[:, 0, :, :], AX.X, ALU.add))
                        nc.vector.tensor_scalar(sm(22), sm(21), float(K), None, ALU.is_ge)
                        step(nc.vector.tensor_scalar(sm(23), sm(20), 1e-6, None, ALU.add))
                        step(nc.vector.reciprocal(sm(23), sm(23)))
                        nc.vector.tensor_tensor(sm(20), sm(20), sm(23), ALU.mult)
                        nc.vector.tensor_tensor(sm(19), sm(9), sm(22), ALU.mult)
                        step(nc.vector.tensor_tensor(sm(18), sm(9), sm(23), ALU.mult))
                        nc.vector.tensor_copy(scat[:, :, ROW_BIAS], sm(22))
                        nc.vector.tensor_tensor(scat[:, :, ROW_B1], sm(19), sm(20), ALU.mult)
                        flat = scat[:, :, :].rearrange("p t k -> p (t k)")
                        for i in range(2):
                            r = parts(i)
                            nc.vector.tensor_copy(gath[r, :, 2 * K + i], sm(18)[r])
                            nc.vector.tensor_copy(flat[r, ROW_POOL + i:ROW_POOL + i + (T - 1) * (RR + 2) + 1:RR + 2], sm(19)[r])
                            rank_b = sm(21)[r].unsqueeze(2).to_broadcast([L, T, K])
                            iota_b = iota[r].unsqueeze(1).to_broadcast([L, T, K])
                            nc.vector.tensor_tensor(gath[r, :, i * K:(i + 1) * K], iota_b, rank_b, ALU.is_equal)
                            for t in range(T):
                                ins = nc.vector.tensor_scalar(scat[r, t, (2 * t + i) * K:(2 * t + i + 1) * K], iota[r],
                                                              small[r, 21, t:t + 1], None, ALU.is_equal)
                        ins.then_inc(q["picks_ready"], 1)
                        dve.wait_ge(q["picks_ready"], g + 1)
                        for t in range(T):
                            nc.vector.scalar_tensor_tensor(out=y_sb[:, t, 0:D], in0=y_sb[:, t, 0:D], scalar=small[:, 22, t:t + 1],
                                                           in1=hid[:, t, :], op0=ALU.mult, op1=ALU.add)
                        dve.wait_ge(q["sel_taken"], g + 1)
                        step(nc.vector.tensor_copy(pool_f[:, :, :].rearrange("p c (t k) -> p c t k", t=T), sel_sb[:, :, :, 2 * K:SELW]))
                        nc.vector.tensor_copy(POOL[0][:, :, ROW_POOL:ROW_BIAS], pool_f[:, :, :]).then_inc(q["pool_hi"], 1)
                        dve.wait_ge(q["pool_hi"], g + 1)
                        nc.vector.tensor_tensor(POOL[1][:, :, ROW_POOL:ROW_BIAS], pool_f[:, :, :], POOL[0][:, :, ROW_POOL:ROW_BIAS],
                                                ALU.subtract).then_inc(q["pool_lo"], 1)
                        dve.wait_ge(q["q_mm"], g + 1)
                        qp = bank[4][:, 0:C * GB * K].rearrange("p (c b k) -> p c b k", c=C, b=GB)
                        for h in range(HC):
                            r = slice(h * DH, (h + 1) * DH)
                            for c in range(C):
                                ins = nc.vector.tensor_scalar(q_blk[r, c, :, c * HC + h, :], qp[r, c, :, :], bqT[r, c:c + 1], None,
                                                              ALU.add)
                        ins.then_inc(q["q_taken"], 1)
                        dve.wait_ge(q["lg_mm"], g + 1)
                        lgp = bank[5][0:H * K, :].rearrange("p (b m) -> p b m", b=GB)
                        mx = small[0:H * K, 10, 0:GB]
                        step(nc.vector.tensor_reduce(mx, lgp, AX.X, ALU.max))
                        nc.vector.tensor_tensor(prob[:, :, :], lgp, mx.unsqueeze(2).to_broadcast([H * K, GB, L]), ALU.subtract)\
                            .then_inc(q["lg_taken"], 1)
                        dve.wait_ge(q["lgexp"], g + 1)
                        step(nc.vector.tensor_reduce(mx, prob[:, :, :], AX.X, ALU.add))
                        step(nc.vector.reciprocal(mx, mx))
                        nc.vector.tensor_tensor(prob[:, :, :], prob[:, :, :], mx.unsqueeze(2).to_broadcast([H * K, GB, L]), ALU.mult)\
                            .then_inc(q["prob_ready"], 1)
                        for n2 in range(2):
                            dve.wait_ge(q["pv_mm"], g * 2 + n2 + 1)
                            pv = bank[(7, 4)[n2]][:, 0:C * 4 * HC * K].rearrange("p (c b h k) -> p c b h k", c=C, b=4, h=HC)
                            for h in range(HC):
                                r = slice(h * DH, (h + 1) * DH)
                                for c in range(C):
                                    dst = ctxT[r, c, n2 * 4 * K:(n2 + 1) * 4 * K].rearrange("p (b k) -> p b k", b=4)
                                    ins = nc.vector.tensor_scalar(dst, pv[r, c, :, h, :], bvT[r, c:c + 1], None, ALU.add)
                            ins.then_inc(q["pv_taken"], 1)
                        dve.wait_ge(q["r_mm"], g + 1)
                        nc.vector.tensor_tensor(r_sb[:, :], bank[5][0:RR, 0:D], r_bias[:, :], ALU.add).then_inc(q["r_taken"], 1)
                        for t in range(T):
                            dve.wait_ge(q["out_mm"], g * T + t + 1)
                            nc.vector.tensor_tensor(y_sb[:, t, 0:D], bank[(7, 4, 5, 6)[t]][:, 0:D], y_sb[:, t, 0:D], ALU.add)\
                                .then_inc(q["h_ready"], 1)
                        dve.wait_ge(q["h_ready"], g * T + T)
                        stat(y_sb, mvh)
                        nc.vector.tensor_scalar(sm(6), mvh[:, :, 1], EPS, None, ALU.add).then_inc(q["var2_ready"], 1)
                        dve.wait_ge(q["rstd2_ready"], g + 1)
                        for t in range(T):
                            ins = nc.vector.tensor_scalar(nh[:, t, :], y_sb[:, t, 0:D], mvh[:, t, 0:1], small[:, 7, t:t + 1],
                                                          ALU.subtract, ALU.mult)
                        ins.then_inc(q["n2_ready"], 1)
                        assert n[0] == DVE_STEPS, n

                @block.tensor
                def _(pe):
                    pe.wait_ge(q["zeroed"], 2)

                    def split(out, lhs, rhs, sems, **kw):
                        n = len(lhs[0])
                        for c in range(n):
                            for i, (a, b) in enumerate(ONES):
                                mm = nc.tensor.matmul(out, lhs[a][c], rhs[b][c], start=(c == 0 and i == 0),
                                                      stop=(c == n - 1 and i == 2), **kw)
                        return mm

                    with pe.Fori(0, G) as g:
                        pe.wait_ge(q["x1_taken"], g * T)
                        pe.wait_ge(q["xn_ready"], g * T + T)
                        for c in range(C):
                            for t in range(T):
                                mm = nc.tensor.transpose(bank[c][:, t * P:(t + 1) * P], xn[:, t, c * P:(c + 1) * P], ident)
                            mm.then_inc(q["xt_mm"], 1)
                        pe.wait_ge(q["xt_lo"], g * 3 + 3)
                        for m in range(C):
                            split(bank[(3, 0, 1)[m]][:, :], [[WA[a][:, c, m * P:(m + 1) * P] for c in range(C)] for a in range(2)],
                                  [[XT[a][:, c, :] for c in range(C)] for a in range(2)], None).then_inc(q["t_mm"], 1)
                        pe.wait_ge(q["t_lo"], g * 3 + 3)
                        for t in range(T):
                            ts = slice(t * P, (t + 1) * P)
                            mm = split(bank[2][:, ts], [[TT[a][:, c, ts] for c in range(C)] for a in range(2)],
                                       [[XT[a][:, c, ts] for c in range(C)] for a in range(2)], None)
                        mm.then_inc(q["att_mm"], 1)
                        pe.wait_ge(q["blocks_ready"], g + 1)
                        for src, b in ((Fb, 3), (Nb, 0)):
                            for t in range(T):
                                mm = nc.tensor.transpose(bank[b][:, t * P:(t + 1) * P], src[:, t, :], ident)
                            mm.then_inc(q["fn_mm"], 1)
                        pe.wait_ge(q["fn_taken"], g * 2 + 1)
                        for c in range(C):
                            for t in range(T):
                                mm = nc.tensor.matmul(bank[1 + c][:, t * P:(t + 1) * P], xn[:, t, c * P:(c + 1) * P], FT[:, t, :],
                                                      start=True, stop=True)
                            mm.then_inc(q["y_mm"], 1)
                        pe.wait_ge(q["y_lo"], g * 3 + 3)
                        pe.wait_ge(q["fn_taken"], g * 2 + 2)
                        for t in range(T):
                            ts = slice(t * P, (t + 1) * P)
                            split(bank[t][:, 0:D], [[XT[a][:, c, ts] for c in range(C)] for a in range(2)],
                                  [[W3T[a][:, c, :] for c in range(C)] for a in range(2)], None).then_inc(q["g_mm"], 1)
                        pe.wait_ge(q["g_added"], g * T + T)
                        for c in range(C):
                            for t in range(T):
                                mm = nc.tensor.matmul(bank[c][:, t * P:(t + 1) * P], g_sb[:, t, c * P:(c + 1) * P], NT[:, t, :],
                                                      start=True, stop=True)
                            mm.then_inc(q["ng_mm"], 1)
                        pe.wait_ge(q["ng_lo"], g * 3 + 3)
                        for t in range(T):
                            ts = slice(t * P, (t + 1) * P)
                            split(bank[(3, 0, 1, 2)[t]][:, 0:D], [[TT[a][:, c, ts] for c in range(C)] for a in range(2)],
                                  [[W4T[a][:, c, :] for c in range(C)] for a in range(2)], None).then_inc(q["x1_mm"], 1)
                        pe.wait_ge(q["h_ready"], g * T)
                        pe.wait_ge(q["nh_ready"], g * T + T)
                        for c in range(C):
                            for t in range(T):
                                mm = nc.tensor.transpose(bank[4 + c][:, t * P:(t + 1) * P], nh[:, t, c * P:(c + 1) * P], ident)
                            mm.then_inc(q["nht_mm"], 1)
                        pe.wait_ge(q["nht_lo"], g * 3 + 3)
                        nhT = [[[NHT[a][:, c, t * P:(t + 1) * P] for c in range(C)] for a in range(2)] for t in range(T)]
                        for t in range(T):
                            split(bank[(7, 4, 5, 6)[t]][:, 0:WM], nhT[t], [[WMR[a][:, c, :] for c in range(C)] for a in range(2)],
                                  None).then_inc(q["wm_mm"], 1)
                        for m in range(C):
                            pe.wait_ge(q["wm_taken"], g * T + m + 1)
                            split(bank[(7, 4, 5)[m]][:, :], [[WK[a][:, c, m * P:(m + 1) * P] for c in range(C)] for a in range(2)],
                                  [[NHT[a][:, c, :] for c in range(C)] for a in range(2)], None).then_inc(q["k_mm"], 1)
                        pe.wait_ge(q["wm_taken"], g * T + 4)
                        pe.wait_ge(q["score_diag"], g + 1)
                        nc.tensor.matmul(bank[6][:, 0:T * L], same, diag[:, :, :], start=True, stop=True).then_inc(q["bc_mm"], 1)
                        for t in range(T):
                            if t < 3:
                                pe.wait_ge(q["k_taken"], g * 3 + t + 1)
                            else:
                                pe.wait_ge(q["bc_taken"], g + 1)
                            split(bank[(7, 4, 5, 6)[t]][:, 0:D], nhT[t], [[WV[a][:, c, :] for c in range(C)] for a in range(2)],
                                  None).then_inc(q["v_mm"], 1)
                        pe.wait_ge(q["v_taken"], g * T + 1)
                        pe.wait_ge(q["picks_ready"], g + 1)
                        for c in range(C):
                            for t in range(T):
                                at = (c * T + t) * SELW
                                mm = nc.tensor.matmul(bank[7][:, at:at + SELW], nh[:, t, c * P:(c + 1) * P], gath[:, t, :],
                                                      start=True, stop=True)
                        mm.then_inc(q["sel_mm"], 1)
                        pe.wait_ge(q["v_taken"], g * T + 4)
                        pe.wait_ge(q["sel_taken"], g + 1)
                        for m in range(C):
                            for c in range(C):
                                mm = nc.tensor.matmul(bank[4][:, m * GB * K:(m + 1) * GB * K], WQ[:, c, m * P:(m + 1) * P],
                                                      sel_sb[:, c, :, 0:2 * K], start=(c == 0), stop=(c == C - 1))
                        mm.then_inc(q["q_mm"], 1)
                        pe.wait_ge(q["q_taken"], g + 1)
                        for b in range(GB):
                            for c in range(C):
                                mm = nc.tensor.matmul(bank[5][0:H * K, b * L:(b + 1) * L], q_blk[:, c, b, :, :].rearrange("p h k -> p (h k)"),
                                                      kT[:, c, b * L:(b + 1) * L], start=(c == 0), stop=(c == C - 1))
                        mm.then_inc(q["lg_mm"], 1)
                        pe.wait_ge(q["prob_ready"], g + 1)
                        for t in range(T):
                            mm = nc.tensor.transpose(bank[6][:, t * H * K:(t + 1) * H * K],
                                                     prob[:, 2 * t:2 * t + 2, :].rearrange("p b m -> p (b m)"), ident[0:H * K, 0:H * K])
                        mm.then_inc(q["pt_mm"], 1)
                        pe.wait_ge(q["pt_taken"], g * 2 + 2)
                        for n2 in range(2):
                            for c in range(C):
                                for t in range(2):
                                    at = (c * 2 + t) * 2 * HC * K
                                    mm = nc.tensor.matmul(bank[(7, 4)[n2]][:, at:at + 2 * HC * K], v_sb[:, 2 * n2 + t, c * P:(c + 1) * P],
                                                          p_blk[:, c, 2 * n2 + t, :, :].rearrange("p b k -> p (b k)"), start=True, stop=True)
                            mm.then_inc(q["pv_mm"], 1)
                        for t in range(T):
                            mm = nc.tensor.transpose(bank[6][0:RR, t * P:(t + 1) * P], scat[:, t, :], ident)
                        mm.then_inc(q["st_mm"], 1)
                        pe.wait_ge(q["pool_lo"], g + 1)
                        for c in range(C):
                            for i, (a, b) in enumerate(ONES):
                                nc.tensor.matmul(bank[5][0:RR, 0:D], POOL[a][:, c, :], WMR[b][:, c, 0:D],
                                                 start=(c == 0 and i == 0), stop=False, skip_group_check=True)
                        pe.wait_ge(q["pv_taken"], g * 2 + 2)
                        for c in range(C):
                            mm = nc.tensor.matmul(bank[5][0:GB * K, 0:D], ctxT[:, c, :], WO[:, c, :], start=False,
                                                  stop=(c == C - 1), skip_group_check=True)
                        mm.then_inc(q["r_mm"], 1)
                        pe.wait_ge(q["r_taken"], g + 1)
                        pe.wait_ge(q["st_taken"], g + 1)
                        for t in range(T):
                            nc.tensor.matmul(bank[(7, 4, 5, 6)[t]][:, 0:D], scatT[:, t, :], r_sb[:, :], start=True, stop=True)\
                                .then_inc(q["out_mm"], 1)
        phase1.close()

        W1S = [sb(f"w1s{i}", [P, C, F], F32R) for i in range(2)]
        W2S = [sb(f"w2s{i}", [P, FC, D], F32R) for i in range(2)]
        hb = sb("hb", [P, FC])
        bf2_bc = sb("bf2_bc", [P, D])
        with ExitStack() as stage:
            s = lambda name, shape, dt=F32: sb(name, shape, dt, stage)
            w1_raw, w2_raw = s("w1_raw", [P, C, F]), s("w2_raw", [P, FC, D])
            g2c, b2c, bf1c = s("g2c", [P, C]), s("b2c", [P, C]), s("bf1c", [P, FC])
            bf2r, one_row = s("bf2r", [1, D]), s("one_row", [1, P])
            loaded, mults, scaled, hi_made, ones_set = (sem(n, stage) for n in
                                                       ("mlp_loaded", "mlp_bias", "mlp_scaled", "mlp_high", "mlp_ones"))
            with nc.Block() as block:
                @block.sync
                def _(sp):
                    for dst, src in ((w1_raw[:, :, :], chunks(W1)), (w2_raw[:, :, :], W2.rearrange("(c p) n -> p c n", p=P)),
                                     (g2c[:, :], column(g2)), (b2c[:, :], column(b2)), (bf1c[:, :], column(bf1)), (bf2r[:, :], row(bf2))):
                        sp.dma_start(dst, src, allow_slow_non_contiguous=True).then_inc(loaded, 16)

                @block.tensor
                def _(pe):
                    pe.wait_ge(loaded, 96)
                    pe.wait_ge(ones_set, 1)
                    for m in range(FC):
                        for c in range(C):
                            nc.tensor.matmul(bank[0][:, m:m + 1], w1_raw[:, c, m * P:(m + 1) * P], b2c[:, c:c + 1],
                                             start=(c == 0), stop=(c == C - 1))
                    nc.tensor.matmul(bank[1][:, 0:D], one_row[:, :], bf2r[:, :], start=True, stop=True).then_inc(mults, 1)

                @block.scalar
                def _(act):
                    act.wait_ge(loaded, 96)
                    for m in range(FC):
                        nc.scalar.copy(W2S[0][:, m, :], w2_raw[:, m, :]).then_inc(hi_made, 1)

                @block.vector
                def _(dve):
                    nc.vector.memset(one_row[:, :], 1.0).then_inc(ones_set, 1)
                    dve.wait_ge(mults, 1)
                    for c in range(C):
                        nc.vector.tensor_scalar(w1_raw[:, c, :], w1_raw[:, c, :], g2c[:, c:c + 1], None, ALU.mult).then_inc(scaled, 1)
                    dve.wait_ge(scaled, C)
                    for c in range(C):
                        nc.vector.tensor_copy(W1S[0][:, c, :], w1_raw[:, c, :]).then_inc(scaled, 1)
                    dve.wait_ge(scaled, 2 * C)
                    nc.vector.tensor_tensor(W1S[1][:, :, :], w1_raw[:, :, :], W1S[0][:, :, :], ALU.subtract)
                    nc.vector.tensor_tensor(hb[:, :], bank[0][:, 0:FC], bf1c[:, :], ALU.add)
                    nc.vector.tensor_copy(bf2_bc[:, :], bank[1][:, 0:D])
                    for m in range(FC):
                        dve.wait_ge(hi_made, m + 1)
                        nc.vector.tensor_tensor(W2S[1][:, m, :], w2_raw[:, m, :], W2S[0][:, m, :], ALU.subtract)

        n2 = sb("n2", [P, T, D])
        xh = sb("xh", [P, T, D])
        o_sb = sb("o_sb", [P, T, D])
        NT2 = [sb(f"n2t{i}", [P, C, GT], F32R) for i in range(2)]
        R3 = 3
        hid_f = sb("hid_f", [P, R3, GT])
        HID = [sb(f"hid{i}", [P, R3, GT], F32R) for i in range(2)]
        with ExitStack() as c2:
            q = {n: sem(n, c2) for n in ("n2_loaded xh_loaded xh_biased n2t_mm n2t_hi n2t_lo h_mm gelu_done h_hi h_lo out_mm out_taken "
                                         "stored").split()}
            with nc.Block() as block:
                @block.sync
                def _(sp):
                    with sp.Fori(0, G) as g:
                        sp.wait_ge(q["n2t_mm"], g * C)
                        sp.dma_start(n2[:, :, :], n2_g[g]).then_inc(q["n2_loaded"], 16)
                        sp.wait_ge(q["out_taken"], g * T)
                        sp.dma_start(xh[:, :, :], xh_g[g]).then_inc(q["xh_loaded"], 16)

                @block.gpsimd
                def _(pool):
                    with pool.Fori(0, G) as g:
                        pool.wait_ge(q["xh_loaded"], g * 16 + 16)
                        nc.gpsimd.tensor_tensor(xh[:, :, :], xh[:, :, :], bf2_bc[:, :].unsqueeze(1).to_broadcast([P, T, D]),
                                                ALU.add).then_inc(q["xh_biased"], 1)
                        pool.wait_ge(q["out_taken"], g * T + T)
                        pool.dma_start(out_g[g], o_sb[:, :, :]).then_inc(q["stored"], 16)
                    pool.wait_ge(q["stored"], 16 * G)

                @block.scalar
                def _(act):
                    with act.Fori(0, G) as g:
                        for c in range(C):
                            act.wait_ge(q["n2t_mm"], g * C + c + 1)
                            nc.scalar.copy(NT2[0][:, c, :], bank[6][:, :]).then_inc(q["n2t_hi"], 1)
                        for m in range(FC):
                            act.wait_ge(q["h_mm"], g * FC + m + 1)
                            if m >= R3:
                                act.wait_ge(q["h_lo"], g * FC + m - R3 + 1)
                            nc.scalar.activation(hid_f[:, m % R3, :], bank[4 + m % 2][:, :], ACT.Gelu,
                                                 bias=hb[:, m:m + 1]).then_inc(q["gelu_done"], 1)

                @block.vector
                def _(dve):
                    with dve.Fori(0, G) as g:
                        for c in range(C):
                            dve.wait_ge(q["n2t_hi"], g * C + c + 1)
                            nc.vector.tensor_tensor(NT2[1][:, c, :], bank[6][:, :], NT2[0][:, c, :], ALU.subtract)\
                                .then_inc(q["n2t_lo"], 1)
                        for m in range(FC):
                            dve.wait_ge(q["gelu_done"], g * FC + m + 1)
                            if m >= R3:
                                dve.wait_ge(q["out_mm"], g * FC + m - R3 + 1)
                            nc.vector.tensor_copy(HID[0][:, m % R3, :], hid_f[:, m % R3, :]).then_inc(q["h_hi"], 1)
                            dve.wait_ge(q["h_hi"], g * FC + m + 1)
                            nc.vector.tensor_tensor(HID[1][:, m % R3, :], hid_f[:, m % R3, :], HID[0][:, m % R3, :], ALU.subtract)\
                                .then_inc(q["h_lo"], 1)
                        dve.wait_ge(q["xh_biased"], g + 1)
                        dve.wait_ge(q["stored"], g * 16)
                        dve.wait_ge(q["out_mm"], g * FC + FC)
                        for t in range(T):
                            nc.vector.tensor_tensor(o_sb[:, t, :], bank[t][:, 0:D], xh[:, t, :], ALU.add)\
                                .then_inc(q["out_taken"], 1)

                @block.tensor
                def _(pe):
                    with pe.Fori(0, G) as g:
                        pe.wait_ge(q["n2_loaded"], g * 16 + 16)
                        for c in range(C):
                            pe.wait_ge(q["n2t_lo"], g * C + c)
                            for t in range(T):
                                mm = nc.tensor.transpose(bank[6][:, t * P:(t + 1) * P], n2[:, t, c * P:(c + 1) * P], ident)
                            mm.then_inc(q["n2t_mm"], 1)
                        pe.wait_ge(q["n2t_lo"], g * C + C)
                        for m in range(FC + 1):
                            if m < FC:
                                if m >= 2:
                                    pe.wait_ge(q["gelu_done"], g * FC + m - 1)
                                for c in range(C):
                                    for i, (a, b) in enumerate(ONES):
                                        mm = nc.tensor.matmul(bank[4 + m % 2][:, :], W1S[a][:, c, m * P:(m + 1) * P], NT2[b][:, c, :],
                                                              start=(c == 0 and i == 0), stop=(c == C - 1 and i == 2))
                                mm.then_inc(q["h_mm"], 1)
                            if m >= 1:
                                k = m - 1
                                pe.wait_ge(q["h_lo"], g * FC + k + 1)
                                if k == 0:
                                    pe.wait_ge(q["out_taken"], g * T)
                                for t in range(T):
                                    ts = slice(t * P, (t + 1) * P)
                                    for i, (a, b) in enumerate(ONES):
                                        mm = nc.tensor.matmul(bank[t][:, 0:D], HID[a][:, k % R3, ts], W2S[b][:, k, :],
                                                              start=(k == 0 and i == 0), stop=(k == FC - 1 and i == 2))
                                mm.then_inc(q["out_mm"], 1)


_INS = ['x', 'adj', 'L0_gnn_W1', 'L0_gnn_b1', 'L0_gnn_W2', 'L0_gnn_b2', 'L0_gnn_W3', 'L0_gnn_b3', 'L0_gnn_W4', 'L0_gnn_b4',
        'L0_ffn_g1', 'L0_ffn_b1', 'L0_ffn_g2', 'L0_ffn_b2', 'L0_ffn_Wr', 'L0_ffn_br', 'L0_ffn_Wq', 'L0_ffn_bq', 'L0_ffn_Wk',
        'L0_ffn_bk', 'L0_ffn_Wv', 'L0_ffn_bv', 'L0_ffn_Wo', 'L0_ffn_bo', 'L0_ffn_Wm', 'L0_ffn_bm', 'L0_ffn_W1', 'L0_ffn_bf1',
        'L0_ffn_W2', 'L0_ffn_bf2']


def kernel(**inputs):
    import numpy as _np
    import concourse.bacc as _bacc
    from concourse import mybir as _mybir
    from concourse.bass_utils import run_bass_kernel_spmd as _run

    nc = _bacc.Bacc("TRN2", target_bir_lowering=False, num_devices=1)
    arrays, args = {}, []
    for name in _INS:
        a = _np.ascontiguousarray(inputs[name])
        if a.ndim == 0 or name.endswith("_br"):
            a = a.reshape(1, 1)
        arrays[f"in_{name}"] = a
    arrays["in_consts"] = constants()
    for name, a in arrays.items():
        args.append(nc.dram_tensor(name, a.shape, _mybir.dt.from_np(a.dtype), kind="ExternalInput").ap())
    args.append(nc.dram_tensor("out_0", (B, L, D), _mybir.dt.float32, kind="ExternalOutput").ap())
    program(nc, *args)
    r = _run(nc, [arrays], core_ids=[0])
    return r.results[0]["out_0"]
```

```python
from contextlib import ExitStack

import numpy as np
import concourse.bass as bass
from concourse import mybir

F32 = mybir.dt.float32
F32R = mybir.dt.float32r
I32 = mybir.dt.int32
ALU = mybir.AluOpType
ACT = mybir.ActivationFunctionType
AX = mybir.AxisListType

P = 128
B, L, D = 128, 64, 384
C = D // P
H, DH, F = 12, 32, 1536
HC = P // DH
FC = F // P
T = 4
GT = T * P
GB = GT // L
G = B * L // GT
K = max(1, int(round(0.15 * L)))
EPS = 1e-5
NEG = -1e9
WM = D + 2
SELW = 2 * K + 2
RR = 96
ROW_POOL, ROW_BIAS, ROW_B1 = GB * K, GB * K + GB, GB * K + GB + 1
PRODUCTS = [(a, b) for a, b in ((0, 0), (1, 0), (0, 1))]


def constants():
    p = np.arange(P)
    m = np.arange(L)
    ident = np.eye(P)
    same = (p[:, None] // L == p[None, :] // L) * 1.0
    node = (p[:, None] % L == m[None, :]) * 1.0
    earlier = (m[None, :] < p[:, None] % L) * 1.0
    iota = np.broadcast_to(np.arange(K), (P, K))
    picked = np.broadcast_to(np.arange(RR) < GB * K, (P, RR))
    bias = np.broadcast_to(np.arange(RR) == ROW_BIAS, (P, RR))
    return np.concatenate([ident, same, node, earlier, iota, picked, bias], axis=1).astype(np.float32)


CONST_W = 2 * P + 2 * L + K


def program(nc, x, adj, gW1, gb1, gW2, gb2, gW3, gb3, gW4, gb4, g1, b1, g2, b2, Wr, br, Wq, bq, Wk, bk,
            Wv, bv, Wo, bo, Wm, bm, W1, bf1, W2, bf2, consts, out):
    x1_d = nc.dram_tensor("x1_scratch", (B * L, D), F32).ap()
    h_d = nc.dram_tensor("h_scratch", (B * L, D), F32).ap()
    tiles = lambda a: a.rearrange("(g t p) d -> g p t d", t=T, p=P)
    x_g = tiles(x.rearrange("b n d -> (b n) d"))
    adj_g = tiles(adj.rearrange("b n d -> (b n) d"))
    out_g = tiles(out.rearrange("b n d -> (b n) d"))
    x1_g, h_g = tiles(x1_d), tiles(h_d)
    chunks = lambda w: w.rearrange("(c p) n -> p c n", p=P)
    column = lambda v: v.rearrange("(c p) -> p c", p=P)
    row = lambda v: v.rearrange("(a n) -> a n", a=1)

    with ExitStack() as ctx:
        def sb(name, shape, dt=F32, where=ctx):
            return where.enter_context(nc.sbuf_tensor(name, shape, dt))

        def sem(name, where=ctx):
            return where.enter_context(nc.semaphore(name))

        bank = [ctx.enter_context(nc.psum_tensor(f"bank{i}", [P, 512], F32)) for i in range(8)]

        cst = sb("cst", [P, CONST_W])
        ident = cst[:, 0:P]
        same = cst[:, P:2 * P]
        node = cst[:, 2 * P:2 * P + L]
        earlier = cst[:, 2 * P + L:2 * P + 2 * L]
        o = 2 * P + 2 * L
        iota = cst[:, o:o + K]
        phase1 = ctx.enter_context(ExitStack())
        p1 = lambda name, shape, dt=F32: sb(name, shape, dt, phase1)
        WA = [p1(f"wa{i}", [P, C, D], F32R) for i in range(2)]
        W3T = [p1(f"w3t{i}", [P, C, D], F32R) for i in range(2)]
        W4T = [p1(f"w4t{i}", [P, C, D], F32R) for i in range(2)]
        WMR = [p1(f"wmr{i}", [P, C, WM], F32R) for i in range(2)]
        WK = [p1(f"wk{i}", [P, C, D], F32R) for i in range(2)]
        WV = [p1(f"wv{i}", [P, C, D], F32R) for i in range(2)]
        WQ = p1("wq", [P, C, D])
        WO = p1("wo", [P, C, D])
        cT = p1("cT", [P, C])
        u_bc = p1("u_bc", [P, D])
        beta = p1("beta", [P, 1])
        g_bias = p1("g_bias", [P, D])
        bqT, bkT, bvT = (p1(n, [P, C]) for n in ("bqT", "bkT", "bvT"))
        brn = p1("brn", [P, 1])
        r_bias = p1("r_bias", [RR, D])
        mhalf = p1("mhalf", [P, T])
        eps = p1("eps", [P, T])

        with ExitStack() as stage:
            s = lambda name, shape, dt=F32: sb(name, shape, dt, stage)
            raw = {n: s(f"raw_{n}", [P, C, D]) for n in ("w1", "w2", "w3", "w4", "wk", "wv", "wm")}
            raw["wr"] = s("raw_wr", [P, C])
            col = {n: s(f"col_{n}", [P, C]) for n in ("gb1", "gb2", "gb3", "g1", "b1", "bq", "bk", "bv")}
            rows = s("rows", [1, 6, D])
            fold = {n: s(f"fold_{n}", [P, C, WM]) for n in ("wk", "wv", "wm")}
            w4t = s("w4t", [P, C, D])
            b2_bc, b3_bc, b1_bc = (s(n, [P, C, P]) for n in ("b2_bc", "b3_bc", "b1_bc"))
            place = s("place", [P, C, RR])
            bv_rows = s("bv_rows", [P, C, RR])
            ones = s("ones", [P, P])
            rowsel = s("rowsel", [P, 2 * RR])
            picked, biasrow = rowsel[:, 0:RR], rowsel[:, RR:2 * RR]
            loaded = sem("setup_loaded", stage)
            ones_set = sem("setup_ones", stage)
            made = sem("setup_made", stage)
            mults = sem("setup_products", stage)
            taken = sem("setup_taken", stage)
            low = sem("setup_low", stage)
            placed = sem("setup_placed", stage)
            n_dma = 0
            with nc.Block() as block:
                loads = [(cst[:, :], consts[:, 0:CONST_W]), (rowsel[:, :], consts[:, CONST_W:CONST_W + 2 * RR])]
                loads += [(raw[n][:, :, :], chunks(w)) for n, w in
                          (("w1", gW1), ("w2", gW2), ("w3", gW3), ("w4", gW4), ("wk", Wk), ("wv", Wv), ("wm", Wm))]
                loads += [(WQ[:, :, :], chunks(Wq)), (WO[:, :, :], chunks(Wo)), (raw["wr"][:, :], column(Wr))]
                loads += [(col[n][:, :], column(v)) for n, v in
                          (("gb1", gb1), ("gb2", gb2), ("gb3", gb3), ("g1", g1), ("b1", b1), ("bq", bq), ("bk", bk), ("bv", bv))]
                loads += [(rows[0:1, i, :], row(v)) for i, v in enumerate((gb3, gb4, bo, bm))]
                loads += [(rows[0:1, 4, 0:1], br)]
                n_loads = len(loads)

                @block.sync
                def _(sp):
                    for dst, src in loads:
                        sp.dma_start(dst, src, allow_slow_non_contiguous=True).then_inc(loaded, 16)

                @block.vector
                def _(dve):
                    nc.vector.memset(mhalf[:, :], -0.5)
                    nc.vector.memset(eps[:, :], EPS)
                    for n in ("wk", "wv", "wm"):
                        nc.vector.memset(fold[n][:, :, D:WM], 0.0)
                    nc.vector.memset(ones[:, :], 1.0).then_inc(ones_set, 1)
                    nc.vector.memset(place[:, :, :], 0.0).then_inc(ones_set, 1)
                    dve.wait_ge(loaded, 16 * n_loads)
                    dve.wait_ge(ones_set, 2)
                    for c in range(C):
                        for bc, v in ((b2_bc, "gb2"), (b3_bc, "gb3"), (b1_bc, "b1")):
                            nc.vector.tensor_scalar(bc[:, c, :], ones[:, :], col[v][:, c:c + 1], None, ALU.mult)
                        nc.vector.tensor_scalar(place[:, c, ROW_BIAS:ROW_B1 + 1], ones[:, 0:2],
                                                col["b1"][:, c:c + 1], None, ALU.mult)
                        nc.vector.tensor_scalar(fold["wk"][:, c, 0:D], raw["wk"][:, c, :], col["g1"][:, c:c + 1], None, ALU.mult)
                        nc.vector.tensor_scalar(fold["wv"][:, c, 0:D], raw["wv"][:, c, :], col["g1"][:, c:c + 1], None, ALU.mult)
                        nc.vector.tensor_scalar(fold["wm"][:, c, 0:D], raw["wm"][:, c, :], col["g1"][:, c:c + 1], None, ALU.mult)
                        nc.vector.tensor_tensor(fold["wm"][:, c, D:D + 1], raw["wr"][:, c:c + 1], col["g1"][:, c:c + 1],
                                                ALU.mult).then_inc(made, 1)
                    dve.wait_ge(mults, 3)
                    for c in range(C):
                        nc.vector.tensor_scalar(WQ[:, c, :], WQ[:, c, :], col["g1"][:, c:c + 1], float(DH) ** -0.5,
                                                ALU.mult, ALU.mult)
                    dve.wait_ge(made, C)
                    for wide, (hi, lo) in (("wk", WK), ("wv", WV), ("wm", WMR)):
                        w = hi.shape[2]
                        nc.vector.tensor_copy(hi[:, :, :], fold[wide][:, :, 0:w]).then_inc(low, 1)
                    dve.wait_ge(low, 3)
                    for wide, (hi, lo) in (("wk", WK), ("wv", WV), ("wm", WMR)):
                        w = hi.shape[2]
                        nc.vector.tensor_tensor(lo[:, :, :], fold[wide][:, :, 0:w], hi[:, :, :], ALU.subtract)
                    v = bank[7]
                    nc.vector.tensor_copy(cT[:, :], v[:, 0:C])
                    nc.vector.tensor_copy(beta[:, :], v[:, 4:5])
                    nc.vector.tensor_tensor(bkT[:, :], v[:, 8:8 + C], col["bk"][:, :], ALU.add)
                    nc.vector.tensor_tensor(bvT[:, :], v[:, 12:12 + C], col["bv"][:, :], ALU.add)
                    nc.vector.tensor_tensor(bqT[:, :], v[:, 16:16 + C], col["bq"][:, :], ALU.add).then_inc(low, 1)
                    nc.vector.tensor_scalar(brn[:, :], v[:, 20:21], -1.0, None, ALU.mult)
                    dve.wait_ge(low, 4)
                    nc.vector.tensor_scalar(bqT[:, :], bqT[:, :], float(DH) ** -0.5, None, ALU.mult)
                    nc.vector.tensor_copy(u_bc[:, :], bank[6][:, 0:D])
                    for c in range(C):
                        ins = nc.vector.tensor_scalar(bv_rows[:, c, :], picked, bvT[:, c:c + 1], None, ALU.mult)
                    ins.then_inc(placed, 1)
                    for n, (hi, lo) in enumerate((WA, W3T, W4T)):
                        dve.wait_ge(mults, 4 + n)
                        for c in range(C):
                            nc.vector.tensor_copy(hi[:, c, :], bank[c][:, 0:D]).then_inc(low, 1)
                            if n == 2:
                                nc.vector.tensor_copy(w4t[:, c, :], bank[c][:, 0:D])
                            dve.wait_ge(low, 5 + 3 * n + c)
                            nc.vector.tensor_tensor(lo[:, c, :], bank[c][:, 0:D], hi[:, c, :], ALU.subtract).then_inc(taken, 1)
                    dve.wait_ge(mults, 8)
                    nc.vector.tensor_copy(g_bias[:, :], bank[4][:, 0:D])
                    nc.vector.tensor_copy(r_bias[:, :], bank[5][0:RR, 0:D])

                @block.tensor
                def _(pe):
                    pe.wait_ge(loaded, 16 * n_loads)
                    pe.wait_ge(made, C)
                    v = bank[7]

                    def by_feature(at, lhsT, rhs):
                        for m in range(C):
                            for c in range(C):
                                mm = nc.tensor.matmul(v[:, at + m:at + m + 1], lhsT[:, c, m * P:(m + 1) * P], rhs[:, c:c + 1],
                                                      start=(c == 0), stop=(c == C - 1))
                        return mm

                    by_feature(0, raw["w2"], col["gb1"])
                    for c in range(C):
                        nc.tensor.matmul(v[:, 4:5], b2_bc[:, c, :], col["gb1"][:, c:c + 1], start=(c == 0), stop=(c == C - 1))
                    for c in range(C):
                        nc.tensor.matmul(v[:, 20:21], b1_bc[:, c, :], raw["wr"][:, c:c + 1], start=(c == 0), stop=False)
                    nc.tensor.matmul(v[:, 20:21], ones[0:1, :], rows[0:1, 4, 0:1], start=False, stop=True).then_inc(mults, 1)
                    by_feature(8, raw["wk"], col["b1"])
                    by_feature(12, raw["wv"], col["b1"])
                    by_feature(16, WQ, col["b1"]).then_inc(mults, 1)
                    for c in range(C):
                        mm = nc.tensor.matmul(bank[6][:, 0:D], b2_bc[:, c, :], raw["w1"][:, c, :], start=(c == 0), stop=(c == C - 1))
                    mm.then_inc(mults, 1)
                    for m in range(C):
                        for c in range(C):
                            mm = nc.tensor.matmul(bank[m][:, 0:D], raw["w1"][:, c, m * P:(m + 1) * P], raw["w2"][:, c, :],
                                                  start=(c == 0), stop=(c == C - 1))
                    mm.then_inc(mults, 1)
                    for n, w in enumerate(("w3", "w4")):
                        pe.wait_ge(taken, C * (n + 1))
                        for m in range(C):
                            for c in range(C):
                                mm = nc.tensor.transpose(bank[m][:, c * P:(c + 1) * P], raw[w][:, c, m * P:(m + 1) * P], ident)
                        mm.then_inc(mults, 1)
                    pe.wait_ge(taken, 3 * C)
                    for c in range(C):
                        nc.tensor.matmul(bank[4][:, 0:D], b3_bc[:, c, :], w4t[:, c, :], start=(c == 0), stop=False)
                    nc.tensor.matmul(bank[4][:, 0:D], ones[0:1, :], rows[0:1, 0, :], start=False, stop=False)
                    nc.tensor.matmul(bank[4][:, 0:D], ones[0:1, :], rows[0:1, 1, :], start=False, stop=True).then_inc(mults, 1)
                    for c in range(C):
                        nc.tensor.matmul(bank[5][0:RR, 0:D], place[:, c, :], raw["wm"][:, c, :], start=(c == 0), stop=False)
                    pe.wait_ge(placed, 1)
                    for c in range(C):
                        nc.tensor.matmul(bank[5][0:RR, 0:D], bv_rows[:, c, :], WO[:, c, :], start=False, stop=False)
                    nc.tensor.matmul(bank[5][0:RR, 0:D], picked[0:1, :], rows[0:1, 2, :], start=False, stop=False)
                    nc.tensor.matmul(bank[5][0:RR, 0:D], biasrow[0:1, :], rows[0:1, 3, :], start=False, stop=True).then_inc(mults, 1)

        x_in = p1("x_in", [P, T, D])
        xn = p1("xn", [P, T, D])
        adj_in = p1("adj_in", [P, T, L], I32)
        XT = [p1(f"xt{i}", [P, C, GT], F32R) for i in range(2)]
        TT = [p1(f"tt{i}", [P, C, GT], F32R) for i in range(2)]
        keep = p1("keep", [P, 2, T, L])
        neg = p1("neg", [P, 2, T, L])
        lg = p1("lg", [P, 2, T, L])
        prior = p1("prior", [P, T, L])
        Fb, Nb = (p1(n, [P, T, P]) for n in ("Fb", "Nb"))
        FT, NT = (p1(n, [P, T, P]) for n in ("FT", "NT"))
        g_sb = p1("g_sb", [P, T, D])
        xg = p1("xg", [P, T, D])
        x1 = p1("x1", [P, T, D])
        hid = p1("hid", [P, T, D])
        nh = p1("nh", [P, T, D])
        NHT = [p1(f"nht{i}", [P, C, GT], F32R) for i in range(2)]
        y_sb = p1("y_sb", [P, T, WM])
        kT = p1("kT", [P, C * GT])
        v_sb = p1("v_sb", [P, T, D])
        q_blk = p1("q_blk", [P, C, GB, H, K])
        p_blk = p1("p_blk", [P, C, T, 2, HC * K])
        prob = kT[0:H * K, 0:GB * L].rearrange("p (b m) -> p b m", b=GB)
        scatT = kT[0:RR, GT:2 * GT].rearrange("p (t n) -> p t n", t=T)
        r_sb = kT[0:RR, 2 * GT:2 * GT + D]
        ctxT = p1("ctxT", [P, C, GB * K])
        pool_f = p1("pool_f", [P, C, GB])
        POOL = [p1(f"pool{i}", [P, C, RR], F32R) for i in range(2)]
        sel_sb = p1("sel_sb", [P, C, T, SELW])
        gath = p1("gath", [P, T, SELW])
        scat = p1("scat", [P, T, RR])
        bc = p1("bc", [P, T, L])
        cmp = p1("cmp", [P, 2, T, L])
        diag = cmp[:, 1, :, :]
        att_sb = p1("att_sb", [P, D])
        junk = att_sb[:, 0:D]
        att_v = att_sb[:, 0:T * L].rearrange("p (t m) -> p t m", t=T)
        stats = p1("stats", [P, T, 6])
        mv = p1("mv", [P, T, 2])
        mvh = p1("mvh", [P, T, 2])
        small = p1("small", [P, 26, T])
        small8 = p1("small8", [P, 3, 8])
        order = p1("order", [P, 1])

        with ExitStack() as c1:
            q = {n: sem(n, c1) for n in (
                "x_loaded adj_loaded x1_stored h_stored zeroed zeroed_pool "
                "var_ready rstd_ready xn_ready xg_ready adj_read rn_ready xt_mm xt_hi xt_lo t_mm t_hi t_lo att_mm "
                "logits_ready exp_done product_ready exp2_done blocks_ready fn_mm fn_taken y_mm y_hi y_lo g_mm g_taken g_added "
                "ng_mm ng_hi ng_lo x1_mm x1_taken "
                "var1_ready rstd1_ready hid_ready nh_ready nht_mm nht_hi nht_lo wm_mm wm_taken k_mm k_taken z_exp score_diag bc_mm "
                "bc_taken v_mm v_taken picks_ready y_ready sel_mm sel_taken pool_hi pool_lo q_mm q_taken lg_mm lg_taken lgexp "
                "prob_ready pt_mm pt_taken pv_mm pv_taken r_mm r_taken st_mm st_taken out_mm h_ready "
                "norm_step gnn_step attn_step pool_step").split()}

            def sm(i, w=T):
                return small[:, i, 0:w]

            NORM_STEPS, GNN_STEPS, ATTN_STEPS, POOL_STEPS = 7, 18, 15, 4

            def parts(i):
                return (slice(0, L), slice(L, P))[i]

            def over_groups(eng, both):
                both(0, None, 1)
                both(1, 0, 2)
                with eng.Fori(1, G - 2) as i:
                    both(i + 1, i, i + 2)
                both(G - 1, G - 2, None)
                both(None, G - 1, None)

            with nc.Block() as block:
                @block.sync
                def _(sp):
                    def load(g):
                        sp.wait_ge(q["xn_ready"], g * T)
                        sp.wait_ge(q["xg_ready"], g)
                        sp.dma_start(x_in[:, :, :], x_g[g]).then_inc(q["x_loaded"], 16)
                        sp.wait_ge(q["adj_read"], g)
                        sp.dma_start(adj_in[:, :, :], adj_g[g]).then_inc(q["adj_loaded"], 16)

                    def both(a, b, nxt):
                        if nxt is not None:
                            load(nxt)
                        if b is not None:
                            sp.wait_ge(q["h_ready"], b * T + T)
                            sp.dma_start(h_g[b], y_sb[:, :, 0:D]).then_inc(q["h_stored"], 16)
                        if a is not None:
                            sp.wait_ge(q["x1_taken"], a * T + T)
                            sp.dma_start(x1_g[a], x1[:, :, :]).then_inc(q["x1_stored"], 16)

                    sp.dma_start(x_in[:, :, :], x_g[0]).then_inc(q["x_loaded"], 16)
                    sp.dma_start(adj_in[:, :, :], adj_g[0]).then_inc(q["adj_loaded"], 16)
                    over_groups(sp, both)
                    sp.wait_ge(q["x1_stored"], 16 * G)
                    sp.wait_ge(q["h_stored"], 16 * G)

                @block.gpsimd
                def _(pool):
                    nc.gpsimd.memset(Fb[:, :, :], 0.0)
                    nc.gpsimd.memset(Nb[:, :, :], 0.0)
                    nc.gpsimd.memset(scat[:, :, :], 0.0)
                    nc.gpsimd.memset(gath[:, :, :], 0.0)
                    nc.gpsimd.memset(q_blk[:, :, :, :, :], 0.0)
                    nc.gpsimd.memset(p_blk[:, :, :, :, :], 0.0).then_inc(q["zeroed_pool"], 1)

                    def rstd(g):
                        pool.wait_ge(q["var_ready"], g + 1)
                        nc.gpsimd.tensor_tensor(sm(1), sm(0), mhalf[:, :], ALU.pow).then_inc(q["rstd_ready"], 1)

                    def both(a, b, nxt):
                        if b is not None:
                            n = [0]

                            def step(ins):
                                n[0] += 1
                                ins.then_inc(q["pool_step"], 1)
                                pool.wait_ge(q["pool_step"], b * POOL_STEPS + n[0])

                            pool.wait_ge(q["var1_ready"], b + 1)
                            step(nc.gpsimd.tensor_tensor(sm(3), sm(2), mhalf[:, :], ALU.pow))
                            step(nc.gpsimd.tensor_tensor(sm(4), mvh[:, :, 1], sm(3), ALU.mult))
                            step(nc.gpsimd.tensor_tensor(sm(4), sm(4), sm(3), ALU.mult))
                            step(nc.gpsimd.tensor_tensor(sm(4), sm(4), eps[:, :], ALU.add))
                            nc.gpsimd.tensor_tensor(sm(5), sm(4), mhalf[:, :], ALU.pow).then_inc(q["rstd1_ready"], 1)
                            assert n[0] == POOL_STEPS, n
                        if a is not None:
                            pool.wait_ge(q["x_loaded"], a * 16 + 16)
                            pool.wait_ge(q["x1_taken"], a * T)
                            nc.gpsimd.tensor_tensor(xg[:, :, :], x_in[:, :, :], g_bias[:, :].unsqueeze(1).to_broadcast([P, T, D]),
                                                    ALU.add).then_inc(q["xg_ready"], 1)
                            pool.wait_ge(q["xg_ready"], a + 1)
                            for t in range(T):
                                pool.wait_ge(q["g_taken"], a * T + t + 1)
                                nc.gpsimd.tensor_tensor(xg[:, t, :], xg[:, t, :], g_sb[:, t, :], ALU.add).then_inc(q["g_added"], 1)
                        if nxt is not None:
                            rstd(nxt)

                    rstd(0)
                    over_groups(pool, both)

                @block.scalar
                def _(act):
                    def xt_hi(g):
                        for c in range(C):
                            act.wait_ge(q["xt_mm"], g * 3 + c + 1)
                            nc.scalar.copy(XT[0][:, c, :], bank[c][:, :]).then_inc(q["xt_hi"], 1)

                    def t_hi(g):
                        for c in range(C):
                            act.wait_ge(q["t_mm"], g * 3 + c + 1)
                            nc.scalar.activation(TT[0][:, c, :], bank[(3, 0, 1)[c]][:, :], ACT.Identity,
                                                 bias=cT[:, c:c + 1]).then_inc(q["t_hi"], 1)

                    def exp_prior(g):
                        act.wait_ge(q["logits_ready"], g * 2 + 1)
                        nc.scalar.activation(prior[:, :, :], prior[:, :, :], ACT.Exp).then_inc(q["exp_done"], 1)

                    def exp_att(g):
                        act.wait_ge(q["logits_ready"], g * 2 + 2)
                        nc.scalar.activation(lg[:, :, :, :], lg[:, :, :, :], ACT.Exp).then_inc(q["exp_done"], 1)

                    def exp_product(g):
                        act.wait_ge(q["product_ready"], g + 1)
                        nc.scalar.activation(prior[:, :, :], prior[:, :, :], ACT.Exp).then_inc(q["exp2_done"], 1)

                    def fn_take(g):
                        for n, (dst, b) in enumerate(((FT, 3), (NT, 0))):
                            act.wait_ge(q["fn_mm"], g * 2 + n + 1)
                            nc.scalar.copy(dst[:, :, :], bank[b][:, :]).then_inc(q["fn_taken"], 1)

                    def y_hi(g):
                        for c in range(C):
                            act.wait_ge(q["y_mm"], g * 3 + c + 1)
                            nc.scalar.copy(XT[0][:, c, :], bank[1 + c][:, :]).then_inc(q["y_hi"], 1)

                    def g_take(g, ts):
                        for t in ts:
                            act.wait_ge(q["g_mm"], g * T + t + 1)
                            nc.scalar.copy(g_sb[:, t, :], bank[t][:, 0:D]).then_inc(q["g_taken"], 1)

                    def ng_hi(g, cs):
                        for c in cs:
                            act.wait_ge(q["ng_mm"], g * 3 + c + 1)
                            nc.scalar.copy(TT[0][:, c, :], bank[c][:, :]).then_inc(q["ng_hi"], 1)

                    def nht_hi(g):
                        for c in range(C):
                            act.wait_ge(q["nht_mm"], g * 3 + c + 1)
                            nc.scalar.copy(NHT[0][:, c, :], bank[4 + c][:, :]).then_inc(q["nht_hi"], 1)

                    def wm_take(g, ts):
                        act.wait_ge(q["h_stored"], g * 16)
                        for t in ts:
                            act.wait_ge(q["wm_mm"], g * T + t + 1)
                            nc.scalar.copy(y_sb[:, t, :], bank[(7, 4, 5, 6)[t]][:, 0:WM]).then_inc(q["wm_taken"], 1)

                    def z_exp(g):
                        act.wait_ge(q["wm_taken"], g * T + T)
                        nc.scalar.activation(sm(8), y_sb[:, :, D], ACT.Exp, bias=brn[:, :], scale=-1.0).then_inc(q["z_exp"], 1)

                    def k_take(g, cs):
                        for c in cs:
                            act.wait_ge(q["k_mm"], g * 3 + c + 1)
                            nc.scalar.activation(kT[:, c * GT:(c + 1) * GT], bank[(7, 4, 5)[c]][:, :], ACT.Identity,
                                                 bias=bkT[:, c:c + 1]).then_inc(q["k_taken"], 1)

                    def v_take(g):
                        for t in range(T):
                            act.wait_ge(q["v_mm"], g * T + t + 1)
                            nc.scalar.copy(v_sb[:, t, :], bank[(7, 4, 5, 6)[t]][:, 0:D]).then_inc(q["v_taken"], 1)

                    def sel_take(g):
                        act.wait_ge(q["sel_mm"], g + 1)
                        nc.scalar.copy(sel_sb[:, :, :, :], bank[7][:, 0:C * T * SELW].rearrange("p (c t k) -> p c t k", c=C, t=T))\
                            .then_inc(q["sel_taken"], 1)

                    def exp_logits(g):
                        act.wait_ge(q["lg_taken"], g + 1)
                        nc.scalar.activation(prob, prob, ACT.Exp).then_inc(q["lgexp"], 1)

                    def pt_take(g):
                        act.wait_ge(q["pt_mm"], g + 1)
                        pt = bank[6][:, 0:T * H * K].rearrange("p (t c k) -> p c t k", t=T, c=C)
                        for i in range(2):
                            nc.scalar.copy(p_blk[parts(i), :, :, i, :], pt[parts(i), :, :, :]).then_inc(q["pt_taken"], 1)

                    def st_take(g):
                        act.wait_ge(q["st_mm"], g + 1)
                        nc.scalar.copy(scatT, bank[6][0:RR, :].rearrange("p (t n) -> p t n", t=T)).then_inc(q["st_taken"], 1)

                    def pv_take(g):
                        for n in range(2):
                            act.wait_ge(q["pv_mm"], g * 2 + n + 1)
                            pv = bank[(7, 4)[n]][:, 0:C * 4 * HC * K].rearrange("p (c b h k) -> p c b h k", c=C, b=4, h=HC)
                            for h in range(HC):
                                r = slice(h * DH, (h + 1) * DH)
                                dst = ctxT[r, :, n * 4 * K:(n + 1) * 4 * K].rearrange("p c (b k) -> p c b k", b=4)
                                ins = nc.scalar.copy(dst, pv[r, :, :, h, :])
                            ins.then_inc(q["pv_taken"], 1)

                    def both(a, b, nxt):
                        if a is not None:
                            xt_hi(a)
                            t_hi(a)
                        if b is not None:
                            nht_hi(b)
                            wm_take(b, (0,))
                        if a is not None:
                            exp_prior(a)
                        if b is not None:
                            wm_take(b, (1, ))
                        if a is not None:
                            exp_att(a)
                        if b is not None:
                            wm_take(b, (2, 3))
                            z_exp(b)
                            k_take(b, (0, ))
                        if a is not None:
                            exp_product(a)
                        if b is not None:
                            k_take(b, (1, 2))
                        if a is not None:
                            fn_take(a)
                        if b is not None:
                            v_take(b)
                        if a is not None:
                            y_hi(a)
                        if b is not None:
                            sel_take(b)
                        if a is not None:
                            g_take(a, (0, 1))
                        if a is not None:
                            g_take(a, (2, 3))
                        if b is not None:
                            exp_logits(b)
                            pt_take(b)
                            st_take(b)
                        if a is not None:
                            ng_hi(a, (0, 1))
                        if b is not None:
                            pv_take(b)
                        if a is not None:
                            ng_hi(a, (2, ))

                    over_groups(act, both)

                @block.vector
                def _(dve):
                    dve.wait_ge(q["zeroed_pool"], 1)
                    nc.vector.memset(POOL[0][:, :, :].bitcast(F32), 0.0).then_inc(q["zeroed"], 1)
                    nc.vector.memset(POOL[1][:, :, :].bitcast(F32), 0.0).then_inc(q["zeroed"], 1)
                    dve.wait_ge(q["zeroed"], 2)
                    count = {}

                    def stepper(name, g, per, first):
                        if first:
                            count[name] = 0

                        def step(ins):
                            count[name] += 1
                            ins.then_inc(q[name], 1)
                            dve.wait_ge(q[name], g * per + count[name])
                        return step

                    def wide(a):
                        return a.unsqueeze(2).to_broadcast([a.shape[0], T, L])

                    def stat(src, into, step):
                        for t in range(T):
                            ins = nc.vector.bn_stats(stats[:, t, :], src[:, t, 0:D])
                        step(ins)
                        nc.vector.tensor_copy(order[:, :], stats[:, 0, 0:1])
                        for t in range(T):
                            ins = nc.vector.bn_aggr(into[:, t, :], stats[:, t, :])
                        step(ins)

                    def normalise(g):
                        step = stepper("norm_step", g, NORM_STEPS, True)
                        dve.wait_ge(q["x_loaded"], g * 16 + 16)
                        stat(x_in, mv, step)
                        nc.vector.tensor_scalar(sm(0), mv[:, :, 1], EPS, None, ALU.add).then_inc(q["var_ready"], 1)
                        dve.wait_ge(q["rstd_ready"], g + 1)
                        dve.wait_ge(q["y_mm"], g * 3)
                        for t in range(T):
                            nc.vector.tensor_scalar(xn[:, t, :], x_in[:, t, :], mv[:, t, 0:1], small[:, 1, t:t + 1],
                                                    ALU.subtract, ALU.mult).then_inc(q["xn_ready"], 1)
                        dve.wait_ge(q["xn_ready"], g * T + T)
                        for t in range(T):
                            step(nc.vector.tensor_tensor_reduce(out=junk, in0=xn[:, t, :], in1=u_bc[:, :], scale=1.0,
                                                                scalar=0.0, op0=ALU.mult, op1=ALU.add,
                                                                accum_out=small[:, 11, t:t + 1]))
                        step(nc.vector.tensor_scalar(sm(12), sm(11), beta[:, 0:1], None, ALU.add))
                        assert count["norm_step"] == NORM_STEPS, count

                    def masks(g):
                        step = stepper("gnn_step", g, GNN_STEPS, True)
                        dve.wait_ge(q["adj_loaded"], g * 16 + 16)
                        nc.vector.tensor_scalar(keep[:, 0, :, :], adj_in[:, :, :], 0, None, ALU.not_equal)
                        nc.vector.tensor_scalar(keep[:, 1, :, :], adj_in[:, :, :], 1, None, ALU.not_equal)
                        nc.vector.tensor_scalar(neg[:, 0, :, :], adj_in[:, :, :], 0, NEG, ALU.is_equal, ALU.mult)
                        step(nc.vector.tensor_scalar(neg[:, 1, :, :], adj_in[:, :, :], 1, NEG, ALU.is_equal, ALU.mult))
                        nc.vector.scalar_tensor_tensor(out=prior[:, :, :], in0=adj_in[:, :, :], scalar=6.0, in1=neg[:, 0, :, :],
                                                       op0=ALU.mult, op1=ALU.add).then_inc(q["adj_read"], 1)
                        dve.wait_ge(q["adj_read"], g + 1)
                        step(nc.vector.tensor_reduce(sm(10), prior[:, :, :], AX.X, ALU.max))
                        nc.vector.tensor_tensor(prior[:, :, :], prior[:, :, :], wide(sm(10)), ALU.subtract)\
                            .then_inc(q["logits_ready"], 1)

                    def lows(mm_bank, part, hi_sem, lo_sem, g, cs=range(C)):
                        for c in cs:
                            dve.wait_ge(q[hi_sem], g * 3 + c + 1)
                            nc.vector.tensor_tensor(part[1][:, c, :], bank[mm_bank + c][:, :], part[0][:, c, :], ALU.subtract)\
                                .then_inc(q[lo_sem], 1)

                    def t_lo(g):
                        for c in range(C):
                            dve.wait_ge(q["t_hi"], g * 3 + c + 1)
                            nc.vector.scalar_tensor_tensor(out=TT[1][:, c, :], in0=bank[(3, 0, 1)[c]][:, :], scalar=cT[:, c:c + 1],
                                                           in1=TT[0][:, c, :], op0=ALU.add, op1=ALU.subtract)\
                                .then_inc(q["t_lo"], 1)

                    def att_logits(g):
                        step = stepper("gnn_step", g, GNN_STEPS, False)
                        dve.wait_ge(q["att_mm"], g + 1)
                        att = bank[2][:, :].rearrange("p (t m) -> p t m", t=T)
                        for i in range(2):
                            r = parts(i)
                            ins = nc.vector.tensor_tensor(att_v[r, :, :], att[r, :, i * L:(i + 1) * L], wide(sm(12)[r]), ALU.add)
                        step(ins)
                        for i in range(2):
                            ins = nc.vector.scalar_tensor_tensor(out=lg[:, i, :, :], in0=att_v, scalar=1.0 / 28.0,
                                                                 in1=keep[:, i, :, :], op0=ALU.mult, op1=ALU.mult)
                        step(ins)
                        step(nc.vector.tensor_tensor(lg[:, :, :, :], lg[:, :, :, :], neg[:, :, :, :], ALU.add))
                        lgf = lg[:, :, :, :].rearrange("p a t m -> p (a t) m")
                        step(nc.vector.tensor_reduce(small8[:, 0, :], lgf, AX.X, ALU.max))
                        nc.vector.tensor_tensor(lgf, lgf, small8[:, 0, :].unsqueeze(2).to_broadcast([P, 8, L]), ALU.subtract)\
                            .then_inc(q["logits_ready"], 1)

                    def att_product(g):
                        step = stepper("gnn_step", g, GNN_STEPS, False)
                        lgf = lg[:, :, :, :].rearrange("p a t m -> p (a t) m")
                        dve.wait_ge(q["exp_done"], g * 2 + 2)
                        nc.vector.tensor_reduce(sm(13), prior[:, :, :], AX.X, ALU.add)
                        step(nc.vector.tensor_reduce(small8[:, 1, :], lgf, AX.X, ALU.add))
                        step(nc.vector.tensor_tensor(sm(16), sm(13), small8[:, 1, 0:4], ALU.mult))
                        nc.vector.reciprocal(sm(17), small8[:, 1, 4:8])
                        step(nc.vector.reciprocal(sm(16), sm(16)))
                        step(nc.vector.tensor_tensor(prior[:, :, :], prior[:, :, :], lg[:, 0, :, :], ALU.mult))
                        step(nc.vector.tensor_tensor(prior[:, :, :], prior[:, :, :], wide(sm(16)), ALU.mult))
                        step(nc.vector.tensor_tensor(prior[:, :, :], prior[:, :, :], keep[:, 0, :, :], ALU.mult))
                        step(nc.vector.tensor_tensor(prior[:, :, :], prior[:, :, :], neg[:, 0, :, :], ALU.add))
                        step(nc.vector.tensor_reduce(sm(10), prior[:, :, :], AX.X, ALU.max))
                        nc.vector.tensor_tensor(prior[:, :, :], prior[:, :, :], wide(sm(10)), ALU.subtract)\
                            .then_inc(q["product_ready"], 1)
                        for i in range(2):
                            r = parts(i)
                            nc.vector.tensor_tensor(Nb[r, :, i * L:(i + 1) * L], lg[r, 1, :, :], wide(sm(17)[r]), ALU.mult)

                    def att_blocks(g):
                        step = stepper("gnn_step", g, GNN_STEPS, False)
                        dve.wait_ge(q["exp2_done"], g + 1)
                        step(nc.vector.tensor_reduce(sm(18), prior[:, :, :], AX.X, ALU.add))
                        step(nc.vector.reciprocal(sm(18), sm(18)))
                        for i in range(2):
                            r = parts(i)
                            ins = nc.vector.tensor_tensor(Fb[r, :, i * L:(i + 1) * L], prior[r, :, :], wide(sm(18)[r]), ALU.mult)
                        ins.then_inc(q["blocks_ready"], 1)

                    def x1_take(g):
                        step = stepper("gnn_step", g, GNN_STEPS, False)
                        dve.wait_ge(q["x1_stored"], g * 16)
                        dve.wait_ge(q["g_added"], g * T + T)
                        for t in range(T):
                            dve.wait_ge(q["x1_mm"], g * T + t + 1)
                            nc.vector.tensor_tensor(x1[:, t, :], bank[(3, 0, 1, 2)[t]][:, 0:D], xg[:, t, :], ALU.add)\
                                .then_inc(q["x1_taken"], 1)
                        dve.wait_ge(q["x1_taken"], g * T + T)
                        stat(x1, mvh, step)
                        nc.vector.tensor_scalar(sm(2), mvh[:, :, 1], EPS, None, ALU.add).then_inc(q["var1_ready"], 1)
                        assert count["gnn_step"] == GNN_STEPS, count

                    def normalise_twice(g):
                        dve.wait_ge(q["rstd1_ready"], g + 1)
                        for t in range(T):
                            nc.vector.tensor_scalar(hid[:, t, :], x1[:, t, :], mvh[:, t, 0:1], small[:, 3, t:t + 1],
                                                    ALU.subtract, ALU.mult).then_inc(q["hid_ready"], 1)
                        for t in range(T):
                            dve.wait_ge(q["hid_ready"], g * T + t + 1)
                            nc.vector.tensor_scalar(nh[:, t, :], hid[:, t, :], small[:, 5, t:t + 1], None, ALU.mult)\
                                .then_inc(q["nh_ready"], 1)

                    def scores(g):
                        step = stepper("attn_step", g, ATTN_STEPS, True)
                        dve.wait_ge(q["z_exp"], g + 1)
                        step(nc.vector.tensor_scalar(sm(9), sm(8), 1.0, None, ALU.add))
                        step(nc.vector.reciprocal(sm(9), sm(9)))
                        nc.vector.tensor_tensor(diag, node.unsqueeze(1).to_broadcast([P, T, L]), wide(sm(9)), ALU.mult)\
                            .then_inc(q["score_diag"], 1)

                    def picks(g):
                        step = stepper("attn_step", g, ATTN_STEPS, False)
                        dve.wait_ge(q["bc_mm"], g + 1)
                        nc.vector.tensor_copy(bc[:, :, :], bank[6][:, 0:T * L]).then_inc(q["bc_taken"], 1)
                        dve.wait_ge(q["bc_taken"], g + 1)
                        nc.vector.tensor_reduce(sm(20), bc[:, :, :], AX.X, ALU.add)
                        step(nc.vector.tensor_tensor(cmp[:, 0, :, :], bc[:, :, :], node.unsqueeze(1).to_broadcast([P, T, L]), ALU.mult))
                        step(nc.vector.tensor_reduce(sm(9), cmp[:, 0, :, :], AX.X, ALU.add))
                        nc.vector.tensor_tensor(cmp[:, 0, :, :], bc[:, :, :], wide(sm(9)), ALU.is_lt)
                        step(nc.vector.tensor_tensor(cmp[:, 1, :, :], bc[:, :, :], wide(sm(9)), ALU.is_equal))
                        step(nc.vector.tensor_tensor(cmp[:, 1, :, :], cmp[:, 1, :, :], earlier.unsqueeze(1).to_broadcast([P, T, L]), ALU.mult))
                        step(nc.vector.tensor_tensor(cmp[:, 0, :, :], cmp[:, 0, :, :], cmp[:, 1, :, :], ALU.add))
                        step(nc.vector.tensor_reduce(sm(21), cmp[:, 0, :, :], AX.X, ALU.add))
                        nc.vector.tensor_scalar(sm(22), sm(21), float(K), None, ALU.is_ge)
                        step(nc.vector.tensor_scalar(sm(23), sm(20), 1e-6, None, ALU.add))
                        step(nc.vector.reciprocal(sm(23), sm(23)))
                        nc.vector.tensor_tensor(sm(20), sm(20), sm(23), ALU.mult)
                        nc.vector.tensor_tensor(sm(25), sm(9), sm(22), ALU.mult)
                        step(nc.vector.tensor_tensor(sm(24), sm(9), sm(23), ALU.mult))
                        nc.vector.tensor_copy(scat[:, :, ROW_BIAS], sm(22))
                        nc.vector.tensor_tensor(scat[:, :, ROW_B1], sm(25), sm(20), ALU.mult)
                        flat = scat[:, :, :].rearrange("p t k -> p (t k)")
                        for i in range(2):
                            r = parts(i)
                            nc.vector.tensor_copy(gath[r, :, 2 * K + i], sm(24)[r])
                            nc.vector.tensor_copy(flat[r, ROW_POOL + i:ROW_POOL + i + (T - 1) * (RR + 2) + 1:RR + 2], sm(25)[r])
                            rank_b = sm(21)[r].unsqueeze(2).to_broadcast([L, T, K])
                            iota_b = iota[r].unsqueeze(1).to_broadcast([L, T, K])
                            nc.vector.tensor_tensor(gath[r, :, i * K:(i + 1) * K], iota_b, rank_b, ALU.is_equal)
                            for t in range(T):
                                ins = nc.vector.tensor_scalar(scat[r, t, (2 * t + i) * K:(2 * t + i + 1) * K], iota[r],
                                                              small[r, 21, t:t + 1], None, ALU.is_equal)
                        ins.then_inc(q["picks_ready"], 1)
                        assert count["attn_step"] == ATTN_STEPS - 4, count

                    def unrouted(g):
                        dve.wait_ge(q["picks_ready"], g + 1)
                        for t in range(T):
                            nc.vector.scalar_tensor_tensor(out=y_sb[:, t, 0:D], in0=y_sb[:, t, 0:D], scalar=small[:, 22, t:t + 1],
                                                           in1=hid[:, t, :], op0=ALU.mult, op1=ALU.add).then_inc(q["y_ready"], 1)

                    def pooled(g):
                        step = stepper("attn_step", g, ATTN_STEPS, False)
                        dve.wait_ge(q["sel_taken"], g + 1)
                        step(nc.vector.tensor_copy(pool_f[:, :, :].rearrange("p c (t k) -> p c t k", t=T), sel_sb[:, :, :, 2 * K:SELW]))
                        nc.vector.tensor_copy(POOL[0][:, :, ROW_POOL:ROW_BIAS], pool_f[:, :, :]).then_inc(q["pool_hi"], 1)
                        dve.wait_ge(q["pool_hi"], g + 1)
                        nc.vector.tensor_tensor(POOL[1][:, :, ROW_POOL:ROW_BIAS], pool_f[:, :, :], POOL[0][:, :, ROW_POOL:ROW_BIAS],
                                                ALU.subtract).then_inc(q["pool_lo"], 1)

                    def queries(g):
                        dve.wait_ge(q["q_mm"], g + 1)
                        qp = bank[4][:, 0:C * GB * K].rearrange("p (c b k) -> p c b k", c=C, b=GB)
                        for h in range(HC):
                            r = slice(h * DH, (h + 1) * DH)
                            for c in range(C):
                                ins = nc.vector.tensor_scalar(q_blk[r, c, :, c * HC + h, :], qp[r, c, :, :], bqT[r, c:c + 1], None,
                                                              ALU.add)
                        ins.then_inc(q["q_taken"], 1)

                    mx = small8[0:H * K, 2, :]

                    def logits(g):
                        step = stepper("attn_step", g, ATTN_STEPS, False)
                        dve.wait_ge(q["lg_mm"], g + 1)
                        lgp = bank[5][0:H * K, :].rearrange("p (b m) -> p b m", b=GB)
                        step(nc.vector.tensor_reduce(mx, lgp, AX.X, ALU.max))
                        nc.vector.tensor_tensor(prob, lgp, mx.unsqueeze(2).to_broadcast([H * K, GB, L]), ALU.subtract)\
                            .then_inc(q["lg_taken"], 1)

                    def probabilities(g):
                        step = stepper("attn_step", g, ATTN_STEPS, False)
                        dve.wait_ge(q["lgexp"], g + 1)
                        step(nc.vector.tensor_reduce(mx, prob, AX.X, ALU.add))
                        step(nc.vector.reciprocal(mx, mx))
                        nc.vector.tensor_tensor(prob, prob, mx.unsqueeze(2).to_broadcast([H * K, GB, L]), ALU.mult)\
                            .then_inc(q["prob_ready"], 1)
                        assert count["attn_step"] == ATTN_STEPS, count

                    def merge(g):
                        dve.wait_ge(q["r_mm"], g + 1)
                        nc.vector.tensor_tensor(r_sb, bank[5][0:RR, 0:D], r_bias[:, :], ALU.add).then_inc(q["r_taken"], 1)
                        dve.wait_ge(q["y_ready"], g * T + T)
                        for t in range(T):
                            dve.wait_ge(q["out_mm"], g * T + t + 1)
                            nc.vector.tensor_tensor(y_sb[:, t, 0:D], bank[(7, 4, 5, 6)[t]][:, 0:D], y_sb[:, t, 0:D], ALU.add)\
                                .then_inc(q["h_ready"], 1)

                    def both(a, b, nxt):
                        if a is not None:
                            masks(a)
                            lows(0, XT, "xt_hi", "xt_lo", a)
                        if b is not None:
                            normalise_twice(b)
                        if a is not None:
                            t_lo(a)
                        if b is not None:
                            lows(4, NHT, "nht_hi", "nht_lo", b)
                        if a is not None:
                            att_logits(a)
                            att_product(a)
                        if b is not None:
                            scores(b)
                        if a is not None:
                            att_blocks(a)
                        if b is not None:
                            picks(b)
                        if a is not None:
                            lows(1, XT, "y_hi", "y_lo", a)
                        if b is not None:
                            queries(b)
                            pooled(b)
                            unrouted(b)
                            logits(b)
                        if b is not None:
                            probabilities(b)
                        if nxt is not None:
                            normalise(nxt)
                        if a is not None:
                            lows(0, TT, "ng_hi", "ng_lo", a)
                        if b is not None:
                            merge(b)
                        if a is not None:
                            x1_take(a)

                    normalise(0)
                    over_groups(dve, both)

                @block.tensor
                def _(pe):
                    pe.wait_ge(q["zeroed"], 2)

                    def split(out, lhs, rhs):
                        for c in range(C):
                            for i, (a, b) in enumerate(PRODUCTS):
                                mm = nc.tensor.matmul(out, lhs[a][c], rhs[b][c], start=(c == 0 and i == 0),
                                                      stop=(c == C - 1 and i == 2))
                        return mm

                    def cut(pair, at):
                        return [[pair[a][:, c, at] for c in range(C)] for a in range(2)]

                    every = slice(0, GT)
                    rows = slice(0, D)

                    def tile(t):
                        return slice(t * P, (t + 1) * P)

                    def xt(g):
                        pe.wait_ge(q["x1_taken"], g * T)
                        pe.wait_ge(q["xn_ready"], g * T + T)
                        for c in range(C):
                            for t in range(T):
                                mm = nc.tensor.transpose(bank[c][:, tile(t)], xn[:, t, tile(c)], ident)
                            mm.then_inc(q["xt_mm"], 1)

                    def queries_t(g):
                        pe.wait_ge(q["xt_lo"], g * 3 + 3)
                        for m in range(C):
                            split(bank[(3, 0, 1)[m]][:, :], cut(WA, tile(m)), cut(XT, every)).then_inc(q["t_mm"], 1)

                    def att(g):
                        pe.wait_ge(q["t_lo"], g * 3 + 3)
                        for t in range(T):
                            mm = split(bank[2][:, tile(t)], cut(TT, tile(t)), cut(XT, tile(t)))
                        mm.then_inc(q["att_mm"], 1)

                    def fn_t(g):
                        pe.wait_ge(q["blocks_ready"], g + 1)
                        for src, b in ((Fb, 3), (Nb, 0)):
                            for t in range(T):
                                mm = nc.tensor.transpose(bank[b][:, tile(t)], src[:, t, :], ident)
                            mm.then_inc(q["fn_mm"], 1)

                    def fx(g):
                        pe.wait_ge(q["fn_taken"], g * 2 + 1)
                        for c in range(C):
                            for t in range(T):
                                mm = nc.tensor.matmul(bank[1 + c][:, tile(t)], xn[:, t, tile(c)], FT[:, t, :], start=True, stop=True)
                            mm.then_inc(q["y_mm"], 1)

                    def first_g(g, ts):
                        pe.wait_ge(q["y_lo"], g * 3 + 3)
                        pe.wait_ge(q["fn_taken"], g * 2 + 2)
                        for t in ts:
                            split(bank[t][:, 0:D], cut(XT, tile(t)), cut(W3T, rows)).then_inc(q["g_mm"], 1)

                    def ng(g, cs):
                        pe.wait_ge(q["g_taken"], g * T + T)
                        for c in cs:
                            for t in range(T):
                                mm = nc.tensor.matmul(bank[c][:, tile(t)], g_sb[:, t, tile(c)], NT[:, t, :], start=True, stop=True)
                            mm.then_inc(q["ng_mm"], 1)

                    def second_g(g):
                        pe.wait_ge(q["ng_lo"], g * 3 + 3)
                        for t in range(T):
                            split(bank[(3, 0, 1, 2)[t]][:, 0:D], cut(TT, tile(t)), cut(W4T, rows)).then_inc(q["x1_mm"], 1)

                    def nht(g):
                        pe.wait_ge(q["h_ready"], g * T)
                        pe.wait_ge(q["nh_ready"], g * T + T)
                        for c in range(C):
                            for t in range(T):
                                mm = nc.tensor.transpose(bank[4 + c][:, tile(t)], nh[:, t, tile(c)], ident)
                            mm.then_inc(q["nht_mm"], 1)

                    def mixed(g):
                        pe.wait_ge(q["nht_lo"], g * 3 + 3)
                        for t in range(T):
                            split(bank[(7, 4, 5, 6)[t]][:, 0:WM], cut(NHT, tile(t)), cut(WMR, slice(0, WM))).then_inc(q["wm_mm"], 1)

                    def keys(g):
                        for m in range(C):
                            pe.wait_ge(q["wm_taken"], g * T + m + 1)
                            split(bank[(7, 4, 5)[m]][:, :], cut(WK, tile(m)), cut(NHT, every)).then_inc(q["k_mm"], 1)

                    def spread(g):
                        pe.wait_ge(q["wm_taken"], g * T + 4)
                        pe.wait_ge(q["score_diag"], g + 1)
                        nc.tensor.matmul(bank[6][:, 0:T * L], same, diag, start=True, stop=True).then_inc(q["bc_mm"], 1)

                    def values(g):
                        for t in range(T):
                            if t < 3:
                                pe.wait_ge(q["k_taken"], g * 3 + t + 1)
                            else:
                                pe.wait_ge(q["bc_taken"], g + 1)
                            split(bank[(7, 4, 5, 6)[t]][:, 0:D], cut(NHT, tile(t)), cut(WV, rows)).then_inc(q["v_mm"], 1)

                    def gather(g):
                        pe.wait_ge(q["v_taken"], g * T + 1)
                        pe.wait_ge(q["picks_ready"], g + 1)
                        for c in range(C):
                            for t in range(T):
                                at = (c * T + t) * SELW
                                mm = nc.tensor.matmul(bank[7][:, at:at + SELW], nh[:, t, tile(c)], gath[:, t, :], start=True, stop=True)
                        mm.then_inc(q["sel_mm"], 1)

                    def picked_queries(g):
                        pe.wait_ge(q["v_taken"], g * T + 4)
                        pe.wait_ge(q["sel_taken"], g + 1)
                        for m in range(C):
                            for c in range(C):
                                mm = nc.tensor.matmul(bank[4][:, m * GB * K:(m + 1) * GB * K], WQ[:, c, tile(m)],
                                                      sel_sb[:, c, :, 0:2 * K], start=(c == 0), stop=(c == C - 1))
                        mm.then_inc(q["q_mm"], 1)

                    def attn_logits(g):
                        pe.wait_ge(q["q_taken"], g + 1)
                        for b in range(GB):
                            for c in range(C):
                                at = c * GT + b * L
                                mm = nc.tensor.matmul(bank[5][0:H * K, b * L:(b + 1) * L], q_blk[:, c, b, :, :].rearrange("p h k -> p (h k)"),
                                                      kT[:, at:at + L], start=(c == 0), stop=(c == C - 1))
                        mm.then_inc(q["lg_mm"], 1)

                    def prob_t(g):
                        pe.wait_ge(q["prob_ready"], g + 1)
                        for t in range(T):
                            mm = nc.tensor.transpose(bank[6][:, t * H * K:(t + 1) * H * K],
                                                     kT[0:H * K, tile(t)], ident[0:H * K, 0:H * K])
                        mm.then_inc(q["pt_mm"], 1)

                    def contexts(g):
                        pe.wait_ge(q["pt_taken"], g * 2 + 2)
                        for n in range(2):
                            for c in range(C):
                                for t in range(2):
                                    at = (c * 2 + t) * 2 * HC * K
                                    mm = nc.tensor.matmul(bank[(7, 4)[n]][:, at:at + 2 * HC * K], v_sb[:, 2 * n + t, tile(c)],
                                                          p_blk[:, c, 2 * n + t, :, :].rearrange("p b k -> p (b k)"), start=True, stop=True)
                            mm.then_inc(q["pv_mm"], 1)

                    def scatter_t(g):
                        for t in range(T):
                            mm = nc.tensor.transpose(bank[6][0:RR, tile(t)], scat[:, t, :], ident)
                        mm.then_inc(q["st_mm"], 1)

                    def pooled_rows(g):
                        pe.wait_ge(q["pool_lo"], g + 1)
                        for c in range(C):
                            for i, (a, b) in enumerate(PRODUCTS):
                                nc.tensor.matmul(bank[5][0:RR, 0:D], POOL[a][:, c, :], WMR[b][:, c, 0:D],
                                                 start=(c == 0 and i == 0), stop=False, skip_group_check=True)

                    def context_rows(g):
                        pe.wait_ge(q["pv_taken"], g * 2 + 2)
                        for c in range(C):
                            mm = nc.tensor.matmul(bank[5][0:GB * K, 0:D], ctxT[:, c, :], WO[:, c, :], start=False,
                                                  stop=(c == C - 1), skip_group_check=True)
                        mm.then_inc(q["r_mm"], 1)

                    def scatter(g):
                        pe.wait_ge(q["r_taken"], g + 1)
                        pe.wait_ge(q["st_taken"], g + 1)
                        for t in range(T):
                            nc.tensor.matmul(bank[(7, 4, 5, 6)[t]][:, 0:D], scatT[:, t, :], r_sb, start=True, stop=True)\
                                .then_inc(q["out_mm"], 1)

                    def both(a, b, nxt):
                        if a is not None:
                            xt(a)
                            queries_t(a)
                        if b is not None:
                            nht(b)
                        if a is not None:
                            att(a)
                        if b is not None:
                            mixed(b)
                            keys(b)
                            spread(b)
                        if a is not None:
                            fn_t(a)
                        if b is not None:
                            values(b)
                        if a is not None:
                            fx(a)
                        if b is not None:
                            gather(b)
                        if a is not None:
                            first_g(a, (0, 1))
                        if b is not None:
                            picked_queries(b)
                        if a is not None:
                            first_g(a, (2, 3))
                        if b is not None:
                            attn_logits(b)
                        if a is not None:
                            ng(a, (0, 1))
                        if b is not None:
                            prob_t(b)
                            pooled_rows(b)
                            contexts(b)
                            scatter_t(b)
                        if a is not None:
                            ng(a, (2, ))
                        if b is not None:
                            context_rows(b)
                            scatter(b)
                        if a is not None:
                            second_g(a)

                    over_groups(pe, both)
        phase1.close()

        W1S = [sb(f"w1s{i}", [P, C, F], F32R) for i in range(2)]
        W2S = [sb(f"w2s{i}", [P, FC, D], F32R) for i in range(2)]
        hb = sb("hb", [P, FC])
        bf2_bc = sb("bf2_bc", [P, D])
        with ExitStack() as stage:
            s = lambda name, shape, dt=F32: sb(name, shape, dt, stage)
            w1_raw, w2_raw = s("w1_raw", [P, C, F]), s("w2_raw", [P, FC, D])
            g2c, b2c, bf1c = s("g2c", [P, C]), s("b2c", [P, C]), s("bf1c", [P, FC])
            bf2r, one_row = s("bf2r", [1, D]), s("one_row", [1, P])
            loaded, mults, scaled, hi_made, ones_set = (sem(n, stage) for n in
                                                       ("mlp_loaded", "mlp_bias", "mlp_scaled", "mlp_high", "mlp_ones"))
            with nc.Block() as block:
                @block.sync
                def _(sp):
                    for dst, src in ((w1_raw[:, :, :], chunks(W1)), (w2_raw[:, :, :], W2.rearrange("(c p) n -> p c n", p=P)),
                                     (g2c[:, :], column(g2)), (b2c[:, :], column(b2)), (bf1c[:, :], column(bf1)), (bf2r[:, :], row(bf2))):
                        sp.dma_start(dst, src, allow_slow_non_contiguous=True).then_inc(loaded, 16)

                @block.tensor
                def _(pe):
                    pe.wait_ge(loaded, 96)
                    pe.wait_ge(ones_set, 1)
                    for m in range(FC):
                        for c in range(C):
                            nc.tensor.matmul(bank[0][:, m:m + 1], w1_raw[:, c, m * P:(m + 1) * P], b2c[:, c:c + 1],
                                             start=(c == 0), stop=(c == C - 1))
                    nc.tensor.matmul(bank[1][:, 0:D], one_row[:, :], bf2r[:, :], start=True, stop=True).then_inc(mults, 1)

                @block.scalar
                def _(act):
                    act.wait_ge(loaded, 96)
                    for m in range(FC):
                        nc.scalar.copy(W2S[0][:, m, :], w2_raw[:, m, :]).then_inc(hi_made, 1)

                @block.vector
                def _(dve):
                    nc.vector.memset(one_row[:, :], 1.0).then_inc(ones_set, 1)
                    dve.wait_ge(mults, 1)
                    for c in range(C):
                        nc.vector.tensor_scalar(w1_raw[:, c, :], w1_raw[:, c, :], g2c[:, c:c + 1], None, ALU.mult).then_inc(scaled, 1)
                    dve.wait_ge(scaled, C)
                    for c in range(C):
                        nc.vector.tensor_copy(W1S[0][:, c, :], w1_raw[:, c, :]).then_inc(scaled, 1)
                    dve.wait_ge(scaled, 2 * C)
                    nc.vector.tensor_tensor(W1S[1][:, :, :], w1_raw[:, :, :], W1S[0][:, :, :], ALU.subtract)
                    nc.vector.tensor_tensor(hb[:, :], bank[0][:, 0:FC], bf1c[:, :], ALU.add)
                    nc.vector.tensor_copy(bf2_bc[:, :], bank[1][:, 0:D])
                    for m in range(FC):
                        dve.wait_ge(hi_made, m + 1)
                        nc.vector.tensor_tensor(W2S[1][:, m, :], w2_raw[:, m, :], W2S[0][:, m, :], ALU.subtract)

        h_in = sb("h_in", [P, T, D])
        x1_in = sb("x1_in", [P, T, D])
        res = sb("res", [P, T, D])
        n2 = sb("n2", [P, T, D])
        o_sb = sb("o_sb", [P, T, D])
        NT2 = [sb(f"n2t{i}", [P, C, GT], F32R) for i in range(2)]
        R3 = 3
        hid_f = sb("hid_f", [P, R3, GT])
        HID = [sb(f"hid{i}", [P, R3, GT], F32R) for i in range(2)]
        stats = sb("mlp_stats", [P, T, 6])
        mv = sb("mlp_mv", [P, T, 2])
        var = sb("mlp_var", [P, T])
        rstd = sb("mlp_rstd", [P, T])
        half = sb("mlp_mhalf", [P, T])
        order = sb("mlp_order", [P, 1])
        TB = (6, 7, 6)
        with ExitStack() as c2:
            q = {n: sem(n, c2) for n in ("h_loaded x1_loaded stat_step var_ready rstd_ready n2_ready res_step res_ready n2t_mm n2t_hi "
                                         "n2t_lo h_mm gelu_done h_hi h_lo out_mm out_taken stored half_set").split()}

            def over_groups(eng, group):
                group(0, False)
                with eng.Fori(1, G - 1) as g:
                    group(g, False)
                group(G - 1, True)

            with nc.Block() as block:
                @block.sync
                def _(sp):
                    def load(g):
                        sp.wait_ge(q["n2_ready"], g)
                        sp.wait_ge(q["res_ready"], g)
                        sp.dma_start(h_in[:, :, :], h_g[g]).then_inc(q["h_loaded"], 16)
                        sp.dma_start(x1_in[:, :, :], x1_g[g]).then_inc(q["x1_loaded"], 16)

                    sp.dma_start(h_in[:, :, :], h_g[0]).then_inc(q["h_loaded"], 16)
                    sp.dma_start(x1_in[:, :, :], x1_g[0]).then_inc(q["x1_loaded"], 16)

                    def group(g, last):
                        if not last:
                            load(g + 1)
                        sp.wait_ge(q["out_taken"], g * T + T)
                        sp.dma_start(out_g[g], o_sb[:, :, :]).then_inc(q["stored"], 16)

                    over_groups(sp, group)
                    sp.wait_ge(q["stored"], 16 * G)

                @block.gpsimd
                def _(pool):
                    nc.gpsimd.memset(half[:, :], -0.5).then_inc(q["half_set"], 1)
                    pool.wait_ge(q["half_set"], 1)

                    def power(g):
                        pool.wait_ge(q["var_ready"], g + 1)
                        nc.gpsimd.tensor_tensor(rstd[:, :], var[:, :], half[:, :], ALU.pow).then_inc(q["rstd_ready"], 1)

                    def group(g, last):
                        pool.wait_ge(q["out_taken"], g * T)
                        pool.wait_ge(q["x1_loaded"], g * 16 + 16)
                        nc.gpsimd.tensor_tensor(res[:, :, :], x1_in[:, :, :], h_in[:, :, :], ALU.add).then_inc(q["res_step"], 1)
                        pool.wait_ge(q["res_step"], g + 1)
                        nc.gpsimd.tensor_tensor(res[:, :, :], res[:, :, :], bf2_bc[:, :].unsqueeze(1).to_broadcast([P, T, D]),
                                                ALU.add).then_inc(q["res_ready"], 1)
                        if not last:
                            power(g + 1)

                    power(0)
                    over_groups(pool, group)

                @block.scalar
                def _(act):
                    def turned(g):
                        for c in range(C):
                            act.wait_ge(q["n2t_mm"], g * C + c + 1)
                            nc.scalar.copy(NT2[0][:, c, :], bank[TB[c]][:, :]).then_inc(q["n2t_hi"], 1)

                    def group(g, last):
                        for m in range(FC):
                            act.wait_ge(q["h_mm"], g * FC + m + 1)
                            if m >= R3:
                                act.wait_ge(q["h_lo"], g * FC + m - R3 + 1)
                            nc.scalar.activation(hid_f[:, m % R3, :], bank[4 + m % 2][:, :], ACT.Gelu,
                                                 bias=hb[:, m:m + 1]).then_inc(q["gelu_done"], 1)
                        if not last:
                            turned(g + 1)

                    turned(0)
                    over_groups(act, group)

                @block.vector
                def _(dve):
                    def normalise(g):
                        dve.wait_ge(q["h_loaded"], g * 16 + 16)
                        for t in range(T):
                            ins = nc.vector.bn_stats(stats[:, t, :], h_in[:, t, :])
                        ins.then_inc(q["stat_step"], 1)
                        dve.wait_ge(q["stat_step"], g * 2 + 1)
                        nc.vector.tensor_copy(order[:, :], stats[:, 0, 0:1])
                        for t in range(T):
                            ins = nc.vector.bn_aggr(mv[:, t, :], stats[:, t, :])
                        ins.then_inc(q["stat_step"], 1)
                        dve.wait_ge(q["stat_step"], g * 2 + 2)
                        nc.vector.tensor_scalar(var[:, :], mv[:, :, 1], EPS, None, ALU.add).then_inc(q["var_ready"], 1)

                    def scale_rows(g):
                        dve.wait_ge(q["n2t_mm"], g * C)
                        dve.wait_ge(q["rstd_ready"], g + 1)
                        for t in range(T):
                            ins = nc.vector.tensor_scalar(n2[:, t, :], h_in[:, t, :], mv[:, t, 0:1], rstd[:, t:t + 1],
                                                          ALU.subtract, ALU.mult)
                        ins.then_inc(q["n2_ready"], 1)

                    def turned(g):
                        for c in range(C):
                            dve.wait_ge(q["n2t_hi"], g * C + c + 1)
                            nc.vector.tensor_tensor(NT2[1][:, c, :], bank[TB[c]][:, :], NT2[0][:, c, :], ALU.subtract)\
                                .then_inc(q["n2t_lo"], 1)

                    def group(g, last):
                        for m in range(FC):
                            dve.wait_ge(q["gelu_done"], g * FC + m + 1)
                            if m >= R3:
                                dve.wait_ge(q["out_mm"], g * FC + m - R3 + 1)
                            nc.vector.tensor_copy(HID[0][:, m % R3, :], hid_f[:, m % R3, :]).then_inc(q["h_hi"], 1)
                            dve.wait_ge(q["h_hi"], g * FC + m + 1)
                            nc.vector.tensor_tensor(HID[1][:, m % R3, :], hid_f[:, m % R3, :], HID[0][:, m % R3, :], ALU.subtract)\
                                .then_inc(q["h_lo"], 1)
                            if m == 3 and not last:
                                normalise(g + 1)
                            if m == 6 and not last:
                                scale_rows(g + 1)
                        if not last:
                            turned(g + 1)
                        dve.wait_ge(q["res_ready"], g + 1)
                        dve.wait_ge(q["stored"], g * 16)
                        dve.wait_ge(q["out_mm"], g * FC + FC)
                        for t in range(T):
                            nc.vector.tensor_tensor(o_sb[:, t, :], bank[t][:, 0:D], res[:, t, :], ALU.add)\
                                .then_inc(q["out_taken"], 1)

                    normalise(0)
                    scale_rows(0)
                    turned(0)
                    over_groups(dve, group)

                @block.tensor
                def _(pe):
                    def turn(g, cs):
                        for c in cs:
                            if c == 0:
                                pe.wait_ge(q["n2_ready"], g + 1)
                            if c == 2:
                                pe.wait_ge(q["n2t_lo"], g * C + 1)
                            for t in range(T):
                                mm = nc.tensor.transpose(bank[TB[c]][:, t * P:(t + 1) * P], n2[:, t, c * P:(c + 1) * P], ident)
                            mm.then_inc(q["n2t_mm"], 1)

                    def up(g, m):
                        if m >= 2:
                            pe.wait_ge(q["gelu_done"], g * FC + m - 1)
                        elif m == 0:
                            pe.wait_ge(q["n2t_lo"], g * C + C)
                            pe.wait_ge(q["gelu_done"], g * FC)
                        for c in range(C):
                            for i, (a, b) in enumerate(PRODUCTS):
                                mm = nc.tensor.matmul(bank[4 + m % 2][:, :], W1S[a][:, c, m * P:(m + 1) * P], NT2[b][:, c, :],
                                                      start=(c == 0 and i == 0), stop=(c == C - 1 and i == 2))
                        mm.then_inc(q["h_mm"], 1)

                    def down(g, k):
                        pe.wait_ge(q["h_lo"], g * FC + k + 1)
                        if k == 0:
                            pe.wait_ge(q["out_taken"], g * T)
                        for t in range(T):
                            ts = slice(t * P, (t + 1) * P)
                            for i, (a, b) in enumerate(PRODUCTS):
                                mm = nc.tensor.matmul(bank[t][:, 0:D], HID[a][:, k % R3, ts], W2S[b][:, k, :],
                                                      start=(k == 0 and i == 0), stop=(k == FC - 1 and i == 2))
                        mm.then_inc(q["out_mm"], 1)

                    def group(g, last):
                        up(g, 0)
                        for m in range(1, FC):
                            up(g, m)
                            if m == FC - 1 and not last:
                                turn(g + 1, (0, 1))
                            down(g, m - 1)
                        if not last:
                            turn(g + 1, (2,))
                        down(g, FC - 1)

                    turn(0, (0, 1, 2))
                    over_groups(pe, group)


_INS = ['x', 'adj', 'L0_gnn_W1', 'L0_gnn_b1', 'L0_gnn_W2', 'L0_gnn_b2', 'L0_gnn_W3', 'L0_gnn_b3', 'L0_gnn_W4', 'L0_gnn_b4',
        'L0_ffn_g1', 'L0_ffn_b1', 'L0_ffn_g2', 'L0_ffn_b2', 'L0_ffn_Wr', 'L0_ffn_br', 'L0_ffn_Wq', 'L0_ffn_bq', 'L0_ffn_Wk',
        'L0_ffn_bk', 'L0_ffn_Wv', 'L0_ffn_bv', 'L0_ffn_Wo', 'L0_ffn_bo', 'L0_ffn_Wm', 'L0_ffn_bm', 'L0_ffn_W1', 'L0_ffn_bf1',
        'L0_ffn_W2', 'L0_ffn_bf2']


def kernel(**inputs):
    import numpy as _np
    import concourse.bacc as _bacc
    from concourse import mybir as _mybir
    from concourse.bass_utils import run_bass_kernel_spmd as _run

    nc = _bacc.Bacc("TRN2", target_bir_lowering=False, num_devices=1)
    arrays, args = {}, []
    for name in _INS:
        a = _np.ascontiguousarray(inputs[name])
        if a.ndim == 0 or name.endswith("_br"):
            a = a.reshape(1, 1)
        arrays[f"in_{name}"] = a
    arrays["in_consts"] = constants()
    for name, a in arrays.items():
        args.append(nc.dram_tensor(name, a.shape, _mybir.dt.from_np(a.dtype), kind="ExternalInput").ap())
    args.append(nc.dram_tensor("out_0", (B, L, D), _mybir.dt.float32, kind="ExternalOutput").ap())
    program(nc, *args)
    r = _run(nc, [arrays], core_ids=[0])
    return r.results[0]["out_0"]
```

```python
from contextlib import ExitStack

import numpy as np
import concourse.bass as bass
from concourse import mybir

F32 = mybir.dt.float32
F32R = mybir.dt.float32r
I32 = mybir.dt.int32
ALU = mybir.AluOpType
ACT = mybir.ActivationFunctionType
AX = mybir.AxisListType

P = 128
B, L, D = 128, 64, 384
C = D // P
H, DH, F = 12, 32, 1536
HC = P // DH
FC = F // P
T = 4
GT = T * P
GB = GT // L
G = B * L // GT
K = max(1, int(round(0.15 * L)))
EPS = 1e-5
NEG = -1e9
WM = D + 2
SELW = 2 * K + 2
ROW_POOL, ROW_BIAS, ROW_B1 = GB * K, GB * K + GB, GB * K + GB + 1
ROW_POOL_LOW, ROW_B1_LOW = ROW_B1 + 1, ROW_B1 + 1 + GB
RR = -(-(ROW_B1_LOW + 1) // 4) * 4
PRODUCTS = ((0, 0), (1, 0), (0, 1))
COLUMNS = (X_VAR, X_RSTD, X1_VAR, HID_VAR, X1_RSTD, HID_RSTD, BOTH_RSTD, EXP_Z, SCORE, ROW_MAX, ROW_U, SHARED, PRIOR_SUM,
           PRODUCT_SCALE, OTHERS_SCALE, F_SCALE, SCORE_SUM, RANK, UNROUTED, INV_SUM, WEIGHT, PASSED_SCORE, PASSED_SUM) = range(23)


def constants():
    p = np.arange(P)
    m = np.arange(L)
    ident = np.eye(P)
    same = (p[:, None] // L == p[None, :] // L) * 1.0
    node = (p[:, None] % L == m[None, :]) * 1.0
    earlier = (m[None, :] < p[:, None] % L) * 1.0
    iota = np.broadcast_to(np.arange(K), (P, K))
    picked = np.broadcast_to(np.arange(RR) < GB * K, (P, RR))
    bias = np.broadcast_to(np.arange(RR) == ROW_BIAS, (P, RR))
    return np.concatenate([ident, same, node, earlier, iota, picked, bias], axis=1).astype(np.float32)


CONST_W = 2 * P + 2 * L + K


def program(nc, x, adj, gW1, gb1, gW2, gb2, gW3, gb3, gW4, gb4, g1, b1, g2, b2, Wr, br, Wq, bq, Wk, bk,
            Wv, bv, Wo, bo, Wm, bm, W1, bf1, W2, bf2, consts, out):
    x1_d = nc.dram_tensor("x1_scratch", (B * L, D), F32).ap()
    h_d = nc.dram_tensor("h_scratch", (B * L, D), F32).ap()
    tiles = lambda a: a.rearrange("(g t p) d -> g p t d", t=T, p=P)
    x_g = tiles(x.rearrange("b n d -> (b n) d"))
    adj_g = tiles(adj.rearrange("b n d -> (b n) d"))
    out_g = tiles(out.rearrange("b n d -> (b n) d"))
    x1_g, h_g = tiles(x1_d), tiles(h_d)
    chunks = lambda w: w.rearrange("(c p) n -> p c n", p=P)
    column = lambda v: v.rearrange("(c p) -> p c", p=P)
    row = lambda v: v.rearrange("(a n) -> a n", a=1)

    with ExitStack() as ctx:
        def sb(name, shape, dt=F32, where=ctx):
            return where.enter_context(nc.sbuf_tensor(name, shape, dt))

        def sem(name, where=ctx):
            return where.enter_context(nc.semaphore(name))

        bank = [ctx.enter_context(nc.psum_tensor(f"bank{i}", [P, 512], F32)) for i in range(8)]

        cst = sb("cst", [P, CONST_W])
        ident = cst[:, 0:P]
        same = cst[:, P:2 * P]
        node = cst[:, 2 * P:2 * P + L]
        earlier = cst[:, 2 * P + L:2 * P + 2 * L]
        o = 2 * P + 2 * L
        iota = cst[:, o:o + K]
        WMR = [sb(f"wmr{i}", [P, C, WM], F32R) for i in range(2)]
        WK = [sb(f"wk{i}", [P, C, D], F32R) for i in range(2)]
        WV = [sb(f"wv{i}", [P, C, D], F32R) for i in range(2)]
        WQ = sb("wq", [P, C, D])
        WO = sb("wo", [P, C, D])
        names = ("gb1", "gb2", "gb3", "g1", "b1", "bq", "bk", "bv", "wr", "cT", "bqT", "bkT", "bvT")
        cols = sb("cols", [P, len(names), C])
        col = {n: cols[:, i, :] for i, n in enumerate(names)}
        cT, bqT, bkT, bvT = (col[n] for n in ("cT", "bqT", "bkT", "bvT"))
        singles = sb("singles", [P, 3 + T])
        beta = singles[:, 0:1]
        brn = singles[:, 1:2]
        order = singles[:, 2:3]
        mhalf = singles[:, 3:3 + T]
        r_bias = sb("r_bias", [RR, D])

        x1 = sb("x1", [P, T, D])
        hid = sb("hid", [P, T, D])
        nh = sb("nh", [P, T, D])
        NHT = [sb(f"nht{i}", [P, C, GT], F32R) for i in range(2)]
        y_sb = sb("y_sb", [P, T, WM])
        kT = sb("kT", [P, C * GT])
        v_sb = sb("v_sb", [P, T, D])
        q_blk = sb("q_blk", [P, GB, C, C, HC, K])
        p_blk = sb("p_blk", [P, C, T, 2, HC * K])
        prob = kT[0:H * K, 0:GB * L].rearrange("p (b m) -> p b m", b=GB)
        r_sb = kT[0:RR, 2 * GT:2 * GT + D]
        scatT = NHT[1][0:RR, 0, :].rearrange("p (t n) -> p t n", t=T)
        R_PARTS = [NHT[0][0:RR, i, 0:D] for i in range(2)]
        ctxT = sb("ctxT", [P, C, GB * K])
        POOL = [sb(f"pool{i}", [P, C, RR], F32R) for i in range(2)]
        sel_sb = sb("sel_sb", [P, C, T, SELW])
        SKEW = RR + 2 * K
        scat_gath = sb("scat_gath", [P, K + T * SKEW])
        scat = scat_gath[:, 0:T * RR].rearrange("p (t n) -> p t n", t=T)
        gath = scat_gath[:, T * RR:T * (RR + SELW)].rearrange("p (t n) -> p t n", t=T)
        bc = sb("bc", [P, T, L])
        cmp = sb("cmp", [P, 2, T, L])
        diag = cmp[:, 1, :, :]
        att_sb = sb("att_sb", [P, D])
        junk = att_sb[:, 0:D]
        att_v = att_sb[:, 0:T * L].rearrange("p (t m) -> p t m", t=T)
        stats = sb("stats", [P, T, 6])
        mv = sb("mv", [P, T, 2])
        mvh = sb("mvh", [P, T, 2])
        small = sb("small", [P, len(COLUMNS), T])
        small8 = sb("small8", [P, 3, 8])
        passed = [sb("passed_high", [P, 2, T], F32R), sb("passed_low", [P, 2, T])]

        flat = lambda a: a[:, :, :].rearrange("p t d -> p (t d)")
        raw = {n: flat(a)[:, 0:C * D].rearrange("p (c d) -> p c d", c=C) for n, a in (("wk", hid), ("wv", nh), ("wm", y_sb))}
        b1_bc = kT[:, 0:C * P].rearrange("p (c n) -> p c n", c=C)
        o = C * P
        b1_rows = kT[:, o:o + C * RR].rearrange("p (c n) -> p c n", c=C)
        o += C * RR
        bv_rows = kT[:, o:o + C * RR].rearrange("p (c n) -> p c n", c=C)
        o += C * RR
        ones = kT[:, o:o + P]
        o += P
        rowsel = kT[:, o:o + 2 * RR]
        picked, biasrow = rowsel[:, 0:RR], rowsel[:, RR:2 * RR]
        bo_row, bm_row = (flat(a)[0:1, C * D:C * D + D] for a in (hid, nh))
        br_one = flat(y_sb)[0:1, C * D:C * D + 1]

        gnn = ctx.enter_context(ExitStack())
        gn = lambda name, shape, dt=F32: sb(name, shape, dt, gnn)
        WA = [gn(f"wa{i}", [P, C, D], F32R) for i in range(2)]
        W3T = [gn(f"w3t{i}", [P, C, D], F32R) for i in range(2)]
        W4T = [gn(f"w4t{i}", [P, C, D], F32R) for i in range(2)]
        u_bc = gn("u_bc", [P, D])
        g_bias = gn("g_bias", [P, D])

        x_in = gn("x_in", [P, T, D])
        xn = gn("xn", [P, T, D])
        adj_in = gn("adj_in", [P, T, L], I32)
        with ExitStack() as stage:
            gnn_raw = {n: sb(f"raw_{n}", [P, C, D], F32, stage) for n in ("w1", "w2", "w3", "w4")}
            w4t = sb("w4t", [P, C, D], F32, stage)
            b2_bc, b3_bc = (sb(n, [P, C, P], F32, stage) for n in ("b2_bc", "b3_bc"))
            gnn_rows = sb("gnn_rows", [1, 2, D], F32, stage)
        XT = [gn(f"xt{i}", [P, C, GT], F32R) for i in range(2)]
        keep = gn("keep", [P, 2, T, L])
        neg = gn("neg", [P, 2, T, L])
        lg = gn("lg", [P, 2, T, L])
        prior = gn("prior", [P, T, L])
        Fb, Nb = (gn(n, [P, T, P]) for n in ("Fb", "Nb"))
        FT, NT = (gn(n, [P, T, P]) for n in ("FT", "NT"))
        g_sb = gn("g_sb", [P, T, D])
        TT = [gn(f"tt{i}", [P, C, GT], F32R) for i in range(2)]
        xg = gn("xg", [P, T, D])
        xt_f = g_sb[:, :, :].rearrange("p t d -> p (t d)").rearrange("p (c n) -> p c n", c=C)
        t_f = v_sb[:, :, :].rearrange("p t d -> p (t d)").rearrange("p (c n) -> p c n", c=C)

        gnn.close()

        W1S = [sb(f"w1s{i}", [P, C, F], F32R) for i in range(2)]
        W2S = [sb(f"w2s{i}", [P, FC, D], F32R) for i in range(2)]
        hb = sb("hb", [P, FC])
        bf2_bc = sb("bf2_bc", [P, D])
        w_stage = ctx.enter_context(ExitStack())
        w_raw = sb("w_raw", [P, C * F], F32, w_stage)
        w1_raw = w_raw[:, :].rearrange("p (c n) -> p c n", c=C)
        w2_raw = w_raw[:, :].rearrange("p (c n) -> p c n", c=FC)
        g2c, b2c, bf1c = (sb(n, [P, w], F32, w_stage) for n, w in (("g2c", C), ("b2c", C), ("bf1c", FC)))
        bf2r, one_row = (sb(n, [1, w], F32, w_stage) for n, w in (("bf2r", D), ("one_row", P)))
        h_in, x1_in, n2, NT2, res, o_sb = hid, x1, v_sb, NHT, nh, y_sb[:, :, 0:D]
        R3 = 3
        hid_f = kT[:, :].rearrange("p (r n) -> p r n", r=R3)
        mlp_stats, mlp_mv, mlp_var, mlp_rstd = stats, mv, small[:, X_VAR, :], small[:, X_RSTD, :]
        h_stored = sem("h_stored")
        mlp = {n: sem("mlp_" + n) for n in ("h_loaded x1_loaded stat_step var_ready rstd_ready n2_ready res_step res_ready n2t_mm n2t_hi "
                                   "n2t_lo h_mm gelu_done h_hi h_lo out_mm out_taken stored").split()}

        def normalise(dve, g):
            dve.wait_ge(mlp["h_loaded"], g * 16 + 16)
            for t in range(T):
                ins = nc.vector.bn_stats(mlp_stats[:, t, :], h_in[:, t, :])
            ins.then_inc(mlp["stat_step"], 1)
            dve.wait_ge(mlp["stat_step"], g * 2 + 1)
            nc.vector.tensor_copy(order[:, :], mlp_stats[:, 0, 0:1])
            for t in range(T):
                ins = nc.vector.bn_aggr(mlp_mv[:, t, :], mlp_stats[:, t, :])
            ins.then_inc(mlp["stat_step"], 1)
            dve.wait_ge(mlp["stat_step"], g * 2 + 2)
            nc.vector.tensor_scalar(mlp_var[:, :], mlp_mv[:, :, 1], EPS, None, ALU.add).then_inc(mlp["var_ready"], 1)

        def scale_rows(dve, g):
            dve.wait_ge(mlp["n2t_mm"], g * C)
            dve.wait_ge(mlp["rstd_ready"], g + 1)
            for t in range(T):
                ins = nc.vector.tensor_scalar(n2[:, t, :], h_in[:, t, :], mlp_mv[:, t, 0:1], mlp_rstd[:, t:t + 1],
                                              ALU.subtract, ALU.mult)
            ins.then_inc(mlp["n2_ready"], 1)

        def power(pool, g):
            pool.wait_ge(mlp["var_ready"], g + 1)
            nc.gpsimd.tensor_tensor(mlp_rstd[:, :], mlp_var[:, :], mhalf[:, :], ALU.pow).then_inc(mlp["rstd_ready"], 1)

        with ExitStack() as c1:
            q = {n: sem(n, c1) for n in (
                "x_loaded adj_loaded x1_stored zeroed zeroed_pool "
                "var_ready rstd_ready xn_ready xg_ready adj_read xt_mm xt_hi xt_lo xt_taken t_mm t_taken att_mm "
                "logits_ready exp_done product_ready exp2_done blocks_ready fn_mm fn_taken y_mm y_hi y_lo g_mm g_taken g_added "
                "ng_mm ng_hi ng_lo x1_mm x1_taken "
                "var1_ready rstd1_ready both_ready hid_ready nh_ready nht_mm nht_hi nht_lo wm_mm wm_taken k_mm k_taken z_exp score_diag bc_mm "
                "bc_taken v_mm v_taken picks_ready y_ready sel_mm sel_taken pool_hi pool_lo q_mm q_taken lg_mm lg_taken lgexp "
                "prob_ready pt_mm pt_taken pv_mm pv_taken pv_taken2 r_mm r_step r_taken st_mm st_taken out_mm h_ready "
                "gnn_small_loaded small_loaded w12_loaded w34_loaded kvm_loaded qo_loaded ones_set spread_made b1_spread wa_mm w3_mm "
                "w4_mm wa_hi w3_hi w4_hi w4t_taken wa_lo w3_lo w4_lo kvm_hi kvm_lo c_mm kv_mm br_mm bq_mm wr_step b_step u_mm "
                "mhalf_set c_taken placed gb_mm gb_taken rb_mm "
                "w1_loaded w2_loaded0 w2_loaded1 one_set hb_mm w1_hi w1_lo w2_hi "
                "norm_step gnn_step attn_step").split()}

            def sm(i):
                return small[:, i, :]

            NORM_STEPS, GNN_STEPS, ATTN_STEPS = 9, 19, 17
            XT_BANK, T_BANK, ATT_BANK, X1_BANK = (3, 0, 1), (3, 0, 2), 1, (3, 0, 1, 2)

            def parts(i):
                return (slice(0, L), slice(L, P))[i]

            def over_groups(eng, opening, both, closing):
                opening()
                both(1, 0, 2)
                with eng.Fori(1, G - 2) as i:
                    both(i + 1, i, i + 2)
                both(G - 1, G - 2, None)
                closing(G - 1)

            with nc.Block() as block:
                gnn_small_loads = [(cst[:, :], consts[:, 0:CONST_W])]
                gnn_small_loads += [(col[n], column(v)) for n, v in (("gb1", gb1), ("gb2", gb2), ("gb3", gb3))]
                gnn_small_loads += [(gnn_rows[0:1, i, :], row(v)) for i, v in enumerate((gb3, gb4))]
                small_loads = [(col[n], column(v)) for n, v in
                               (("g1", g1), ("b1", b1), ("bq", bq), ("bk", bk), ("bv", bv), ("wr", Wr))]
                small_loads += [(rowsel, consts[:, CONST_W:CONST_W + 2 * RR]), (br_one, br), (bo_row, row(bo)), (bm_row, row(bm))]
                GNN_SMALL, SMALL = 16 * len(gnn_small_loads), 16 * len(small_loads)

                @block.sync
                def _(sp):
                    def load(g):
                        sp.wait_ge(q["xn_ready"], g * T)
                        sp.wait_ge(q["xg_ready"], g)
                        sp.dma_start(x_in[:, :, :], x_g[g]).then_inc(q["x_loaded"], 16)
                        sp.wait_ge(q["adj_read"], g)
                        sp.dma_start(adj_in[:, :, :], adj_g[g]).then_inc(q["adj_loaded"], 16)

                    def both(a, b, nxt):
                        if nxt is not None:
                            load(nxt)
                        if b is not None:
                            sp.wait_ge(q["h_ready"], b * T + T)
                            sp.dma_start(h_g[b], y_sb[:, :, 0:D]).then_inc(h_stored, 16)
                        if a is not None:
                            sp.wait_ge(q["x1_taken"], a * T + T)
                            sp.dma_start(x1_g[a], x1[:, :, :]).then_inc(q["x1_stored"], 16)

                    def opening():
                        def chunked(dst, src, into):
                            sp.dma_start(dst[:, :, :], chunks(src)).then_inc(q[into], 16)

                        chunked(gnn_raw["w1"], gW1, "w12_loaded")
                        chunked(gnn_raw["w2"], gW2, "w12_loaded")
                        sp.dma_start(x_in[:, :, :], x_g[0]).then_inc(q["x_loaded"], 16)
                        chunked(gnn_raw["w3"], gW3, "w34_loaded")
                        chunked(gnn_raw["w4"], gW4, "w34_loaded")
                        sp.dma_start(adj_in[:, :, :], adj_g[0]).then_inc(q["adj_loaded"], 16)
                        for n, src in (("wk", Wk), ("wv", Wv), ("wm", Wm)):
                            chunked(raw[n], src, "kvm_loaded")
                        chunked(WQ, Wq, "qo_loaded")
                        chunked(WO, Wo, "qo_loaded")
                        both(0, None, 1)

                    def closing(b):
                        sp.wait_ge(q["x1_taken"], G * T)
                        for dst, src in ((w1_raw, chunks(W1)), (g2c[:, :], column(g2)), (b2c[:, :], column(b2)),
                                         (bf1c[:, :], column(bf1)), (bf2r[:, :], row(bf2))):
                            sp.dma_start(dst, src, allow_slow_non_contiguous=True).then_inc(q["w1_loaded"], 16)
                        sp.wait_ge(q["y_ready"], G * T)
                        sp.wait_ge(q["x1_stored"], 16 * G)
                        sp.wait_ge(h_stored, 16 * (G - 1))
                        sp.dma_start(h_in[:, :, :], h_g[0]).then_inc(mlp["h_loaded"], 16)
                        sp.dma_start(x1_in[:, :, :], x1_g[0]).then_inc(mlp["x1_loaded"], 16)
                        sp.wait_ge(q["w1_lo"], C)
                        sp.wait_ge(q["hb_mm"], 2)
                        for i in range(2):
                            part = slice(i * FC // 2, (i + 1) * FC // 2)
                            sp.dma_start(w2_raw[:, part, :], chunks(W2)[:, part, :]).then_inc(q[f"w2_loaded{i}"], 16)
                        sp.wait_ge(q["h_ready"], b * T + T)
                        sp.dma_start(h_g[b], y_sb[:, :, 0:D]).then_inc(h_stored, 16)

                    over_groups(sp, opening, both, closing)

                @block.gpsimd
                def _(pool):
                    for dst, src in small_loads:
                        pool.dma_start(dst, src, allow_slow_non_contiguous=True).then_inc(q["small_loaded"], 16)
                    nc.gpsimd.memset(scat_gath[:, :], 0.0)
                    nc.gpsimd.memset(q_blk[:, :, :, :, :, :], 0.0)
                    nc.gpsimd.memset(p_blk[:, :, :, :, :], 0.0).then_inc(q["zeroed_pool"], 1)

                    def rstd(g):
                        pool.wait_ge(q["var_ready"], g + 1)
                        nc.gpsimd.tensor_tensor(sm(X_RSTD), sm(X_VAR), mhalf[:, :], ALU.pow).then_inc(q["rstd_ready"], 1)

                    def rstd_twice(g):
                        pool.wait_ge(q["var1_ready"], g + 1)
                        nc.gpsimd.tensor_tensor(small[:, X1_RSTD:X1_RSTD + 2, :], small[:, X1_VAR:X1_VAR + 2, :],
                                                mhalf[:, :].unsqueeze(1).to_broadcast([P, 2, T]),
                                                ALU.pow).then_inc(q["rstd1_ready"], 1)

                    def x_and_bias(g):
                        pool.wait_ge(q["x_loaded"], g * 16 + 16)
                        pool.wait_ge(q["x1_taken"], g * T)
                        nc.gpsimd.tensor_tensor(xg[:, :, :], x_in[:, :, :], g_bias[:, :].unsqueeze(1).to_broadcast([P, T, D]),
                                                ALU.add).then_inc(q["xg_ready"], 1)
                        pool.wait_ge(q["xg_ready"], g + 1)

                    def add_g(g, ts):
                        for t in ts:
                            pool.wait_ge(q["g_taken"], g * T + t + 1)
                            nc.gpsimd.tensor_tensor(xg[:, t, :], xg[:, t, :], g_sb[:, t, :], ALU.add).then_inc(q["g_added"], 1)

                    def both(a, b, nxt):
                        if a is not None:
                            x_and_bias(a)
                            add_g(a, (0, 1))
                        if nxt is not None:
                            rstd(nxt)
                        if a is not None:
                            add_g(a, (2, 3))
                            rstd_twice(a)

                    def opening():
                        pool.wait_ge(q["mhalf_set"], 1)
                        rstd(0)
                        pool.wait_ge(q["gb_mm"], 1)
                        nc.gpsimd.memset(Fb[:, :, :], 0.0)
                        nc.gpsimd.memset(Nb[:, :, :], 0.0).then_inc(q["zeroed_pool"], 1)
                        pool.wait_ge(q["gb_taken"], 1)
                        both(0, None, 1)

                    def closing(b):
                        power(pool, 0)

                    over_groups(pool, opening, both, closing)

                @block.scalar
                def _(act):
                    def xt_high(g, c):
                        act.wait_ge(q["xt_taken"], g * 3 + c + 1)
                        nc.scalar.copy(XT[0][:, c, :], xt_f[:, c, :]).then_inc(q["xt_hi"], 1)

                    def xt_take(g):
                        act.wait_ge(q["g_added"], g * T)
                        act.wait_ge(q["ng_mm"], g * 3)
                        for c in range(C):
                            act.wait_ge(q["xt_mm"], g * 3 + c + 1)
                            nc.scalar.copy(xt_f[:, c, :], bank[XT_BANK[c]][:, :]).then_inc(q["xt_taken"], 1)
                            if c > 0:
                                xt_high(g, c - 1)
                        xt_high(g, C - 1)

                    def t_take(g):
                        for c in range(C):
                            act.wait_ge(q["t_mm"], g * 3 + c + 1)
                            nc.scalar.activation(t_f[:, c, :], bank[T_BANK[c]][:, :], ACT.Identity,
                                                 bias=cT[:, c:c + 1]).then_inc(q["t_taken"], 1)

                    def exp_prior(g):
                        act.wait_ge(q["logits_ready"], g * 2 + 1)
                        nc.scalar.activation(prior[:, :, :], prior[:, :, :], ACT.Exp).then_inc(q["exp_done"], 1)

                    def exp_att(g):
                        act.wait_ge(q["logits_ready"], g * 2 + 2)
                        nc.scalar.activation(lg[:, :, :, :], lg[:, :, :, :], ACT.Exp).then_inc(q["exp_done"], 1)

                    def exp_product(g):
                        act.wait_ge(q["product_ready"], g + 1)
                        nc.scalar.activation(prior[:, :, :], prior[:, :, :], ACT.Exp).then_inc(q["exp2_done"], 1)

                    def fn_take(g):
                        for n, (dst, b) in enumerate(((FT, 3), (NT, 0))):
                            act.wait_ge(q["fn_mm"], g * 2 + n + 1)
                            nc.scalar.copy(dst[:, :, :], bank[b][:, :]).then_inc(q["fn_taken"], 1)

                    def y_hi(g):
                        for c in range(C):
                            act.wait_ge(q["y_mm"], g * 3 + c + 1)
                            nc.scalar.copy(XT[0][:, c, :], bank[1 + c][:, :]).then_inc(q["y_hi"], 1)

                    def g_take(g, ts):
                        for t in ts:
                            act.wait_ge(q["g_mm"], g * T + t + 1)
                            nc.scalar.copy(g_sb[:, t, :], bank[t][:, 0:D]).then_inc(q["g_taken"], 1)

                    def ng_hi(g, cs):
                        for c in cs:
                            act.wait_ge(q["ng_mm"], g * 3 + c + 1)
                            nc.scalar.copy(TT[0][:, c, :], bank[c][:, :]).then_inc(q["ng_hi"], 1)

                    def nht_hi(g):
                        for c in range(C):
                            act.wait_ge(q["nht_mm"], g * 3 + c + 1)
                            nc.scalar.copy(NHT[0][:, c, :], bank[4 + c][:, :]).then_inc(q["nht_hi"], 1)

                    def wm_take(g, ts):
                        act.wait_ge(h_stored, g * 16)
                        for t in ts:
                            act.wait_ge(q["wm_mm"], g * T + t + 1)
                            nc.scalar.copy(y_sb[:, t, :], bank[(7, 4, 5, 6)[t]][:, 0:WM]).then_inc(q["wm_taken"], 1)

                    def z_exp(g):
                        act.wait_ge(q["wm_taken"], g * T + T)
                        nc.scalar.activation(sm(EXP_Z), y_sb[:, :, D], ACT.Exp, bias=brn[:, :], scale=-1.0).then_inc(q["z_exp"], 1)

                    def k_take(g, cs):
                        for c in cs:
                            act.wait_ge(q["k_mm"], g * 3 + c + 1)
                            nc.scalar.activation(kT[:, c * GT:(c + 1) * GT], bank[(7, 4, 5)[c]][:, :], ACT.Identity,
                                                 bias=bkT[:, c:c + 1]).then_inc(q["k_taken"], 1)

                    def v_take(g, ts):
                        for t in ts:
                            act.wait_ge(q["v_mm"], g * T + t + 1)
                            nc.scalar.copy(v_sb[:, t, :], bank[(7, 4, 5, 7)[t]][:, 0:D]).then_inc(q["v_taken"], 1)

                    def sel_take(g):
                        act.wait_ge(q["sel_mm"], g + 1)
                        nc.scalar.copy(sel_sb[:, :, :, :], bank[7][:, 0:C * T * SELW].rearrange("p (c t k) -> p c t k", c=C, t=T))\
                            .then_inc(q["sel_taken"], 1)

                    def exp_logits(g):
                        act.wait_ge(q["lg_taken"], g + 1)
                        nc.scalar.activation(prob, prob, ACT.Exp).then_inc(q["lgexp"], 1)

                    def pt_take(g):
                        act.wait_ge(q["pt_mm"], g + 1)
                        pt = bank[6][:, 0:T * H * K].rearrange("p (t c k) -> p c t k", t=T, c=C)
                        for i in range(2):
                            nc.scalar.copy(p_blk[parts(i), :, :, i, :], pt[parts(i), :, :, :]).then_inc(q["pt_taken"], 1)

                    def st_take(g):
                        act.wait_ge(q["st_mm"], g + 1)
                        nc.scalar.copy(scatT, bank[6][0:RR, :].rearrange("p (t n) -> p t n", t=T)).then_inc(q["st_taken"], 1)

                    def pv_take(g):
                        for n in (0,):
                            act.wait_ge(q["pv_mm"], g * 2 + n + 1)
                            pv = bank[(7, 4)[n]][:, 0:C * 4 * HC * K].rearrange("p (c b h k) -> p c b h k", c=C, b=4, h=HC)
                            for h in range(HC):
                                r = slice(h * DH, (h + 1) * DH)
                                dst = ctxT[r, :, n * 4 * K:(n + 1) * 4 * K].rearrange("p c (b k) -> p c b k", b=4)
                                ins = nc.scalar.copy(dst, pv[r, :, :, h, :])
                            ins.then_inc(q["pv_taken"], 1)

                    def both(a, b, nxt):
                        if a is not None:
                            t_take(a)
                        if b is not None:
                            nht_hi(b)
                        if a is not None:
                            exp_prior(a)
                        if b is not None:
                            wm_take(b, (0, 1, 2))
                        if a is not None:
                            exp_att(a)
                        if b is not None:
                            wm_take(b, (3,))
                            z_exp(b)
                            k_take(b, (0, 1))
                        if a is not None:
                            exp_product(a)
                        if b is not None:
                            k_take(b, (2,))
                            v_take(b, (0,))
                        if a is not None:
                            fn_take(a)
                        if b is not None:
                            v_take(b, (1,))
                        if a is not None:
                            y_hi(a)
                        if b is not None:
                            v_take(b, (2,))
                        if a is not None:
                            g_take(a, (0,))
                        if b is not None:
                            sel_take(b)
                        if a is not None:
                            g_take(a, (1, 2, 3))
                        if b is not None:
                            exp_logits(b)
                        if a is not None:
                            ng_hi(a, range(C))
                        if b is not None:
                            v_take(b, (3,))
                            pt_take(b)
                            pv_take(b)
                            st_take(b)
                        if nxt is not None:
                            xt_take(nxt)

                    def w1_high():
                        act.wait_ge(q["w1_loaded"], 80)
                        for c in range(C):
                            nc.scalar.activation(W1S[0][:, c, :], w1_raw[:, c, :], ACT.Copy, scale=g2c[:, c:c + 1])\
                                .then_inc(q["w1_hi"], 1)

                    def w2_high(half):
                        act.wait_ge(q[f"w2_loaded{half}"], 16)
                        for m in range(half * FC // 2, (half + 1) * FC // 2):
                            nc.scalar.copy(W2S[0][:, m, :], w2_raw[:, m, :]).then_inc(q["w2_hi"], 1)

                    def closing(b):
                        nht_hi(b)
                        wm_take(b, range(T))
                        z_exp(b)
                        k_take(b, range(C))
                        w1_high()
                        v_take(b, range(3))
                        sel_take(b)
                        w2_high(0)
                        w2_high(1)
                        exp_logits(b)
                        v_take(b, (3,))
                        pt_take(b)
                        pv_take(b)
                        st_take(b)

                    def high(pair, mm, hi, at):
                        act.wait_ge(q[mm], 1)
                        for c in range(C):
                            nc.scalar.copy(pair[0][:, c, :], bank[at + c][:, 0:D]).then_inc(q[hi], 1)

                    def kvm_high(n):
                        wide, pair = (("wk", WK), ("wv", WV), ("wm", WMR))[n]
                        for c in range(C):
                            nc.scalar.activation(pair[0][:, c, 0:D], raw[wide][:, c, :], ACT.Copy, scale=col["g1"][:, c:c + 1])\
                                .then_inc(q["kvm_hi"], 1)

                    def opening():
                        for dst, src in gnn_small_loads:
                            act.dma_start(dst, src, allow_slow_non_contiguous=True).then_inc(q["gnn_small_loaded"], 16)
                        high(WA, "wa_mm", "wa_hi", 0)
                        high(W3T, "w3_mm", "w3_hi", 3)
                        high(W4T, "w4_mm", "w4_hi", 0)
                        for c in range(C):
                            nc.scalar.copy(w4t[:, c, :], bank[c][:, 0:D]).then_inc(q["w4t_taken"], 1)
                        act.wait_ge(q["gb_mm"], 1)
                        xt_take(0)
                        act.wait_ge(q["small_loaded"], SMALL)
                        act.wait_ge(q["kvm_loaded"], 48)
                        kvm_high(0)
                        t_take(0)
                        exp_prior(0)
                        kvm_high(1)
                        exp_att(0)
                        kvm_high(2)
                        exp_product(0)
                        fn_take(0)
                        y_hi(0)
                        g_take(0, range(T))
                        ng_hi(0, range(C))
                        xt_take(1)

                    over_groups(act, opening, both, closing)

                @block.vector
                def _(dve):
                    nc.vector.memset(mhalf[:, :], -0.5).then_inc(q["mhalf_set"], 1)
                    for part in WMR:
                        nc.vector.memset(part[:, :, D + 1:WM].bitcast(F32), 0.0)
                    nc.vector.memset(ones, 1.0).then_inc(q["ones_set"], 1)
                    nc.vector.memset(b1_rows, 0.0).then_inc(q["ones_set"], 1)
                    nc.vector.memset(POOL[0][:, :, :].bitcast(F32), 0.0).then_inc(q["zeroed"], 1)
                    nc.vector.memset(POOL[1][:, :, :].bitcast(F32), 0.0).then_inc(q["zeroed"], 1)
                    dve.wait_ge(q["zeroed"], 2)
                    count = {}

                    def stepper(name, g, per, first):
                        if first:
                            count[name] = 0

                        def step(ins):
                            count[name] += 1
                            ins.then_inc(q[name], 1)
                            dve.wait_ge(q[name], g * per + count[name])
                        return step

                    def wide(a):
                        return a.unsqueeze(2).to_broadcast([a.shape[0], T, L])

                    def stat(src, into, step, ts=range(T)):
                        for t in ts:
                            ins = nc.vector.bn_stats(stats[:, t, :], src[:, t, 0:D])
                        step(ins)
                        nc.vector.tensor_copy(order[:, :], stats[:, 0, 0:1])
                        for t in range(T):
                            ins = nc.vector.bn_aggr(into[:, t, :], stats[:, t, :])
                        step(ins)

                    def x_stats(g):
                        step = stepper("norm_step", g, NORM_STEPS, True)
                        dve.wait_ge(q["x_loaded"], g * 16 + 16)
                        stat(x_in, mv, step)
                        nc.vector.tensor_scalar(sm(X_VAR), mv[:, :, 1], EPS, None, ALU.add).then_inc(q["var_ready"], 1)

                    def x_rows(g):
                        dve.wait_ge(q["rstd_ready"], g + 1)
                        dve.wait_ge(q["y_mm"], g * 3)
                        for t in range(T):
                            nc.vector.tensor_scalar(xn[:, t, :], x_in[:, t, :], mv[:, t, 0:1], small[:, X_RSTD, t:t + 1],
                                                    ALU.subtract, ALU.mult).then_inc(q["xn_ready"], 1)

                    def shared_logit(g):
                        step = stepper("norm_step", g, NORM_STEPS, False)
                        dve.wait_ge(q["xn_ready"], g * T + T)
                        for t in range(T):
                            step(nc.vector.tensor_tensor_reduce(out=junk, in0=xn[:, t, :], in1=u_bc[:, :], scale=1.0,
                                                                scalar=0.0, op0=ALU.mult, op1=ALU.add,
                                                                accum_out=small[:, ROW_U, t:t + 1]))
                        step(nc.vector.tensor_scalar(sm(SHARED), sm(ROW_U), beta[:, 0:1], None, ALU.add))
                        assert count["norm_step"] == NORM_STEPS, count

                    def masks(g):
                        step = stepper("norm_step", g, NORM_STEPS, False)
                        dve.wait_ge(q["adj_loaded"], g * 16 + 16)
                        nc.vector.tensor_scalar(keep[:, 0, :, :], adj_in[:, :, :], 0, None, ALU.not_equal)
                        nc.vector.tensor_scalar(keep[:, 1, :, :], adj_in[:, :, :], 1, None, ALU.not_equal)
                        nc.vector.tensor_scalar(neg[:, 0, :, :], adj_in[:, :, :], 0, NEG, ALU.is_equal, ALU.mult)
                        step(nc.vector.tensor_scalar(neg[:, 1, :, :], adj_in[:, :, :], 1, NEG, ALU.is_equal, ALU.mult))
                        nc.vector.scalar_tensor_tensor(out=prior[:, :, :], in0=adj_in[:, :, :], scalar=6.0, in1=neg[:, 0, :, :],
                                                       op0=ALU.mult, op1=ALU.add).then_inc(q["adj_read"], 1)
                        dve.wait_ge(q["adj_read"], g + 1)
                        step(nc.vector.tensor_reduce(sm(ROW_MAX), prior[:, :, :], AX.X, ALU.max))
                        nc.vector.tensor_tensor(prior[:, :, :], prior[:, :, :], wide(sm(ROW_MAX)), ALU.subtract)\
                            .then_inc(q["logits_ready"], 1)

                    def lows(banks, part, hi_sem, lo_sem, g, cs=range(C)):
                        for c in cs:
                            dve.wait_ge(q[hi_sem], g * 3 + c + 1)
                            nc.vector.tensor_tensor(part[1][:, c, :], bank[banks[c]][:, :], part[0][:, c, :], ALU.subtract)\
                                .then_inc(q[lo_sem], 1)

                    def xt_lo(g, cs):
                        for c in cs:
                            dve.wait_ge(q["xt_hi"], g * 3 + c + 1)
                            nc.vector.tensor_tensor(XT[1][:, c, :], xt_f[:, c, :], XT[0][:, c, :], ALU.subtract)\
                                .then_inc(q["xt_lo"], 1)

                    def att_logits(g):
                        step = stepper("gnn_step", g, GNN_STEPS, True)
                        dve.wait_ge(q["att_mm"], g + 1)
                        att = bank[ATT_BANK][:, :].rearrange("p (t m) -> p t m", t=T)
                        for i in range(2):
                            r = parts(i)
                            ins = nc.vector.tensor_tensor(att_v[r, :, :], att[r, :, i * L:(i + 1) * L], wide(sm(SHARED)[r]), ALU.add)
                        step(ins)
                        for i in range(2):
                            ins = nc.vector.scalar_tensor_tensor(out=lg[:, i, :, :], in0=att_v, scalar=1.0 / 28.0,
                                                                 in1=keep[:, i, :, :], op0=ALU.mult, op1=ALU.mult)
                        step(ins)
                        step(nc.vector.tensor_tensor(lg[:, :, :, :], lg[:, :, :, :], neg[:, :, :, :], ALU.add))
                        lgf = lg[:, :, :, :].rearrange("p a t m -> p (a t) m")
                        step(nc.vector.tensor_reduce(small8[:, 0, :], lgf, AX.X, ALU.max))
                        nc.vector.tensor_tensor(lgf, lgf, small8[:, 0, :].unsqueeze(2).to_broadcast([P, 8, L]), ALU.subtract)\
                            .then_inc(q["logits_ready"], 1)

                    def att_product(g):
                        step = stepper("gnn_step", g, GNN_STEPS, False)
                        lgf = lg[:, :, :, :].rearrange("p a t m -> p (a t) m")
                        dve.wait_ge(q["exp_done"], g * 2 + 2)
                        nc.vector.tensor_reduce(sm(PRIOR_SUM), prior[:, :, :], AX.X, ALU.add)
                        step(nc.vector.tensor_reduce(small8[:, 1, :], lgf, AX.X, ALU.add))
                        step(nc.vector.tensor_tensor(sm(PRODUCT_SCALE), sm(PRIOR_SUM), small8[:, 1, 0:4], ALU.mult))
                        nc.vector.reciprocal(sm(OTHERS_SCALE), small8[:, 1, 4:8])
                        step(nc.vector.reciprocal(sm(PRODUCT_SCALE), sm(PRODUCT_SCALE)))
                        step(nc.vector.tensor_tensor(prior[:, :, :], prior[:, :, :], lg[:, 0, :, :], ALU.mult))
                        step(nc.vector.tensor_tensor(prior[:, :, :], prior[:, :, :], wide(sm(PRODUCT_SCALE)), ALU.mult))
                        step(nc.vector.tensor_tensor(prior[:, :, :], prior[:, :, :], keep[:, 0, :, :], ALU.mult))
                        step(nc.vector.tensor_tensor(prior[:, :, :], prior[:, :, :], neg[:, 0, :, :], ALU.add))
                        step(nc.vector.tensor_reduce(sm(ROW_MAX), prior[:, :, :], AX.X, ALU.max))
                        nc.vector.tensor_tensor(prior[:, :, :], prior[:, :, :], wide(sm(ROW_MAX)), ALU.subtract)\
                            .then_inc(q["product_ready"], 1)
                        for i in range(2):
                            r = parts(i)
                            nc.vector.tensor_tensor(Nb[r, :, i * L:(i + 1) * L], lg[r, 1, :, :], wide(sm(OTHERS_SCALE)[r]), ALU.mult)

                    def att_blocks(g):
                        step = stepper("gnn_step", g, GNN_STEPS, False)
                        dve.wait_ge(q["exp2_done"], g + 1)
                        step(nc.vector.tensor_reduce(sm(F_SCALE), prior[:, :, :], AX.X, ALU.add))
                        step(nc.vector.reciprocal(sm(F_SCALE), sm(F_SCALE)))
                        for i in range(2):
                            r = parts(i)
                            ins = nc.vector.tensor_tensor(Fb[r, :, i * L:(i + 1) * L], prior[r, :, :], wide(sm(F_SCALE)[r]), ALU.mult)
                        ins.then_inc(q["blocks_ready"], 1)

                    def x1_take(g, ts):
                        dve.wait_ge(q["x1_stored"], g * 16)
                        dve.wait_ge(q["g_added"], g * T + T)
                        for t in ts:
                            dve.wait_ge(q["x1_mm"], g * T + t + 1)
                            nc.vector.tensor_tensor(x1[:, t, :], bank[X1_BANK[t]][:, 0:D], xg[:, t, :], ALU.add)\
                                .then_inc(q["x1_taken"], 1)

                    def x1_stats_open(g, t):
                        dve.wait_ge(q["x1_taken"], g * T + t + 1)
                        nc.vector.bn_stats(stats[:, t, :], x1[:, t, :])

                    def x1_stats(g):
                        step = stepper("gnn_step", g, GNN_STEPS, False)
                        dve.wait_ge(q["x1_taken"], g * T + T)
                        stat(x1, mvh, step, range(3, T))
                        step(nc.vector.tensor_scalar(sm(X1_VAR), mvh[:, :, 1], EPS, None, ALU.add))
                        step(nc.vector.reciprocal(sm(HID_VAR), sm(X1_VAR)))
                        step(nc.vector.tensor_tensor(sm(HID_VAR), sm(HID_VAR), mvh[:, :, 1], ALU.mult))
                        nc.vector.tensor_scalar(sm(HID_VAR), sm(HID_VAR), EPS, None, ALU.add).then_inc(q["var1_ready"], 1)
                        assert count["gnn_step"] == GNN_STEPS, count

                    def normalise_twice(g):
                        dve.wait_ge(q["rstd1_ready"], g + 1)
                        nc.vector.tensor_tensor(sm(BOTH_RSTD), sm(X1_RSTD), sm(HID_RSTD), ALU.mult).then_inc(q["both_ready"], 1)
                        dve.wait_ge(q["both_ready"], g + 1)
                        for t in range(T):
                            nc.vector.tensor_scalar(nh[:, t, :], x1[:, t, :], mvh[:, t, 0:1], small[:, BOTH_RSTD, t:t + 1],
                                                    ALU.subtract, ALU.mult).then_inc(q["nh_ready"], 1)
                        for t in range(T):
                            ins = nc.vector.tensor_scalar(hid[:, t, :], x1[:, t, :], mvh[:, t, 0:1], small[:, X1_RSTD, t:t + 1],
                                                          ALU.subtract, ALU.mult)
                        ins.then_inc(q["hid_ready"], 1)

                    def scores(g):
                        step = stepper("attn_step", g, ATTN_STEPS, True)
                        dve.wait_ge(q["z_exp"], g + 1)
                        step(nc.vector.tensor_scalar(sm(SCORE), sm(EXP_Z), 1.0, None, ALU.add))
                        step(nc.vector.reciprocal(sm(SCORE), sm(SCORE)))
                        nc.vector.tensor_tensor(diag, node.unsqueeze(1).to_broadcast([P, T, L]), wide(sm(SCORE)), ALU.mult)\
                            .then_inc(q["score_diag"], 1)

                    def picks(g):
                        step = stepper("attn_step", g, ATTN_STEPS, False)
                        dve.wait_ge(q["bc_mm"], g + 1)
                        nc.vector.tensor_copy(bc[:, :, :], bank[6][:, 0:T * L]).then_inc(q["bc_taken"], 1)
                        dve.wait_ge(q["bc_taken"], g + 1)
                        nc.vector.tensor_reduce(sm(SCORE_SUM), bc[:, :, :], AX.X, ALU.add)
                        step(nc.vector.tensor_tensor(cmp[:, 0, :, :], bc[:, :, :], node.unsqueeze(1).to_broadcast([P, T, L]), ALU.mult))
                        step(nc.vector.tensor_reduce(sm(SCORE), cmp[:, 0, :, :], AX.X, ALU.add))
                        nc.vector.tensor_tensor(cmp[:, 0, :, :], bc[:, :, :], wide(sm(SCORE)), ALU.is_lt)
                        step(nc.vector.tensor_tensor(cmp[:, 1, :, :], bc[:, :, :], wide(sm(SCORE)), ALU.is_equal))
                        step(nc.vector.tensor_tensor(cmp[:, 1, :, :], cmp[:, 1, :, :], earlier.unsqueeze(1).to_broadcast([P, T, L]), ALU.mult))
                        step(nc.vector.tensor_tensor(cmp[:, 0, :, :], cmp[:, 0, :, :], cmp[:, 1, :, :], ALU.add))
                        step(nc.vector.tensor_reduce(sm(RANK), cmp[:, 0, :, :], AX.X, ALU.add))
                        nc.vector.tensor_scalar(sm(UNROUTED), sm(RANK), float(K), None, ALU.is_ge)
                        step(nc.vector.tensor_scalar(sm(INV_SUM), sm(SCORE_SUM), 1e-6, None, ALU.add))
                        step(nc.vector.reciprocal(sm(INV_SUM), sm(INV_SUM)))
                        nc.vector.tensor_tensor(sm(SCORE_SUM), sm(SCORE_SUM), sm(INV_SUM), ALU.mult)
                        nc.vector.tensor_tensor(sm(PASSED_SCORE), sm(SCORE), sm(UNROUTED), ALU.mult)
                        step(nc.vector.tensor_tensor(sm(WEIGHT), sm(SCORE), sm(INV_SUM), ALU.mult))
                        step(nc.vector.tensor_tensor(sm(PASSED_SUM), sm(PASSED_SCORE), sm(SCORE_SUM), ALU.mult))
                        pair = small[:, PASSED_SCORE:PASSED_SCORE + 2, :]
                        step(nc.vector.tensor_copy(passed[0][:, :, :], pair))
                        step(nc.vector.tensor_tensor(passed[1][:, :, :], pair, passed[0][:, :, :], ALU.subtract))
                        nc.vector.tensor_copy(scat[:, :, ROW_BIAS], sm(UNROUTED))
                        nc.vector.tensor_copy(scat[:, :, ROW_B1], passed[0][:, 1, :])
                        nc.vector.tensor_copy(scat[:, :, ROW_B1_LOW], passed[1][:, 1, :])
                        for i in range(2):
                            r = parts(i)
                            nc.vector.tensor_copy(gath[r, :, 2 * K + i], sm(WEIGHT)[r])
                            for at, part in ((ROW_POOL + i, passed[0]), (ROW_POOL_LOW + i, passed[1])):
                                nc.vector.tensor_copy(scat_gath[r, at:at + (T - 1) * (RR + 2) + 1:RR + 2], part[r, 0, :])
                            rank_b = sm(RANK)[r].unsqueeze(2).to_broadcast([L, T, K])
                            iota_b = iota[r].unsqueeze(1).to_broadcast([L, T, K])
                            nc.vector.tensor_tensor(gath[r, :, i * K:(i + 1) * K], iota_b, rank_b, ALU.is_equal)
                            own = scat_gath[r, i * K:i * K + T * SKEW].rearrange("p (t s) -> p t s", t=T)[:, :, 0:K]
                            ins = nc.vector.tensor_tensor(own, iota_b, rank_b, ALU.is_equal)
                        ins.then_inc(q["picks_ready"], 1)
                        assert count["attn_step"] == ATTN_STEPS - 3, count

                    def unrouted(g):
                        dve.wait_ge(q["picks_ready"], g + 1)
                        dve.wait_ge(q["hid_ready"], g + 1)
                        for t in range(T):
                            nc.vector.scalar_tensor_tensor(out=y_sb[:, t, 0:D], in0=y_sb[:, t, 0:D], scalar=small[:, UNROUTED, t:t + 1],
                                                           in1=hid[:, t, :], op0=ALU.mult, op1=ALU.add).then_inc(q["y_ready"], 1)

                    def pooled(g):
                        dve.wait_ge(q["sel_taken"], g + 1)
                        sel = sel_sb[:, :, :, 2 * K:SELW]

                        def cols_of(part, at):
                            return POOL[part][:, :, at:at + GB].rearrange("p c (t k) -> p c t k", t=T)

                        for at in (ROW_POOL, ROW_POOL_LOW):
                            nc.vector.tensor_copy(cols_of(0, at), sel).then_inc(q["pool_hi"], 1)
                        dve.wait_ge(q["pool_hi"], 2 * g + 2)
                        for at in (ROW_POOL, ROW_POOL_LOW):
                            nc.vector.tensor_tensor(cols_of(1, at), sel, cols_of(0, at), ALU.subtract).then_inc(q["pool_lo"], 1)

                    def queries(g):
                        dve.wait_ge(q["q_mm"], g + 1)
                        qp = bank[4][:, 0:C * GB * K].rearrange("p (c b k) -> p b c k", c=C, b=GB)
                        blk = q_blk[:, :, :, :, :, :].rearrange("p b c a h k -> p b (c a) h k")
                        for h in range(HC):
                            r = slice(h * DH, (h + 1) * DH)
                            ins = nc.vector.tensor_tensor(blk[r, :, 0:C * C:C + 1, h, :], qp[r, :, :, :],
                                                          bqT[r, :].unsqueeze(1).unsqueeze(3).to_broadcast([DH, GB, C, K]), ALU.add)
                        ins.then_inc(q["q_taken"], 1)

                    mx = small8[0:H * K, 2, :]

                    def logits(g):
                        step = stepper("attn_step", g, ATTN_STEPS, False)
                        dve.wait_ge(q["lg_mm"], g + 1)
                        lgp = bank[5][0:H * K, :].rearrange("p (b m) -> p b m", b=GB)
                        step(nc.vector.tensor_reduce(mx, lgp, AX.X, ALU.max))
                        nc.vector.tensor_tensor(prob, lgp, mx.unsqueeze(2).to_broadcast([H * K, GB, L]), ALU.subtract)\
                            .then_inc(q["lg_taken"], 1)

                    def probabilities(g):
                        step = stepper("attn_step", g, ATTN_STEPS, False)
                        dve.wait_ge(q["lgexp"], g + 1)
                        step(nc.vector.tensor_reduce(mx, prob, AX.X, ALU.add))
                        step(nc.vector.reciprocal(mx, mx))
                        nc.vector.tensor_tensor(prob, prob, mx.unsqueeze(2).to_broadcast([H * K, GB, L]), ALU.mult)\
                            .then_inc(q["prob_ready"], 1)
                        assert count["attn_step"] == ATTN_STEPS, count

                    def pv_take(g):
                        dve.wait_ge(q["pv_mm"], g * 2 + 2)
                        pv = bank[4][:, 0:C * 4 * HC * K].rearrange("p (c b h k) -> p c b h k", c=C, b=4, h=HC)
                        for h in range(HC):
                            r = slice(h * DH, (h + 1) * DH)
                            dst = ctxT[r, :, 4 * K:8 * K].rearrange("p c (b k) -> p c b k", b=4)
                            ins = nc.vector.tensor_copy(dst, pv[r, :, :, h, :])
                        ins.then_inc(q["pv_taken2"], 1)

                    def row_take(g):
                        dve.wait_ge(q["r_mm"], g + 1)
                        nc.vector.tensor_tensor(r_sb, bank[5][0:RR, 0:D], r_bias[:, :], ALU.add).then_inc(q["r_step"], 1)
                        dve.wait_ge(q["r_step"], 2 * g + 1)
                        nc.vector.tensor_copy(R_PARTS[0], r_sb).then_inc(q["r_step"], 1)
                        dve.wait_ge(q["r_step"], 2 * g + 2)
                        nc.vector.tensor_tensor(R_PARTS[1], r_sb, R_PARTS[0], ALU.subtract).then_inc(q["r_taken"], 1)

                    def merge(g):
                        dve.wait_ge(q["y_ready"], g * T + T)
                        for t in range(T):
                            dve.wait_ge(q["out_mm"], g * T + t + 1)
                            nc.vector.tensor_tensor(y_sb[:, t, 0:D], bank[(7, 4, 5, 6)[t]][:, 0:D], y_sb[:, t, 0:D], ALU.add)\
                                .then_inc(q["h_ready"], 1)

                    def both(a, b, nxt):
                        if b is not None:
                            normalise_twice(b)
                        if b is not None:
                            lows((4, 5, 6), NHT, "nht_hi", "nht_lo", b)
                        if a is not None:
                            att_logits(a)
                            att_product(a)
                        if b is not None:
                            scores(b)
                        if a is not None:
                            att_blocks(a)
                        if b is not None:
                            picks(b)
                        if a is not None:
                            lows((1, 2, 3), XT, "y_hi", "y_lo", a)
                        if b is not None:
                            unrouted(b)
                        if nxt is not None:
                            x_stats(nxt)
                        if b is not None:
                            queries(b)
                            pooled(b)
                        if nxt is not None:
                            x_rows(nxt)
                            masks(nxt)
                        if b is not None:
                            logits(b)
                            probabilities(b)
                        if a is not None:
                            lows((0, 1, 2), TT, "ng_hi", "ng_lo", a)
                        if nxt is not None:
                            shared_logit(nxt)
                        if a is not None:
                            x1_take(a, (0, 1))
                            x1_stats_open(a, 0)
                            x1_stats_open(a, 1)
                        if b is not None:
                            pv_take(b)
                        if a is not None:
                            x1_take(a, (2,))
                            x1_stats_open(a, 2)
                        if b is not None:
                            row_take(b)
                        if nxt is not None:
                            xt_lo(nxt, (0,))
                        if a is not None:
                            x1_take(a, (3,))
                        if nxt is not None:
                            xt_lo(nxt, (1, 2))
                        if a is not None:
                            x1_stats(a)
                        if b is not None:
                            merge(b)

                    def w1_low():
                        for c in range(C):
                            dve.wait_ge(q["w1_hi"], c + 1)
                            nc.vector.scalar_tensor_tensor(out=W1S[1][:, c, :], in0=w1_raw[:, c, :], scalar=g2c[:, c:c + 1],
                                                           in1=W1S[0][:, c, :], op0=ALU.mult, op1=ALU.subtract)\
                                .then_inc(q["w1_lo"], 1)

                    def mlp_biases():
                        dve.wait_ge(q["hb_mm"], 2)
                        nc.vector.tensor_tensor(hb[:, :], bank[0][:, 0:FC], bf1c[:, :], ALU.add)
                        nc.vector.tensor_copy(bf2_bc[:, :], bank[1][:, 0:D])

                    def w2_low(half):
                        for m in range(half * FC // 2, (half + 1) * FC // 2):
                            dve.wait_ge(q["w2_hi"], m + 1)
                            nc.vector.tensor_tensor(W2S[1][:, m, :], w2_raw[:, m, :], W2S[0][:, m, :], ALU.subtract)

                    def closing(b):
                        nc.vector.memset(one_row[:, :], 1.0).then_inc(q["one_set"], 1)
                        normalise_twice(b)
                        lows((4, 5, 6), NHT, "nht_hi", "nht_lo", b)
                        scores(b)
                        picks(b)
                        unrouted(b)
                        w1_low()
                        queries(b)
                        pooled(b)
                        w2_low(0)
                        w2_low(1)
                        logits(b)
                        probabilities(b)
                        mlp_biases()
                        normalise(dve, 0)
                        pv_take(b)
                        row_take(b)
                        scale_rows(dve, 0)
                        merge(b)

                    def gnn_rows_spread():
                        dve.wait_ge(q["gnn_small_loaded"], GNN_SMALL)
                        dve.wait_ge(q["ones_set"], 2)
                        for c in range(C):
                            for bc_, v in ((b2_bc, "gb2"), (b3_bc, "gb3")):
                                ins = nc.vector.tensor_scalar(bc_[:, c, :], ones, col[v][:, c:c + 1], None, ALU.mult)
                        ins.then_inc(q["spread_made"], 1)

                    def b1_spread():
                        dve.wait_ge(q["small_loaded"], SMALL)
                        for c in range(C):
                            nc.vector.tensor_scalar(b1_bc[:, c, :], ones, col["b1"][:, c:c + 1], None, ALU.mult)
                            nc.vector.tensor_scalar(b1_rows[:, c, ROW_B1_LOW:ROW_B1_LOW + 1], ones[:, 0:1],
                                                    col["b1"][:, c:c + 1], None, ALU.mult)
                            ins = nc.vector.tensor_scalar(b1_rows[:, c, ROW_BIAS:ROW_B1 + 1], ones[:, 0:2],
                                                          col["b1"][:, c:c + 1], None, ALU.mult)
                        ins.then_inc(q["b1_spread"], 1)

                    def low(pair, hi, lo, at):
                        dve.wait_ge(q[hi], C)
                        for c in range(C):
                            nc.vector.tensor_tensor(pair[1][:, c, :], bank[at + c][:, 0:D], pair[0][:, c, :], ALU.subtract)\
                                .then_inc(q[lo], 1)

                    def kvm_low(n):
                        wide, (hi, lo) = (("wk", WK), ("wv", WV), ("wm", WMR))[n]
                        for c in range(C):
                            dve.wait_ge(q["kvm_hi"], n * C + c + 1)
                            nc.vector.scalar_tensor_tensor(out=lo[:, c, 0:D], in0=raw[wide][:, c, :], scalar=col["g1"][:, c:c + 1],
                                                           in1=hi[:, c, 0:D], op0=ALU.mult, op1=ALU.subtract)\
                                .then_inc(q["kvm_lo"], 1)

                    def router_column():
                        dve.wait_ge(q["br_mm"], 1)
                        nc.vector.tensor_tensor(WMR[0][:, :, D], col["wr"], col["g1"], ALU.mult).then_inc(q["wr_step"], 1)
                        nc.vector.tensor_tensor(col["wr"], col["wr"], col["g1"], ALU.mult).then_inc(q["wr_step"], 1)
                        dve.wait_ge(q["wr_step"], 2)
                        nc.vector.tensor_tensor(WMR[1][:, :, D], col["wr"], WMR[0][:, :, D], ALU.subtract).then_inc(q["wr_step"], 1)

                    v = bank[7]

                    def key_and_value_bias():
                        dve.wait_ge(q["kv_mm"], 1)
                        nc.vector.tensor_tensor(bkT[:, :], v[:, 8:8 + C], col["bk"], ALU.add)
                        nc.vector.tensor_scalar(brn[:, :], v[:, 20:21], -1.0, None, ALU.mult)
                        nc.vector.tensor_tensor(bvT, v[:, 12:12 + C], col["bv"], ALU.add).then_inc(q["b_step"], 1)
                        dve.wait_ge(q["b_step"], 1)
                        for c in range(C):
                            ins = nc.vector.tensor_scalar(bv_rows[:, c, :], picked, bvT[:, c:c + 1], None, ALU.mult)
                        ins.then_inc(q["placed"], 1)

                    def query_weights():
                        dve.wait_ge(q["bq_mm"], 1)
                        nc.vector.tensor_tensor(bqT[:, :], bank[6][:, 16:16 + C], col["bq"], ALU.add).then_inc(q["b_step"], 1)
                        for c in range(C):
                            nc.vector.tensor_scalar(WQ[:, c, :], WQ[:, c, :], col["g1"][:, c:c + 1], float(DH) ** -0.5,
                                                    ALU.mult, ALU.mult).then_inc(q["b_step"], 1)
                        dve.wait_ge(q["b_step"], 3)
                        nc.vector.tensor_scalar(bqT[:, :], bqT[:, :], float(DH) ** -0.5, None, ALU.mult).then_inc(q["b_step"], 1)

                    def opening():
                        gnn_rows_spread()
                        x_stats(0)
                        x_rows(0)
                        low(WA, "wa_hi", "wa_lo", 0)
                        low(W3T, "w3_hi", "w3_lo", 3)
                        dve.wait_ge(q["w4t_taken"], C)
                        low(W4T, "w4_hi", "w4_lo", 0)
                        dve.wait_ge(q["c_mm"], 1)
                        nc.vector.tensor_copy(cT[:, :], v[:, 0:C]).then_inc(q["c_taken"], 1)
                        nc.vector.tensor_copy(beta[:, :], v[:, 4:5]).then_inc(q["c_taken"], 1)
                        dve.wait_ge(q["u_mm"], 1)
                        nc.vector.tensor_copy(u_bc[:, :], bank[6][:, 0:D]).then_inc(q["c_taken"], 1)
                        dve.wait_ge(q["gb_mm"], 1)
                        nc.vector.tensor_copy(g_bias[:, :], bank[5][:, 0:D]).then_inc(q["gb_taken"], 1)
                        xt_lo(0, range(C))
                        masks(0)
                        dve.wait_ge(q["c_taken"], 3)
                        shared_logit(0)
                        b1_spread()
                        att_logits(0)
                        dve.wait_ge(q["zeroed_pool"], 2)
                        att_product(0)
                        key_and_value_bias()
                        att_blocks(0)
                        kvm_low(0)
                        kvm_low(1)
                        kvm_low(2)
                        lows((1, 2, 3), XT, "y_hi", "y_lo", 0)
                        router_column()
                        x_stats(1)
                        masks(1)
                        x_rows(1)
                        dve.wait_ge(q["rb_mm"], 1)
                        nc.vector.tensor_copy(r_bias[:, :], bank[4][0:RR, 0:D]).then_inc(q["b_step"], 1)
                        lows((0, 1, 2), TT, "ng_hi", "ng_lo", 0)
                        query_weights()
                        x1_take(0, (0, 1))
                        x1_stats_open(0, 0)
                        x1_stats_open(0, 1)
                        x1_take(0, (2,))
                        x1_stats_open(0, 2)
                        xt_lo(1, (0,))
                        x1_take(0, (3,))
                        xt_lo(1, (1, 2))
                        x1_stats(0)
                        shared_logit(1)

                    over_groups(dve, opening, both, closing)

                @block.tensor
                def _(pe):
                    def split(out, lhs, rhs, low=None, g=None):
                        for c in range(C):
                            if low:
                                pe.wait_ge(q[low], g * 3 + c + 1)
                            for i, (a, b) in enumerate(PRODUCTS):
                                mm = nc.tensor.matmul(out, lhs[a][c], rhs[b][c], start=(c == 0 and i == 0),
                                                      stop=(c == C - 1 and i == 2))
                        return mm

                    def cut(pair, at):
                        return [[pair[a][:, c, at] for c in range(C)] for a in range(2)]

                    every = slice(0, GT)
                    rows = slice(0, D)

                    def tile(t):
                        return slice(t * P, (t + 1) * P)

                    def xt(g, first=False):
                        if not first:
                            pe.wait_ge(q["x1_taken"], (g - 1) * T + 3)
                        pe.wait_ge(q["xn_ready"], g * T + T)
                        for c in range(C):
                            for t in range(T):
                                mm = nc.tensor.transpose(bank[XT_BANK[c]][:, tile(t)], xn[:, t, tile(c)], ident)
                            mm.then_inc(q["xt_mm"], 1)

                    def queries_t(g):
                        for m in range(C):
                            pe.wait_ge(q["xt_taken"], g * 3 + m + 1)
                            if m == 2:
                                pe.wait_ge(q["x1_taken"], g * T)
                            split(bank[T_BANK[m]][:, :], cut(WA, tile(m)), cut(XT, every), "xt_lo" if m == 0 else None, g).then_inc(q["t_mm"], 1)

                    def att(g):
                        pe.wait_ge(q["t_taken"], g * 3 + 3)
                        pe.wait_ge(q["xt_taken"], g * 3 + 3)
                        for t in range(T):
                            for c in range(C):
                                mm = nc.tensor.matmul(bank[ATT_BANK][:, tile(t)], t_f[:, c, tile(t)], xt_f[:, c, tile(t)],
                                                      start=(c == 0), stop=(c == C - 1))
                        mm.then_inc(q["att_mm"], 1)

                    def fn_t(g):
                        pe.wait_ge(q["blocks_ready"], g + 1)
                        for src, b in ((Fb, 3), (Nb, 0)):
                            for t in range(T):
                                mm = nc.tensor.transpose(bank[b][:, tile(t)], src[:, t, :], ident)
                            mm.then_inc(q["fn_mm"], 1)

                    def fx(g):
                        pe.wait_ge(q["fn_taken"], g * 2 + 1)
                        for c in range(C):
                            for t in range(T):
                                mm = nc.tensor.matmul(bank[1 + c][:, tile(t)], xn[:, t, tile(c)], FT[:, t, :], start=True, stop=True)
                            mm.then_inc(q["y_mm"], 1)

                    def first_g(g, ts):
                        pe.wait_ge(q["fn_taken"], g * 2 + 2)
                        for t in ts:
                            split(bank[t][:, 0:D], cut(XT, tile(t)), cut(W3T, rows), "y_lo" if t == 0 else None, g).then_inc(q["g_mm"], 1)

                    def ng(g, cs):
                        pe.wait_ge(q["g_taken"], g * T + T)
                        for c in cs:
                            for t in range(T):
                                mm = nc.tensor.matmul(bank[c][:, tile(t)], g_sb[:, t, tile(c)], NT[:, t, :], start=True, stop=True)
                            mm.then_inc(q["ng_mm"], 1)

                    def second_g(g, ts):
                        for t in ts:
                            split(bank[X1_BANK[t]][:, 0:D], cut(TT, tile(t)), cut(W4T, rows), "ng_lo" if t == 0 else None, g).then_inc(q["x1_mm"], 1)

                    def nht(g):
                        pe.wait_ge(q["h_ready"], g * T)
                        for c in range(C):
                            for t in range(T):
                                if c == 0:
                                    pe.wait_ge(q["nh_ready"], g * T + t + 1)
                                mm = nc.tensor.transpose(bank[4 + c][:, tile(t)], nh[:, t, tile(c)], ident)
                            mm.then_inc(q["nht_mm"], 1)

                    def mixed(g, ts):
                        for t in ts:
                            split(bank[(7, 4, 5, 6)[t]][:, 0:WM], cut(NHT, tile(t)), cut(WMR, slice(0, WM)),
                                  "nht_lo" if t == 0 else None, g).then_inc(q["wm_mm"], 1)

                    def keys(g):
                        for m in range(C):
                            pe.wait_ge(q["wm_taken"], g * T + m + 1)
                            split(bank[(7, 4, 5)[m]][:, :], cut(WK, tile(m)), cut(NHT, every)).then_inc(q["k_mm"], 1)

                    def spread(g):
                        pe.wait_ge(q["wm_taken"], g * T + 4)
                        pe.wait_ge(q["score_diag"], g + 1)
                        nc.tensor.matmul(bank[6][:, 0:T * L], same, diag, start=True, stop=True).then_inc(q["bc_mm"], 1)

                    def values(g, ts):
                        for t in ts:
                            if t < 3:
                                pe.wait_ge(q["k_taken"], g * 3 + t + 1)
                            else:
                                pe.wait_ge(q["sel_taken"], g + 1)
                            split(bank[(7, 4, 5, 7)[t]][:, 0:D], cut(NHT, tile(t)), cut(WV, rows)).then_inc(q["v_mm"], 1)

                    def gather(g):
                        pe.wait_ge(q["v_taken"], g * T + 1)
                        pe.wait_ge(q["picks_ready"], g + 1)
                        for c in range(C):
                            for t in range(T):
                                at = (c * T + t) * SELW
                                mm = nc.tensor.matmul(bank[7][:, at:at + SELW], nh[:, t, tile(c)], gath[:, t, :], start=True, stop=True)
                        mm.then_inc(q["sel_mm"], 1)

                    def picked_queries(g):
                        pe.wait_ge(q["v_taken"], g * T + 3)
                        pe.wait_ge(q["sel_taken"], g + 1)
                        for m in range(C):
                            for c in range(C):
                                mm = nc.tensor.matmul(bank[4][:, m * GB * K:(m + 1) * GB * K], WQ[:, c, tile(m)],
                                                      sel_sb[:, c, :, 0:2 * K], start=(c == 0), stop=(c == C - 1))
                        mm.then_inc(q["q_mm"], 1)

                    def attn_logits(g):
                        pe.wait_ge(q["q_taken"], g + 1)
                        for b in range(GB):
                            for c in range(C):
                                at = c * GT + b * L
                                mm = nc.tensor.matmul(bank[5][0:H * K, b * L:(b + 1) * L], q_blk[:, b, c, :, :, :].rearrange("p a h k -> p (a h k)"),
                                                      kT[:, at:at + L], start=(c == 0), stop=(c == C - 1))
                        mm.then_inc(q["lg_mm"], 1)

                    def prob_t(g):
                        pe.wait_ge(q["prob_ready"], g + 1)
                        pe.wait_ge(q["bc_taken"], g + 1)
                        for t in range(T):
                            mm = nc.tensor.transpose(bank[6][:, t * H * K:(t + 1) * H * K],
                                                     kT[0:H * K, tile(t)], ident[0:H * K, 0:H * K])
                        mm.then_inc(q["pt_mm"], 1)

                    def contexts(g):
                        pe.wait_ge(q["v_taken"], g * T + 4)
                        pe.wait_ge(q["pt_taken"], g * 2 + 2)
                        for n in range(2):
                            for c in range(C):
                                for t in range(2):
                                    at = (c * 2 + t) * 2 * HC * K
                                    mm = nc.tensor.matmul(bank[(7, 4)[n]][:, at:at + 2 * HC * K], v_sb[:, 2 * n + t, tile(c)],
                                                          p_blk[:, c, 2 * n + t, :, :].rearrange("p b k -> p (b k)"), start=True, stop=True)
                            mm.then_inc(q["pv_mm"], 1)

                    def scatter_t(g):
                        for t in range(T):
                            mm = nc.tensor.transpose(bank[6][0:RR, tile(t)], scat[:, t, :], ident)
                        mm.then_inc(q["st_mm"], 1)

                    def pooled_rows(g):
                        pe.wait_ge(q["pool_lo"], 2 * g + 2)
                        pe.wait_ge(q["lg_taken"], g + 1)
                        for c in range(C):
                            for i, (a, b) in enumerate(PRODUCTS):
                                nc.tensor.matmul(bank[5][0:RR, 0:D], POOL[a][:, c, :], WMR[b][:, c, 0:D],
                                                 start=(c == 0 and i == 0), stop=False, skip_group_check=True)

                    def context_rows(g):
                        pe.wait_ge(q["pv_taken"], g + 1)
                        pe.wait_ge(q["pv_taken2"], g + 1)
                        for c in range(C):
                            mm = nc.tensor.matmul(bank[5][0:GB * K, 0:D], ctxT[:, c, :], WO[:, c, :], start=False,
                                                  stop=(c == C - 1), skip_group_check=True)
                        mm.then_inc(q["r_mm"], 1)

                    def scatter(g):
                        pe.wait_ge(q["r_taken"], g + 1)
                        pe.wait_ge(q["st_taken"], g + 1)
                        for t in range(T):
                            out_t = bank[(7, 4, 5, 6)[t]][:, 0:D]
                            nc.tensor.matmul(out_t, scatT[:, t, :], R_PARTS[0], start=True, stop=False)
                            nc.tensor.matmul(out_t, scatT[:, t, :], R_PARTS[1], start=False, stop=True).then_inc(q["out_mm"], 1)

                    def both(a, b, nxt):
                        if a is not None:
                            queries_t(a)
                        if b is not None:
                            nht(b)
                        if a is not None:
                            att(a)
                        if b is not None:
                            mixed(b, range(T))
                            keys(b)
                            spread(b)
                            values(b, (0,))
                        if a is not None:
                            fn_t(a)
                        if b is not None:
                            values(b, (1,))
                        if a is not None:
                            fx(a)
                        if b is not None:
                            values(b, (2,))
                        if a is not None:
                            first_g(a, (0,))
                        if b is not None:
                            gather(b)
                        if a is not None:
                            first_g(a, (1,))
                        if b is not None:
                            picked_queries(b)
                        if a is not None:
                            first_g(a, (2, 3))
                        if b is not None:
                            attn_logits(b)
                        if a is not None:
                            ng(a, range(C))
                        if b is not None:
                            pooled_rows(b)
                            prob_t(b)
                            values(b, (3,))
                        if a is not None:
                            second_g(a, (0, 1))
                        if b is not None:
                            contexts(b)
                            scatter_t(b)
                        if a is not None:
                            second_g(a, (2,))
                        if b is not None:
                            context_rows(b)
                        if nxt is not None:
                            xt(nxt)
                        if a is not None:
                            second_g(a, (3,))
                        if b is not None:
                            scatter(b)

                    def mlp_bias(ms):
                        pe.wait_ge(q["w1_loaded"], 80)
                        pe.wait_ge(q["one_set"], 1)
                        if 0 in ms:
                            nc.tensor.matmul(bank[1][:, 0:D], one_row[:, :], bf2r[:, :], start=True, stop=True)
                        for m in ms:
                            for c in range(C):
                                mm = nc.tensor.matmul(bank[0][:, m:m + 1], w1_raw[:, c, tile(m)], b2c[:, c:c + 1],
                                                      start=(c == 0), stop=(c == C - 1))
                        mm.then_inc(q["hb_mm"], 1)

                    def closing(b):
                        nht(b)
                        mixed(b, range(T))
                        keys(b)
                        spread(b)
                        mlp_bias(range(0, 4))
                        values(b, range(3))
                        mlp_bias(range(4, FC))
                        gather(b)
                        picked_queries(b)
                        attn_logits(b)
                        pooled_rows(b)
                        values(b, (3,))
                        prob_t(b)
                        contexts(b)
                        scatter_t(b)
                        context_rows(b)
                        scatter(b)

                    v = bank[7]

                    def by_feature(at, lhsT, rhs, into=v):
                        for m in range(C):
                            for c in range(C):
                                mm = nc.tensor.matmul(into[:, at + m:at + m + 1], lhsT[:, c, tile(m)], rhs[:, c:c + 1],
                                                      start=(c == 0), stop=(c == C - 1))
                        return mm

                    def turned(name, at):
                        for m in range(C):
                            for c in range(C):
                                mm = nc.tensor.transpose(bank[at + m][:, tile(c)], gnn_raw[name][:, c, tile(m)], ident)
                        return mm

                    def opening():
                        pe.wait_ge(q["w12_loaded"], 32)
                        for m in range(C):
                            for c in range(C):
                                mm = nc.tensor.matmul(bank[m][:, 0:D], gnn_raw["w1"][:, c, tile(m)], gnn_raw["w2"][:, c, :],
                                                      start=(c == 0), stop=(c == C - 1))
                        mm.then_inc(q["wa_mm"], 1)
                        pe.wait_ge(q["gnn_small_loaded"], GNN_SMALL)
                        pe.wait_ge(q["spread_made"], 1)
                        for c in range(C):
                            mm = nc.tensor.matmul(bank[6][:, 0:D], b2_bc[:, c, :], gnn_raw["w1"][:, c, :],
                                                  start=(c == 0), stop=(c == C - 1))
                        mm.then_inc(q["u_mm"], 1)
                        pe.wait_ge(q["w34_loaded"], 32)
                        turned("w3", 3).then_inc(q["w3_mm"], 1)
                        by_feature(0, gnn_raw["w2"], col["gb1"])
                        pe.wait_ge(q["wa_lo"], C)
                        turned("w4", 0).then_inc(q["w4_mm"], 1)
                        for c in range(C):
                            mm = nc.tensor.matmul(v[:, 4:5], b2_bc[:, c, :], col["gb1"][:, c:c + 1], start=(c == 0), stop=(c == C - 1))
                        mm.then_inc(q["c_mm"], 1)
                        pe.wait_ge(q["w3_lo"], C)
                        pe.wait_ge(q["w4t_taken"], C)
                        for c in range(C):
                            nc.tensor.matmul(bank[5][:, 0:D], b3_bc[:, c, :], w4t[:, c, :], start=(c == 0), stop=False)
                        nc.tensor.matmul(bank[5][:, 0:D], ones[0:1, :], gnn_rows[0:1, 0, :], start=False, stop=False)
                        nc.tensor.matmul(bank[5][:, 0:D], ones[0:1, :], gnn_rows[0:1, 1, :], start=False, stop=True)\
                            .then_inc(q["gb_mm"], 1)
                        pe.wait_ge(q["w4_lo"], C)
                        xt(0, first=True)
                        pe.wait_ge(q["kvm_loaded"], 48)
                        pe.wait_ge(q["small_loaded"], SMALL)
                        pe.wait_ge(q["c_taken"], 2)
                        by_feature(8, raw["wk"], col["b1"])
                        queries_t(0)
                        pe.wait_ge(q["b1_spread"], 1)
                        for c in range(C):
                            nc.tensor.matmul(v[:, 20:21], b1_bc[:, c, :], col["wr"][:, c:c + 1], start=(c == 0), stop=False)
                        nc.tensor.matmul(v[:, 20:21], ones[0:1, :], br_one, start=False, stop=True).then_inc(q["br_mm"], 1)
                        att(0)
                        by_feature(12, raw["wv"], col["b1"]).then_inc(q["kv_mm"], 1)
                        for c in range(C):
                            nc.tensor.matmul(bank[4][0:RR, 0:D], b1_rows[:, c, :], raw["wm"][:, c, :], start=(c == 0), stop=False)
                        nc.tensor.matmul(bank[4][0:RR, 0:D], picked[0:1, :], bo_row, start=False, stop=False)
                        nc.tensor.matmul(bank[4][0:RR, 0:D], biasrow[0:1, :], bm_row, start=False, stop=False)
                        pe.wait_ge(q["c_taken"], 3)
                        pe.wait_ge(q["qo_loaded"], 32)
                        by_feature(16, WQ, col["b1"], bank[6]).then_inc(q["bq_mm"], 1)
                        pe.wait_ge(q["placed"], 1)
                        for c in range(C):
                            mm = nc.tensor.matmul(bank[4][0:RR, 0:D], bv_rows[:, c, :], WO[:, c, :], start=False, stop=(c == C - 1))
                        mm.then_inc(q["rb_mm"], 1)
                        fn_t(0)
                        fx(0)
                        first_g(0, range(T))
                        ng(0, range(C))
                        second_g(0, (0, 1, 2))
                        xt(1)
                        second_g(0, (3,))
                        pe.wait_ge(q["kvm_lo"], 3 * C)
                        pe.wait_ge(q["wr_step"], 3)
                        pe.wait_ge(q["b_step"], 7)
                        pe.wait_ge(q["zeroed"], 2)

                    over_groups(pe, opening, both, closing)
        w_stage.close()

        HID = [sb(f"hid{i}", [P, R3, GT], F32R) for i in range(2)]
        TB = (6, 7, 6)

        def over_groups(eng, group):
            group(0, False)
            with eng.Fori(1, G - 1) as g:
                group(g, False)
            group(G - 1, True)

        with nc.Block() as block:
            @block.sync
            def _(sp):
                def load(g):
                    sp.wait_ge(mlp["n2_ready"], g)
                    sp.wait_ge(mlp["res_ready"], g)
                    sp.dma_start(h_in[:, :, :], h_g[g]).then_inc(mlp["h_loaded"], 16)
                    sp.dma_start(x1_in[:, :, :], x1_g[g]).then_inc(mlp["x1_loaded"], 16)

                def group(g, last):
                    if not last:
                        load(g + 1)
                    sp.wait_ge(mlp["out_taken"], g * T + T)
                    sp.dma_start(out_g[g], o_sb[:, :, :]).then_inc(mlp["stored"], 16)

                sp.wait_ge(h_stored, 16 * G)
                over_groups(sp, group)
                sp.wait_ge(mlp["stored"], 16 * G)

            @block.gpsimd
            def _(pool):
                def group(g, last):
                    pool.wait_ge(mlp["out_taken"], g * T)
                    pool.wait_ge(mlp["x1_loaded"], g * 16 + 16)
                    nc.gpsimd.tensor_tensor(res[:, :, :], x1_in[:, :, :], h_in[:, :, :], ALU.add).then_inc(mlp["res_step"], 1)
                    pool.wait_ge(mlp["res_step"], g + 1)
                    nc.gpsimd.tensor_tensor(res[:, :, :], res[:, :, :], bf2_bc[:, :].unsqueeze(1).to_broadcast([P, T, D]),
                                            ALU.add).then_inc(mlp["res_ready"], 1)
                    if not last:
                        power(pool, g + 1)

                over_groups(pool, group)

            @block.scalar
            def _(act):
                def turned(g):
                    for c in range(C):
                        act.wait_ge(mlp["n2t_mm"], g * C + c + 1)
                        nc.scalar.copy(NT2[0][:, c, :], bank[TB[c]][:, :]).then_inc(mlp["n2t_hi"], 1)

                def group(g, last):
                    for m in range(FC):
                        act.wait_ge(mlp["h_mm"], g * FC + m + 1)
                        if m >= R3:
                            act.wait_ge(mlp["h_lo"], g * FC + m - R3 + 1)
                        nc.scalar.activation(hid_f[:, m % R3, :], bank[4 + m % 2][:, :], ACT.Gelu,
                                             bias=hb[:, m:m + 1]).then_inc(mlp["gelu_done"], 1)
                    if not last:
                        turned(g + 1)

                turned(0)
                over_groups(act, group)

            @block.vector
            def _(dve):
                def turned(g):
                    for c in range(C):
                        dve.wait_ge(mlp["n2t_hi"], g * C + c + 1)
                        nc.vector.tensor_tensor(NT2[1][:, c, :], bank[TB[c]][:, :], NT2[0][:, c, :], ALU.subtract)\
                            .then_inc(mlp["n2t_lo"], 1)

                def group(g, last):
                    for m in range(FC):
                        dve.wait_ge(mlp["gelu_done"], g * FC + m + 1)
                        if m >= R3:
                            dve.wait_ge(mlp["out_mm"], g * FC + m - R3 + 1)
                        nc.vector.tensor_copy(HID[0][:, m % R3, :], hid_f[:, m % R3, :]).then_inc(mlp["h_hi"], 1)
                        dve.wait_ge(mlp["h_hi"], g * FC + m + 1)
                        nc.vector.tensor_tensor(HID[1][:, m % R3, :], hid_f[:, m % R3, :], HID[0][:, m % R3, :], ALU.subtract)\
                            .then_inc(mlp["h_lo"], 1)
                        if m == 3 and not last:
                            normalise(dve, g + 1)
                        if m == 6 and not last:
                            scale_rows(dve, g + 1)
                    if not last:
                        turned(g + 1)
                    dve.wait_ge(mlp["res_ready"], g + 1)
                    dve.wait_ge(h_stored, 16 * G)
                    dve.wait_ge(mlp["stored"], g * 16)
                    dve.wait_ge(mlp["out_mm"], g * FC + FC)
                    for t in range(T):
                        nc.vector.tensor_tensor(o_sb[:, t, :], bank[t][:, 0:D], res[:, t, :], ALU.add)\
                            .then_inc(mlp["out_taken"], 1)

                turned(0)
                over_groups(dve, group)

            @block.tensor
            def _(pe):
                def turn(g, cs):
                    for c in cs:
                        if c == 0:
                            pe.wait_ge(mlp["n2_ready"], g + 1)
                        if c == 2:
                            pe.wait_ge(mlp["n2t_lo"], g * C + 1)
                        for t in range(T):
                            mm = nc.tensor.transpose(bank[TB[c]][:, t * P:(t + 1) * P], n2[:, t, c * P:(c + 1) * P], ident)
                        mm.then_inc(mlp["n2t_mm"], 1)

                def up(g, m):
                    if m >= 2:
                        pe.wait_ge(mlp["gelu_done"], g * FC + m - 1)
                    elif m == 0:
                        pe.wait_ge(mlp["gelu_done"], g * FC)
                    for c in range(C):
                        if m == 0:
                            pe.wait_ge(mlp["n2t_lo"], g * C + c + 1)
                        for i, (a, b) in enumerate(PRODUCTS):
                            mm = nc.tensor.matmul(bank[4 + m % 2][:, :], W1S[a][:, c, m * P:(m + 1) * P], NT2[b][:, c, :],
                                                  start=(c == 0 and i == 0), stop=(c == C - 1 and i == 2))
                    mm.then_inc(mlp["h_mm"], 1)

                def down(g, k):
                    pe.wait_ge(mlp["h_lo"], g * FC + k + 1)
                    if k == 0:
                        pe.wait_ge(mlp["out_taken"], g * T)
                    for t in range(T):
                        ts = slice(t * P, (t + 1) * P)
                        for i, (a, b) in enumerate(PRODUCTS):
                            mm = nc.tensor.matmul(bank[t][:, 0:D], HID[a][:, k % R3, ts], W2S[b][:, k, :],
                                                  start=(k == 0 and i == 0), stop=(k == FC - 1 and i == 2))
                    mm.then_inc(mlp["out_mm"], 1)

                def group(g, last):
                    up(g, 0)
                    for m in range(1, FC):
                        up(g, m)
                        if m == FC - 1 and not last:
                            turn(g + 1, (0, 1))
                        down(g, m - 1)
                    if not last:
                        turn(g + 1, (2,))
                    down(g, FC - 1)

                turn(0, (0, 1, 2))
                over_groups(pe, group)


_INS = ['x', 'adj', 'L0_gnn_W1', 'L0_gnn_b1', 'L0_gnn_W2', 'L0_gnn_b2', 'L0_gnn_W3', 'L0_gnn_b3', 'L0_gnn_W4', 'L0_gnn_b4',
        'L0_ffn_g1', 'L0_ffn_b1', 'L0_ffn_g2', 'L0_ffn_b2', 'L0_ffn_Wr', 'L0_ffn_br', 'L0_ffn_Wq', 'L0_ffn_bq', 'L0_ffn_Wk',
        'L0_ffn_bk', 'L0_ffn_Wv', 'L0_ffn_bv', 'L0_ffn_Wo', 'L0_ffn_bo', 'L0_ffn_Wm', 'L0_ffn_bm', 'L0_ffn_W1', 'L0_ffn_bf1',
        'L0_ffn_W2', 'L0_ffn_bf2']


def kernel(**inputs):
    import numpy as _np
    import concourse.bacc as _bacc
    from concourse import mybir as _mybir
    from concourse.bass_utils import run_bass_kernel_spmd as _run

    nc = _bacc.Bacc("TRN2", target_bir_lowering=False, num_devices=1)
    arrays, args = {}, []
    for name in _INS:
        a = _np.ascontiguousarray(inputs[name])
        if a.ndim == 0 or name.endswith("_br"):
            a = a.reshape(1, 1)
        arrays[f"in_{name}"] = a
    arrays["in_consts"] = constants()
    for name, a in arrays.items():
        args.append(nc.dram_tensor(name, a.shape, _mybir.dt.from_np(a.dtype), kind="ExternalInput").ap())
    args.append(nc.dram_tensor("out_0", (B, L, D), _mybir.dt.float32, kind="ExternalOutput").ap())
    program(nc, *args)
    r = _run(nc, [arrays], core_ids=[0])
    return r.results[0]["out_0"]
```
